# Optimizing a Trainium2 kernel written in Bass

```python
import numpy as np
import jax
import jax.numpy as jnp

def _softmax(x, axis=-1):
    return jax.nn.softmax(x, axis=axis)

def _gelu(x):
    return jax.nn.gelu(x, approximate=True)

def _silu(x):
    return jax.nn.silu(x)

def _sigmoid(x):
    return jax.nn.sigmoid(x)

def _layernorm(x, axis=-1, eps=1e-05):
    m = jnp.mean(x, axis=axis, keepdims=True)
    v = jnp.var(x, axis=axis, keepdims=True)
    return (x - m) / jnp.sqrt(v + eps)

def _scatter_add(tgt, idx, src, axis=0):
    return tgt.at[idx].add(src)

def _segment_sum(src, seg, n):
    return jax.ops.segment_sum(src, seg, n)
kernel_name = 'mk_flamingo_gated_d1_seqx_r4_d1af39'

def setup_inputs(seed: int=0):
    np.random.seed(seed)
    _w = jnp.asarray

    def _rec_inputs():
        import jax
        import jax.numpy as jnp
        _rk = jax.random.key(seed)
        x = 4.136e-05 + 0.9999 * jax.random.normal(jax.random.fold_in(_rk, 1), (4, 512, 512), jnp.float32)
        _lenS = 512 - jax.random.randint(jax.random.fold_in(_rk, 7), (4,), 0, max(1, 512 // 4) + 1, jnp.int32)
        _lenS2 = 512 - jax.random.randint(jax.random.fold_in(_rk, 8), (4,), 0, max(1, 512 // 4) + 1, jnp.int32)
        _ctx_1024P = jax.random.normal(jax.random.fold_in(_rk, 11), (4, 16, 256), jnp.float32)
        _ctx_1024c = jax.random.dirichlet(jax.random.fold_in(_rk, 511), 0.3 * jnp.ones((16,), jnp.float32), (4, 512))
        _ctx_1024t = jnp.einsum('bsk,bkd->bsd', _ctx_1024c, _ctx_1024P)
        _ctx_1024t = _ctx_1024t * jax.lax.rsqrt(jnp.mean(jnp.square(_ctx_1024t)) + 1e-12) * 0.953939
        ctx_1024 = -0.000292821 + 1.00034 * (_ctx_1024t + 0.3 * jax.random.normal(jax.random.fold_in(_rk, 611), (4, 512, 256), jnp.float32))
        _g = jax.random.normal(jax.random.fold_in(_rk, 9001), (2, 1), jnp.float32)
        _g = jnp.sign(_g) * jnp.maximum(jnp.abs(_g), 1.0) + (_g == 0) * 1.0
        g_xattn = _g[0]
        g_ffn = _g[1]
        return (x, ctx_1024, g_xattn, g_ffn)
    x, ctx_1024, g_xattn, g_ffn = _rec_inputs()

    def _L0_xattn_setup():
        import jax, jax.numpy as jnp
        import numpy as np
        import math
        B, L, DM = (2, 512, 256)
        DS, DC, EXP = (16, 4, 2)
        DI = EXP * DM
        DR = math.ceil(DM / 16)
        DT_MIN, DT_MAX, DT_FLOOR = (0.001, 0.1, 0.0001)

        def _ssm_forward(hidden_states, z, in_proj_w, conv_w, conv_b, x_proj_w, dt_proj_w, dt_proj_b, A_log, D):
            b = hidden_states.shape[0]
            x = jnp.einsum('ed,bld->bel', in_proj_w, hidden_states)
            xp = jnp.pad(x, ((0, 0), (0, 0), (DC - 1, 0)))
            xc = jax.lax.conv_general_dilated(xp, conv_w[:, None, :], window_strides=(1,), padding='VALID', dimension_numbers=('NCH', 'OIH', 'NCH'), feature_group_count=DI)
            u = jax.nn.silu(xc + conv_b[None, :, None])
            x_dbl = jnp.einsum('ke,bel->bkl', x_proj_w, u)
            dt_lo = x_dbl[:, :DR]
            Bm = x_dbl[:, DR:DR + DS]
            Cm = x_dbl[:, DR + DS:]
            delta = jax.nn.softplus(jnp.einsum('er,brl->bel', dt_proj_w, dt_lo) + dt_proj_b[None, :, None])
            A = -jnp.exp(A_log)

            def step(state, xs):
                d_t, B_t, C_t, u_t = xs
                dA = jnp.exp(d_t[..., None] * A)
                state = state * dA + (d_t * u_t)[..., None] * B_t[:, None, :]
                y_t = jnp.einsum('ben,bn->be', state, C_t)
                return (state, y_t)
            xs = (jnp.moveaxis(delta, -1, 0), jnp.moveaxis(Bm, -1, 0), jnp.moveaxis(Cm, -1, 0), jnp.moveaxis(u, -1, 0))
            state0 = jnp.zeros((b, DI, DS), delta.dtype)
            _, ys = jax.lax.scan(step, state0, xs)
            y = jnp.moveaxis(ys, 0, -1)
            y = y + D[None, :, None] * u
            y = y * jax.nn.silu(z)
            return jnp.swapaxes(y, 1, 2)
        key = jax.random.key(seed)
        ks = jax.random.split(key, 8)
        hidden_states = jax.random.normal(ks[0], (B, L, DM), jnp.float32)
        z = jax.random.normal(ks[1], (B, DI, L), jnp.float32)
        in_proj_w = jax.random.normal(ks[2], (DI, DM), jnp.float32) * DM ** (-0.5)
        conv_w = jax.random.normal(ks[3], (DI, DC), jnp.float32) * DC ** (-0.5)
        conv_b = jnp.zeros((DI,), jnp.float32)
        x_proj_w = jax.random.normal(ks[4], (DR + 2 * DS, DI), jnp.float32) * DI ** (-0.5)
        dt_std = DR ** (-0.5)
        dt_proj_w = jax.random.uniform(ks[5], (DI, DR), jnp.float32, -dt_std, dt_std)
        dt = jnp.exp(jax.random.uniform(ks[6], (DI,), jnp.float32) * (math.log(DT_MAX) - math.log(DT_MIN)) + math.log(DT_MIN))
        dt = jnp.clip(dt, DT_FLOOR)
        dt_proj_b = dt + jnp.log(-jnp.expm1(-dt))
        A_log = jnp.log(jnp.broadcast_to(jnp.arange(1, DS + 1, dtype=jnp.float32), (DI, DS)))
        D = jnp.ones((DI,), jnp.float32)
        return dict(hidden_states=hidden_states, z=z, in_proj_w=in_proj_w, conv_w=conv_w, conv_b=conv_b, x_proj_w=x_proj_w, dt_proj_w=dt_proj_w, dt_proj_b=dt_proj_b, A_log=A_log, D=D)
    _L0_xattn_all = _L0_xattn_setup()
    _L0_xattn_in = {k: v for k, v in _L0_xattn_all.items() if k in ('in_proj_w', 'conv_w', 'conv_b', 'x_proj_w', 'dt_proj_w', 'dt_proj_b', 'A_log', 'D')}
    del _L0_xattn_all

    def _L0_ffn_setup():
        import jax, jax.numpy as jnp
        import numpy as np
        NUM_EXPERTS = 32
        TOP_K = 4
        HIDDEN = 512
        INTER = 192
        key = jax.random.key(seed)
        k1, k2, k3, k4 = jax.random.split(key, 4)
        hidden_states = jax.random.normal(k1, (4, 128, HIDDEN), dtype=jnp.float32)
        gate = jax.random.normal(k2, (HIDDEN, NUM_EXPERTS), dtype=jnp.float32) * 0.02
        gate_up_proj = jax.random.normal(k3, (NUM_EXPERTS, HIDDEN, 2 * INTER), dtype=jnp.float32) * 0.02
        down_proj = jax.random.normal(k4, (NUM_EXPERTS, INTER, HIDDEN), dtype=jnp.float32) * 0.02
        return {'hidden_states': hidden_states, 'gate': gate, 'gate_up_proj': gate_up_proj, 'down_proj': down_proj}
    _L0_ffn_all = _L0_ffn_setup()
    _L0_ffn_in = {k: v for k, v in _L0_ffn_all.items() if k in ('gate', 'gate_up_proj', 'down_proj')}
    del _L0_ffn_all
    return {'x': x, 'ctx_1024': ctx_1024, 'g_xattn': g_xattn, 'g_ffn': g_ffn, 'L0_xattn_in_proj_w': _L0_xattn_in['in_proj_w'], 'L0_xattn_conv_w': _L0_xattn_in['conv_w'], 'L0_xattn_conv_b': _L0_xattn_in['conv_b'], 'L0_xattn_x_proj_w': _L0_xattn_in['x_proj_w'], 'L0_xattn_dt_proj_w': _L0_xattn_in['dt_proj_w'], 'L0_xattn_dt_proj_b': _L0_xattn_in['dt_proj_b'], 'L0_xattn_A_log': _L0_xattn_in['A_log'], 'L0_xattn_D': _L0_xattn_in['D'], 'L0_ffn_gate': _L0_ffn_in['gate'], 'L0_ffn_gate_up_proj': _L0_ffn_in['gate_up_proj'], 'L0_ffn_down_proj': _L0_ffn_in['down_proj']}

def reference(x, ctx_1024, g_xattn, g_ffn, L0_xattn_in_proj_w, L0_xattn_conv_w, L0_xattn_conv_b, L0_xattn_x_proj_w, L0_xattn_dt_proj_w, L0_xattn_dt_proj_b, L0_xattn_A_log, L0_xattn_D, L0_ffn_gate, L0_ffn_gate_up_proj, L0_ffn_down_proj):
    import jax
    import jax.numpy as jnp

    def _L0_xattn_ref(hidden_states, z, in_proj_w, conv_w, conv_b, x_proj_w, dt_proj_w, dt_proj_b, A_log, D):
        import jax, jax.numpy as jnp
        import numpy as np
        import math
        B, L, DM = (2, 512, 256)
        DS, DC, EXP = (16, 4, 2)
        DI = EXP * DM
        DR = math.ceil(DM / 16)
        DT_MIN, DT_MAX, DT_FLOOR = (0.001, 0.1, 0.0001)

        def _ssm_forward(hidden_states, z, in_proj_w, conv_w, conv_b, x_proj_w, dt_proj_w, dt_proj_b, A_log, D):
            b = hidden_states.shape[0]
            x = jnp.einsum('ed,bld->bel', in_proj_w, hidden_states)
            xp = jnp.pad(x, ((0, 0), (0, 0), (DC - 1, 0)))
            xc = jax.lax.conv_general_dilated(xp, conv_w[:, None, :], window_strides=(1,), padding='VALID', dimension_numbers=('NCH', 'OIH', 'NCH'), feature_group_count=DI)
            u = jax.nn.silu(xc + conv_b[None, :, None])
            x_dbl = jnp.einsum('ke,bel->bkl', x_proj_w, u)
            dt_lo = x_dbl[:, :DR]
            Bm = x_dbl[:, DR:DR + DS]
            Cm = x_dbl[:, DR + DS:]
            delta = jax.nn.softplus(jnp.einsum('er,brl->bel', dt_proj_w, dt_lo) + dt_proj_b[None, :, None])
            A = -jnp.exp(A_log)

            def step(state, xs):
                d_t, B_t, C_t, u_t = xs
                dA = jnp.exp(d_t[..., None] * A)
                state = state * dA + (d_t * u_t)[..., None] * B_t[:, None, :]
                y_t = jnp.einsum('ben,bn->be', state, C_t)
                return (state, y_t)
            xs = (jnp.moveaxis(delta, -1, 0), jnp.moveaxis(Bm, -1, 0), jnp.moveaxis(Cm, -1, 0), jnp.moveaxis(u, -1, 0))
            state0 = jnp.zeros((b, DI, DS), delta.dtype)
            _, ys = jax.lax.scan(step, state0, xs)
            y = jnp.moveaxis(ys, 0, -1)
            y = y + D[None, :, None] * u
            y = y * jax.nn.silu(z)
            return jnp.swapaxes(y, 1, 2)
        return _ssm_forward(hidden_states, z, in_proj_w, conv_w, conv_b, x_proj_w, dt_proj_w, dt_proj_b, A_log, D)

    def _L0_ffn_ref(hidden_states, gate, gate_up_proj, down_proj):
        import jax, jax.numpy as jnp
        import numpy as np
        NUM_EXPERTS = 32
        TOP_K = 4
        HIDDEN = 512
        INTER = 192
        batch_size = hidden_states.shape[0]
        x = hidden_states.reshape(-1, HIDDEN)
        num_tokens = x.shape[0]
        router_logits = jnp.einsum('TD,DE->TE', x, gate)
        routing_weights = jax.nn.softmax(router_logits.astype(jnp.float32), axis=-1)
        top_k_weights, top_k_indices = jax.lax.top_k(routing_weights, TOP_K)
        top_k_weights = top_k_weights / top_k_weights.sum(axis=-1, keepdims=True)
        top_k_weights = top_k_weights.astype(x.dtype)
        router_weights = jnp.zeros((num_tokens, NUM_EXPERTS), dtype=x.dtype)
        token_indices = jnp.broadcast_to(jnp.arange(num_tokens)[:, None], top_k_indices.shape)
        router_weights = router_weights.at[token_indices, top_k_indices].set(top_k_weights)
        gate_up = jnp.einsum('TD,EDF->TEF', x, gate_up_proj)
        g, u = jnp.split(gate_up, 2, axis=-1)
        gated = u * jax.nn.silu(g)
        next_states = jnp.einsum('TEF,EFD->TED', gated, down_proj)
        next_states = (next_states * router_weights[..., None]).sum(axis=1)
        return next_states.reshape(batch_size, -1, HIDDEN)
    x = x + jnp.tanh(g_xattn[0]) * _L0_xattn_ref(ctx_1024, _layernorm(x, axis=-1), L0_xattn_in_proj_w, L0_xattn_conv_w, L0_xattn_conv_b, L0_xattn_x_proj_w, L0_xattn_dt_proj_w, L0_xattn_dt_proj_b, L0_xattn_A_log, L0_xattn_D)
    x = x + jnp.tanh(g_ffn[0]) * _L0_ffn_ref(_layernorm(x, axis=-1), L0_ffn_gate, L0_ffn_gate_up_proj, L0_ffn_down_proj)
    return x

_drawn_inputs = setup_inputs


def setup_inputs(seed=0):
    import zlib

    import numpy as np

    out = dict(_drawn_inputs(seed))
    spreads = {'L0_xattn_conv_b': (0.0, 0.28), 'L0_xattn_D': (1.0, 0.2)}
    factors = {'L0_xattn_dt_proj_w': 6.675,
     'L0_xattn_dt_proj_b': 2.934,
     'L0_ffn_gate': 4.32,
     'L0_ffn_gate_up_proj': 4.055,
     'L0_ffn_down_proj': 4.055}
    for name, (base, spread) in spreads.items():
        noise = np.random.default_rng([zlib.crc32(name.encode()), seed]).standard_normal(out[name].shape)
        drawn = base * np.exp(spread * noise) if base else spread * noise
        out[name] = jnp.asarray(drawn.astype(out[name].dtype))
    for name, factor in factors.items():
        out[name] = (out[name] * factor).astype(out[name].dtype)
    return out
```

```python
from contextlib import ExitStack

import concourse.bass as bass
from concourse import mybir

P = 128
F32 = mybir.dt.float32
F32R = mybir.dt.float32r
BF16 = mybir.dt.bfloat16
I32 = mybir.dt.int32
U32 = mybir.dt.uint32
ALU = mybir.AluOpType
ACT = mybir.ActivationFunctionType
AX = mybir.AxisListType
LN_EPS = 1e-5


def flamingo_kernel(nc, x, ctx_in, g_xattn, g_ffn, in_proj_w, conv_w, conv_b, x_proj_w,
                    dt_proj_w, dt_proj_b, A_log, D, gate, gate_up, down, out):
    NB, L, DM = x.shape
    DC = ctx_in.shape[2]
    DI = in_proj_w.shape[0]
    TAPS = conv_w.shape[1]
    DR = dt_proj_w.shape[1]
    NS = A_log.shape[1]
    assert DI == L == DM
    ET, LC, CT = DI // P, L // P, DC // P
    NT = NB * LC
    XR = DR + 2 * NS
    RING = ET

    NE = gate.shape[1]
    TOPK = 4
    FI = gate_up.shape[2] // 2
    TOK = NB * L
    UNR = 4
    SLOTS = -(-(TOK * TOPK // P + NE - 1) // UNR) * UNR
    REGION = P + TOK
    DUMMY = NE * REGION
    HK = FI // 2

    stack = ExitStack()
    first_branch = ExitStack()
    with stack:
        def keep(name, shape, dt=F32):
            return stack.enter_context(nc.sbuf_tensor(name, shape, dt))

        def sb(name, shape, dt=F32):
            return first_branch.enter_context(nc.sbuf_tensor(name, shape, dt))

        def sem(name):
            return stack.enter_context(nc.semaphore(name))

        bank = [stack.enter_context(nc.psum_tensor(f"bank{i}", [P, 512], F32)) for i in range(8)]
        c_dram = nc.dram_tensor("c_rows", [NB * NS, L], F32, kind="Internal").ap()
        skip_dram = nc.dram_tensor("skip_rows", [NB, P, ET * L], F32, kind="Internal").ap()

        xs_dram = nc.dram_tensor("tokens_by_expert", [DUMMY + P, DM], F32, kind="Internal").ap()
        ys_dram = nc.dram_tensor("results_by_expert", [SLOTS * P, DM], F32, kind="Internal").ap()

        ident = keep("ident", [P, P])
        x1 = keep("x1", [P, NT, DM])
        eps = keep("eps", [P, 1])
        zeros = keep("zeros", [P, DM])
        slot_f = keep("slot_f", [P, NT, TOPK])
        slot_i = keep("slot_i", [P, NT, TOPK], I32)
        y_i = keep("y_i", [P, NT, TOPK], I32)
        weight = keep("weight", [P, NT, TOPK])
        gf = keep("gf", [P, 1])
        tgf = keep("tgf", [P, 1])
        w_in_nat = sb("w_in_nat", [P, ET, DC])
        w_inT = sb("w_inT", [P, CT, DI])
        xproj_nat = sb("xproj_nat", [XR, DI])
        xprojT = sb("xprojT", [P, ET, XR])
        dtw_nat = sb("dtw_nat", [P, ET, DR])
        dtwT = sb("dtwT", [DR, DI])
        cw = sb("cw", [P, ET, TAPS])
        cb = sb("cb", [P, ET])
        dtb = sb("dtb", [P, ET])
        Dp = sb("Dp", [P, ET])
        Alog = sb("Alog", [P, ET, NS])
        Aexp = sb("Aexp", [P, ET, NS])
        Aneg = sb("Aneg", [P, ET, NS])
        gx = sb("gx", [P, 1])
        tgx = sb("tgx", [P, 1])
        zT = sb("zT", [P, NT, DI])
        delta = sb("delta", [P, NB, ET, L])
        duT = sb("duT", [P, NT, DI])
        BT = sb("BT", [P, NB, LC * NS])
        ctxn = sb("ctxn", [P, LC, DC])
        ctxT = sb("ctxT", [P, CT, L])
        u = sb("u", [P, ET, L])
        w0, w1, w2, w3 = [sb(f"work{i}", [P, ET, L]) for i in range(4)]
        xdbl = sb("xdbl", [XR, L])
        skip = sb("skip", [P, ET, L])
        stats = sb("stats", [P, NT, 6])
        mv = sb("mv", [P, NT, 2])
        rstd = sb("rstd", [P, NT])
        std = sb("std", [P, NT])
        nmr = sb("nmr", [P, NT])
        dBuT = [w0, w1]
        dA = [w2[:, i, :] for i in range(RING)]
        h = [w3[:, i, :] for i in range(RING)]
        hC = [u[:, i, :] for i in range(RING)]
        crow = [ctxT[:, i, :] for i in range(2)]
        first_branch.close()

        gate_sb = keep("gate_sb", [P, DM // P, NE])
        upper = keep("upper", [P, P], BF16)
        ones = keep("ones", [P, P], BF16)
        eidx = keep("eidx", [P, NE])
        ebase = keep("ebase", [P, NE])
        xn = keep("xn", [P, LC, DM])
        xnT = keep("xnT", [P, LC, DM])
        stats2 = keep("stats2", [P, LC, 6])
        mv2 = keep("mv2", [P, LC, 2])
        std2 = keep("std2", [P, LC])
        rstd2 = keep("rstd2", [P, LC])
        nmr2 = keep("nmr2", [P, LC])
        logit = keep("logit", [P, LC, NE])
        top = keep("top", [P, LC, 8])
        topi = keep("topi", [P, LC, 8], U32)
        topf = keep("topf", [P, NT * TOPK])
        ex = keep("ex", [P, LC, TOPK])
        exs = keep("exs", [P, LC])
        onehot = keep("onehot", [P, LC * TOPK, NE])
        picked = keep("picked", [P, LC * TOPK, NE])
        chosen = keep("chosen", [P, LC, NE], BF16)
        cum = keep("cum", [P, NE])
        cumb = keep("cumb", [P, NE])
        nti = keep("nti", [P, NE], I32)
        ntf = keep("ntf", [P, NE])
        ntcum = keep("ntcum", [P, NE])
        ntone = keep("ntone", [P, NE])
        shift = keep("shift", [P, NE])
        sidx = keep("sidx", [1, SLOTS])
        slot_e = keep("slot_e", [1, SLOTS])
        tab = keep("tab", [1, 2 * SLOTS], I32)
        last_slot = keep("last_slot", [1, NE], I32)
        srow = keep("srow", [1, SLOTS])
        svalid = keep("svalid", [1, SLOTS])
        stmp = keep("stmp", [1, SLOTS])
        NWR = 4
        WG, WD = (DM // P) * 2 * FI, 2 * DM
        raw = [keep(f"raw{i}", [P, WG]) for i in range(2)]
        whi = keep("whi", [P, NWR * WG], F32R)
        wlo = keep("wlo", [P, NWR * WG], F32R)
        wdn = keep("wdn", [P, NWR * WD])
        NX = 4
        xrow = [keep(f"xrow{i}", [P, DM]) for i in range(NX)]
        xhi = [keep(f"xhi{i}", [P, DM], F32R) for i in range(2)]
        xlo = [keep(f"xlo{i}", [P, DM], F32R) for i in range(2)]
        sg = [keep(f"sg{i}", [P, FI]) for i in range(2)]
        gated = [keep(f"gated{i}", [P, FI]) for i in range(2)]
        gT = [keep(f"gT{i}", [P, 2 * P]) for i in range(2)]
        yrow = [keep(f"yrow{i}", [P, DM]) for i in range(4)]
        NY = 6
        ygat = keep("ygat", [P, NY, DM])
        compare = ygat[0:1, :, :].rearrange("p a b -> p (a b)")[:, 0:SLOTS * NE].rearrange("p (s e) -> p s e", e=NE)

        s_w = sem("weights_loaded")
        s_x = sem("x_loaded")
        s_id0 = sem("ident_zeroed")
        s_eps = sem("eps_ready")
        s_apart = sem("act_waits_passed")
        s_id = sem("ident_ready")
        s_ctx = sem("ctx_loaded")
        s_wt = sem("weights_transposed")
        s_wtc = sem("weights_copied")
        s_ctxt = sem("ctx_transposed")
        s_ctxe = sem("ctx_copied")
        s_xin = sem("in_proj_done")
        s_tap = sem("last_tap_done")
        s_cv = sem("conv_chain")
        s_conv = sem("conv_done")
        s_u = sem("u_ready")
        s_xd = sem("x_proj_done")
        s_xde = sem("x_proj_copied")
        s_cst = sem("c_rows_stored")
        s_dp = sem("dt_proj_done")
        s_abs = sem("abs_done")
        s_ez = sem("expneg_done")
        s_lw = sem("ln_done")
        s_wm = sem("rounded_minus_one")
        s_t1 = sem("rounding_error_done")
        s_t2 = sem("log1p_done")
        s_rl = sem("relu_done")
        s_dl = sem("delta_ready")
        s_du = sem("du_ready")
        s_dut = sem("du_transposed")
        s_dute = sem("duT_copied")
        s_skc = sem("skip_computed")
        s_sks = sem("skip_stored")
        s_skl = sem("skip_loaded")
        s_sku = sem("skip_used")
        s_A = sem("A_exp_done")
        s_An = sem("A_negated")
        s_tg = sem("tanh_g_ready")
        s_st = sem("stats_done")
        s_mv = sem("mean_var_done")
        s_sd = sem("std_done")
        s_rs = sem("rstd_done")
        s_nm = sem("nmr_done")
        s_zn = sem("silu_z_done")
        s_zt = sem("z_transposed")
        s_zte = sem("zT_copied")
        s_bua = sem("dBuT_scaled_act")
        s_bud = sem("dBuT_scaled_dve")
        s_dbu = sem("dBu_in_psum")
        s_h = sem("scan_done")
        s_hc = sem("hC_ready")
        s_y = sem("y_accumulated")
        s_dA = sem("dA_ready")
        s_c = [sem(f"c_row_loaded{i}") for i in range(2)]
        s_yz = sem("y_times_z")
        s_x1 = sem("x1_ready")
        r_gl = sem("gate_and_g_loaded")
        r_cst0 = sem("router_constants_filled")
        r_cst2 = sem("router_constants_ready")
        r_st2 = sem("stats2_done")
        r_mv2 = sem("mean_var2_done")
        r_sd2 = sem("std2_done")
        r_rs2 = sem("rstd2_done")
        r_nm2 = sem("nmr2_done")
        r_xn2 = sem("normed_ready")
        r_xnt = sem("normed_transposed")
        r_xnte = sem("normed_copied")
        r_lg = sem("logits_done")
        r_lgc = sem("logits_copied")
        r_mx = sem("top8_done")
        r_mi = sem("top8_index_done")
        r_tf = sem("index_float_done")
        r_sub = sem("max_subtracted")
        r_ex = sem("exp_done")
        r_exsum = sem("exp_sum_done")
        r_exr = sem("exp_sum_inverted")
        r_w = sem("weights_of_tokens_done")
        r_oh = sem("onehot_done")
        r_ch = sem("chosen_done")
        r_pos = sem("positions_done")
        r_posb = sem("rows_based")
        r_cumb = sem("base_done")
        r_cum = sem("counts_added")
        r_pk = sem("picked_done")
        r_sf = sem("rows_float_done")
        r_si = sem("rows_ready")
        r_zero = sem("zeros_ready")
        r_zst = sem("zeros_stored")
        r_sc = sem("tokens_scattered")
        r_tb = sem("table_step")
        r_tbl = sem("table_ready")
        r_hi = sem("weights_hi_done")
        r_spl = sem("weights_split")
        r_mmx = sem("x_transposed")
        r_xh = sem("xhi_ready")
        r_gu = sem("gate_up_done")
        r_sg = sem("silu_g_ready")
        r_gd = sem("gated_ready")
        r_gt = sem("gated_transposed")
        r_gh = sem("gT_ready")
        r_dnl = sem("down_loaded")
        r_dn = sem("down_done")
        r_ye = sem("y_copied")
        r_xlo = sem("xlo_ready")
        r_raw = [sem(f"weights_loaded{i}") for i in range(2)]
        r_xl = [sem(f"x_rows_loaded{i}") for i in range(NX)]
        r_ys = [sem(f"y_rows_stored{i}") for i in range(NX)]
        r_yg = [sem(f"y_rows_gathered{i}") for i in range(6)]
        r_acc = sem("y_added")
        r_yi = sem("rows_of_y_ready")
        r_apart = sem("pool_waits_passed")
        r_out = sem("out_stored")

        x_rows = x.rearrange("b (c p) d -> p (b c) d", p=P)
        ctx_rows = ctx_in.rearrange("b (c p) d -> b p c d", p=P)
        NW = 9
        block = stack.enter_context(nc.Block())

        def cols(i, n=P):
            return slice(i * n, (i + 1) * n)

        def tile(t, i, k=1):
            return t[:, bass.ds(i, k), :].rearrange("p t n -> p (t n)")

        @block.sync
        def _(sp):
            sp.dma_start(w_in_nat[:], in_proj_w.rearrange("(t p) d -> p t d", p=P)).then_inc(s_w, 16)
            sp.dma_start(ctxn[:], ctx_rows[0]).then_inc(s_ctx, 16)
            sp.dma_start(xproj_nat[:], x_proj_w).then_inc(s_w, 16)
            sp.dma_start(dtw_nat[:], dt_proj_w.rearrange("(t p) r -> p t r", p=P)).then_inc(s_w, 16)
            sp.dma_start(cw[:], conv_w.rearrange("(t p) k -> p t k", p=P)).then_inc(s_w, 16)
            sp.dma_start(Alog[:], A_log.rearrange("(t p) n -> p t n", p=P)).then_inc(s_w, 16)
            for dst, src in ((cb, conv_b), (dtb, dt_proj_b), (Dp, D)):
                sp.dma_start(dst[:], src.rearrange("(t p) -> p t", p=P), allow_slow_non_contiguous=True).then_inc(s_w, 16)
            sp.dma_start(gx[:], g_xattn.partition_broadcast(P)).then_inc(s_w, 16)
            sp.dma_start(gf[:], g_ffn.partition_broadcast(P)).then_inc(r_gl, 16)
            sp.dma_start(x1[:], x_rows).then_inc(s_x, 16)
            sp.wait_ge(r_zero, 1)
            with sp.Fori(0, NE + 1) as e:
                sp.dma_start(xs_dram[bass.ds(e * REGION, P), :], zeros[:]).then_inc(r_zst, 16)

            def store_rows(b):
                sp.wait_ge(s_xde, b * 2 + 1)
                sp.dma_start(c_dram[bass.ds(b * NS, NS), :], xdbl[DR + NS:XR, :]).then_inc(s_cst, 16)
                sp.wait_ge(s_skc, b * ET + ET)
                sp.dma_start(skip_dram[bass.ds(b, 1)].rearrange("o p n -> (o p) n"),
                             skip[:].rearrange("p t n -> p (t n)")).then_inc(s_sks, 16)

            with sp.Fori(0, NB - 1) as b:
                sp.wait_ge(s_ctxt, b + 1)
                sp.dma_start(ctxn[:], ctx_rows[bass.ds(b + 1, 1)].rearrange("o p c d -> p (o c) d")).then_inc(s_ctx, 16)
                store_rows(b)
            store_rows(NB - 1)

            sp.wait_ge(s_cst, NB * 16 + 1)
            sp.wait_ge(s_xin, NB * ET + 1)
            for q in range(2):
                sp.dma_start(crow[q], c_dram[q:q + 1, :].partition_broadcast(P)).then_inc(s_c[q], 16)
            with sp.Fori(1, NB * NS // 2) as j:
                for q in range(2):
                    sp.wait_ge(s_hc, j * (2 * ET) + q * ET)
                    sp.dma_start(crow[q], c_dram[bass.ds(j * 2 + q, 1), :].partition_broadcast(P)).then_inc(s_c[q], 16)

            sp.wait_ge(s_x1, NT)
            sp.dma_start(gate_sb[:], gate.rearrange("(k p) e -> p k e", p=P)).then_inc(r_gl, 16)

            sp.wait_ge(r_zst, (NE + 1) * 16)
            sp.wait_ge(r_tbl, 1)
            sp.wait_ge(r_sc, NT * TOPK * 16)

            def load_x(s, q):
                row = sp.value_load(tab[0:1, bass.ds(s + SLOTS, 1)], min_val=0, max_val=DUMMY)
                sp.dma_start(xrow[q][:], xs_dram[bass.ds(row, P), :]).then_inc(r_xl[q], 16)

            def store_y(s, q):
                sp.wait_ge(r_ye, s + 1 + UNR)
                sp.dma_start(ys_dram[bass.ds(s * P, P), :], yrow[q][:]).then_inc(r_ys[q], 16)

            for q in range(NX):
                load_x(q, q)
            with sp.Fori(0, SLOTS // UNR - 1) as rnd:
                for q in range(UNR):
                    s = rnd * UNR + q
                    store_y(s, q)
                    sp.wait_ge(r_mmx, s + 1)
                    load_x(s + NX, q)
            for q in range(NX):
                store_y(SLOTS - NX + q, q)
            for t in range(NT):
                sp.wait_ge(r_acc, (t + 1) * TOPK)
                sp.dma_start(out.rearrange("b (c p) d -> (b c) p d", p=P)[t], x1[:, t, :]).then_inc(r_out, 16)
            sp.wait_ge(r_out, NT * 16)

        @block.gpsimd
        def _(pool):
            pool.sem_inc(s_t2, 1)
            nc.gpsimd.memset(ident[:], 0.0).then_inc(s_id0, 1)
            pool.wait_ge(s_id0, 1)
            nc.gpsimd.affine_select(out=ident[:], in_=ident[:], compare_op=ALU.not_equal, fill=1.0, base=0,
                                    pattern=[[-1, P]], channel_multiplier=1).then_inc(s_id, 1)
            nc.gpsimd.memset(zeros[:], 0.0).then_inc(r_zero, 1)
            pool.sem_inc(s_hc, RING)
            with pool.Fori(0, NB) as b:
                pool.wait_ge(s_wm, b + 1)
                nc.gpsimd.tensor_tensor(w3[:], w3[:], w2[:], ALU.subtract).then_inc(s_t1, 1)
                pool.wait_ge(s_lw, b + 1)
                pool.wait_ge(s_t1, b + 1)
                nc.gpsimd.tensor_tensor(w3[:], w1[:], w3[:], ALU.subtract).then_inc(s_t2, 1)

            pool.wait_ge(s_du, NB + 1)
            with pool.Fori(0, NB) as b:
                def times_c(n, q):
                    m = b * NS + n
                    pool.wait_ge(s_c[q], b * (NS * 8) + (n - q) * 8 + 16)
                    for et in range(ET):
                        k = m * ET + et
                        pool.wait_ge(s_h, k + 1 + RING)
                        pool.wait_ge(s_y, k + 1)
                        nc.gpsimd.tensor_tensor(hC[et], h[et], crow[q], ALU.mult).then_inc(s_hc, 1)

                with pool.Fori(0, NS, 2) as n:
                    for q in range(2):
                        times_c(n + q, q)
                for lc in range(LC):
                    pool.wait_ge(s_yz, b * LC + lc + 1 + 1)
                    t = b * LC + lc
                    nc.gpsimd.tensor_tensor(tile(x1, t), tile(x1, t), tile(zT, t), ALU.add).then_inc(s_x1, 1)

            pool.wait_ge(s_x1, NT)
            nc.gpsimd.memset(ones[:], 1.0).then_inc(r_cst0, 1)
            nc.gpsimd.memset(upper[:], 1.0).then_inc(r_cst0, 1)
            pool.wait_ge(r_cst0, 2)
            nc.gpsimd.affine_select(out=upper[:], in_=upper[:], compare_op=ALU.is_gt, fill=0.0, base=0,
                                    pattern=[[1, P]], channel_multiplier=-1).then_inc(r_cst2, 1)
            nc.gpsimd.iota(eidx[:], pattern=[[1, NE]], base=0, channel_multiplier=0,
                           allow_small_or_imprecise_dtypes=True).then_inc(r_cst2, 1)
            nc.gpsimd.iota(ebase[:], pattern=[[REGION, NE]], base=P, channel_multiplier=0,
                           allow_small_or_imprecise_dtypes=True).then_inc(r_cst2, 1)
            nc.gpsimd.iota(sidx[:], pattern=[[1, SLOTS]], base=0, channel_multiplier=0,
                           allow_small_or_imprecise_dtypes=True).then_inc(r_cst2, 1)

            def load_gate_up(e, q):
                pool.dma_start(raw[q][:].rearrange("p (k f) -> p k f", f=2 * FI),
                               gate_up[bass.ds(e, 1)].rearrange("o (k p) f -> p (o k) f", p=P)).then_inc(r_raw[q], 16)

            def fill_slot(e, q, r):
                at = slice(r * WG, (r + 1) * WG)
                pool.sem_inc(r_apart, 1)
                pool.dma_start(wdn[0:HK, r * WD:(r + 1) * WD].rearrange("p (k n) -> p k n", n=DM),
                               down[bass.ds(e, 1)].rearrange("o (k p) n -> p (o k) n", p=HK)).then_inc(r_dnl, 16)
                nc.gpsimd.tensor_copy(whi[:, at], raw[q][:]).then_inc(r_hi, 1)
                pool.wait_ge(r_hi, e + 1)
                nc.gpsimd.tensor_tensor(wlo[:, at], raw[q][:], whi[:, at].bitcast(F32), ALU.subtract).then_inc(r_spl, 1)
                pool.wait_ge(r_dnl, e * 16 + 16)
                pool.sem_inc(r_spl, 1)

            load_gate_up(0, 0)
            load_gate_up(1, 1)
            for b in range(NB):
                pool.wait_ge(r_si, b + 1)
                for t in range(LC):
                    for j in range(TOPK):
                        nc.gpsimd.indirect_dma_start(
                            out=xs_dram, out_offset=bass.IndirectOffsetOnAxis(ap=slot_i[:, b * LC + t, j:j + 1], axis=0),
                            in_=xn[:, t, :], in_offset=None).then_inc(r_sc, 16)
            def turn_of(e0, first):
                for i in range(NWR):
                    e, q = e0 + i, i % 2
                    pool.wait_ge(r_raw[q], (e - q) * 8 + 16)
                    if not first:
                        used = pool.value_load(last_slot[0:1, bass.ds(e - NWR, 1)], min_val=1, max_val=SLOTS + 1)
                        pool.wait_ge(r_dn, used)
                    fill_slot(e, q, i)
                    pool.wait_ge(r_spl, e * 2 + 2)
                    yield e, q

            for e, q in turn_of(0, True):
                load_gate_up(e + 2, q)
            pool.wait_ge(r_tbl, 1)
            with pool.Fori(1, NE // NWR - 1) as rnd:
                for e, q in turn_of(rnd * NWR, False):
                    load_gate_up(e + 2, q)
            for e, q in turn_of(NE - NWR, False):
                if e + 2 < NE:
                    load_gate_up(e + 2, q)
            pool.wait_ge(r_yi, 1)
            for q in range(NX):
                pool.wait_ge(r_ys[q], SLOTS // NX * 16)
            for t in range(NT):
                for j in range(TOPK):
                    k = t * TOPK + j
                    if k >= NY:
                        pool.wait_ge(r_acc, k - NY + 1)
                    nc.gpsimd.indirect_dma_start(
                        out=ygat[:, k % NY, :], out_offset=None, in_=ys_dram,
                        in_offset=bass.IndirectOffsetOnAxis(ap=y_i[:, t, j:j + 1], axis=0)).then_inc(r_yg[k % NY], 16)

        @block.tensor
        def _(pe):
            pe.sem_inc(s_xin, 1)
            pe.sem_inc(s_dut, 1)
            pe.sem_inc(s_dp, 1)
            pe.sem_inc(s_zt, 1)
            pe.sem_inc(s_sku, 1)
            def turn(dst, src, start=True, stop=True):
                k = src.shape[0]
                return nc.tensor.matmul(dst, src, ident[0:k, 0:k], start=start, stop=stop, is_transpose=True)

            pe.wait_ge(s_id, 1)
            pe.wait_ge(s_w, NW * 16)
            for ct in range(CT):
                for et in range(ET):
                    last = turn(bank[ct][:, cols(et)], w_in_nat[:, et, cols(ct)])
                last.then_inc(s_wt, 1)
            for et in range(ET):
                last = turn(bank[2][:, cols(et, XR)], xproj_nat[:, cols(et)])
            last.then_inc(s_wt, 1)
            for et in range(ET):
                last = turn(bank[3][0:DR, cols(et)], dtw_nat[:, et, :])
            last.then_inc(s_wt, 1)
            pe.wait_ge(s_wtc, 4)
            with pe.Fori(0, NB) as b:
                pe.wait_ge(s_ctx, b * 16 + 16)
                pe.wait_ge(s_rl, b * ET + 1)
                for ct in range(CT):
                    for lc in range(LC):
                        last = turn(bank[ct][:, cols(lc)], ctxn[:, lc, cols(ct)])
                last.then_inc(s_ctxt, 1)
                pe.wait_ge(s_ctxe, b * CT + CT)
                pe.wait_ge(s_dute, b * LC + 1)
                for et in range(ET):
                    for ct in range(CT):
                        last = nc.tensor.matmul(bank[2 + et][:], w_inT[:, ct, cols(et)], ctxT[:, ct, :],
                                                start=(ct == 0), stop=(ct == CT - 1))
                    last.then_inc(s_xin, 1)
                pe.wait_ge(s_u, b * ET + ET)
                for et in range(ET):
                    nc.tensor.matmul(bank[6][0:XR, :], xprojT[:, et, :], u[:, et, :], start=(et == 0), stop=(et == ET - 1))
                for lc in range(LC):
                    for et in range(ET):
                        last = nc.tensor.matmul(bank[7][:, cols(lc, NS)], u[:, et, cols(lc)], xprojT[:, et, DR:DR + NS],
                                                start=(et == 0), stop=(et == ET - 1))
                last.then_inc(s_xd, 1)
                pe.wait_ge(s_xde, b * 2 + 2)
                for et in range(ET):
                    nc.tensor.matmul(bank[et][:], dtwT[:, cols(et)], xdbl[0:DR, :], start=True, stop=True).then_inc(s_dp, 1)
                pe.wait_ge(s_du, b + 1 + 1)
                for lc in range(LC):
                    for et in range(ET):
                        last = turn(bank[4 + lc][:, cols(et)], w0[:, et, cols(lc)])
                    last.then_inc(s_dut, 1)

            pe.wait_ge(s_rl, NB * ET + 1)
            with pe.Fori(0, NB) as b:
                pe.wait_ge(s_zn, b * ET + ET)
                pe.wait_ge(s_zte, b * LC + 1)
                for lc in range(LC):
                    for et in range(ET):
                        last = turn(bank[lc][:, cols(et)], w3[:, et, cols(lc)])
                    last.then_inc(s_zt, 1)

            pe.sem_inc(s_dbu, 2 * RING)
            pe.sem_inc(s_y, RING)
            pe.wait_ge(s_zte, NB * LC + 1)
            pe.wait_ge(s_dute, NB * LC + 1)
            with pe.Fori(0, NB) as b:
                def to_channels(n, q, et):
                    m = b * NS + n
                    if et == 0:
                        pe.wait_ge(s_bua, m * (LC - 1) + LC - 1)
                        pe.wait_ge(s_bud, m + 1)
                    pe.wait_ge(s_h, m * ET + et + 1)
                    for lc in range(LC):
                        last = turn(bank[et][:, cols(lc)], dBuT[q][:, lc, cols(et)])
                    last.then_inc(s_dbu, 1)

                def add_to_y(n, et, stop=False):
                    pe.wait_ge(s_hc, (b * NS + n) * ET + et + 1 + RING)
                    for lc in range(LC):
                        last = turn(bank[4 + lc][:, cols(et)], hC[et][:, cols(lc)], start=False, stop=stop)
                    last.then_inc(s_y, 1)

                pe.wait_ge(s_skl, b * 16 + 16)
                pe.wait_ge(s_yz, b * LC + 1)
                for et in range(ET):
                    for lc in range(LC):
                        last = turn(bank[4 + lc][:, cols(et)], skip[:, et, cols(lc)], start=(et == 0), stop=False)
                last.then_inc(s_sku, 1)
                for et in range(ET):
                    to_channels(0, 0, et)
                with pe.Fori(0, NS - 2, 2) as n:
                    for q in range(2):
                        for et in range(ET):
                            add_to_y(n + q, et)
                            to_channels(n + q + 1, 1 - q, et)
                for et in range(ET):
                    add_to_y(NS - 2, et)
                    to_channels(NS - 1, 1, et)
                for et in range(ET):
                    add_to_y(NS - 1, et, stop=(et == ET - 1))

            pe.wait_ge(s_x1, NT)
            pe.wait_ge(r_gl, 32)
            pe.wait_ge(r_cst2, 4)
            for b in range(NB):
                for t in range(LC):
                    pe.wait_ge(r_xn2, b * LC + t + 1)
                    if b:
                        pe.wait_ge(r_xnte, b * LC)
                    for d in range(DM // P):
                        last = turn(bank[t][:, cols(d)], xn[:, t, cols(d)])
                    last.then_inc(r_xnt, 1)
                pe.wait_ge(r_xnte, (b + 1) * LC)
                if b:
                    pe.wait_ge(r_lgc, b)
                for t in range(LC):
                    for d in range(DM // P):
                        last = nc.tensor.matmul(bank[4][:, cols(t, NE)], xnT[:, t, cols(d)], gate_sb[:, d, :],
                                                start=(d == 0), stop=(d == DM // P - 1))
                last.then_inc(r_lg, 1)
                pe.wait_ge(r_ch, b + 1)
                if b:
                    pe.wait_ge(r_cum, b)
                nc.tensor.matmul(bank[5][:, 0:LC * NE], upper[:], chosen[:].rearrange("p t e -> p (t e)"),
                                 start=True, stop=False)
                for t in range(LC - 1):
                    later = LC - 1 - t
                    nc.tensor.matmul(bank[5][:, (t + 1) * NE:LC * NE], ones[:],
                                     chosen[:, t:t + 1, :].broadcast_to([P, later, NE]), start=False, stop=(t == LC - 2))
                for t in range(LC):
                    last = nc.tensor.matmul(bank[5][:, LC * NE:(LC + 1) * NE], ones[:], chosen[:, t, :],
                                            start=(t == 0), stop=(t == LC - 1))
                last.then_inc(r_pos, 1)

            KD = DM // P

            def turn_x(s, q):
                pe.wait_ge(r_xl[q], (s - q) * (16 // NX) + 16)
                pe.wait_ge(r_xlo, s + 1)
                for d in range(KD):
                    last = turn(bank[q % 2][:, cols(d)], xrow[q][:, cols(d)])
                last.then_inc(r_mmx, 1)

            def three(dst, lh, ll, rh, rl, start, stop):
                nc.tensor.matmul(dst, lh, rh, start=start, stop=False)
                nc.tensor.matmul(dst, lh, rl, start=False, stop=False)
                return nc.tensor.matmul(dst, ll, rh, start=False, stop=stop)

            def look_up(s):
                return pe.value_load(tab[0:1, bass.ds(s, 1)], min_val=2, max_val=2 * NE)

            def column(need, width):
                return (((need >> 1) - 1) & (NWR - 1)) * width

            def up(s, q, need):
                pe.wait_ge(r_spl, need)
                pe.wait_ge(r_xlo, s + 1 + 2)
                pe.wait_ge(r_gd, s + 1)
                for d in range(KD):
                    at = column(need, WG) + d * 2 * FI
                    last = three(bank[2 + q % 2][:, 0:2 * FI], xhi[q % 2][:, cols(d)], xlo[q % 2][:, cols(d)],
                                 whi[:, bass.ds(at, 2 * FI)], wlo[:, bass.ds(at, 2 * FI)], d == 0, d == KD - 1)
                last.then_inc(r_gu, 1)

            def turn_g(s, q):
                pe.wait_ge(r_gd, s + 1 + 2)
                pe.wait_ge(r_gh, s + 1)
                for i in range(2):
                    last = turn(bank[4 + q % 2][0:HK, cols(i)], gated[q % 2][:, cols(i, HK)])
                last.then_inc(r_gt, 1)

            def dn(s, q, need):
                pe.wait_ge(r_gh, s + 1 + 2)
                pe.wait_ge(r_ye, s + 1 + UNR - 2)
                for i in range(2):
                    last = nc.tensor.matmul(bank[6 + q % 2][:], gT[q % 2][0:HK, cols(i)],
                                            wdn[0:HK, bass.ds(column(need, WD) + i * DM, DM)], start=(i == 0), stop=(i == 1))
                last.then_inc(r_dn, 1)

            pe.wait_ge(r_tbl, 1)
            pe.wait_ge(r_cum, NB)
            pe.sem_inc(r_dn, 1)
            pe.sem_inc(r_gu, 2)
            def turn_of_slot(s, i, last=False):
                dn(s - 1, (i - 1) % UNR, look_up(s - 1))
                need = None if last else look_up(s + 1)
                turn_g(s, i)
                if not isinstance(s, int) or s + 2 < SLOTS:
                    turn_x(s + 2, (i + 2) % UNR)
                if not last:
                    up(s + 1, (i + 1) % UNR, need)

            turn_x(0, 0)
            turn_x(1, 1)
            up(0, 0, look_up(0))
            turn_g(0, 0)
            turn_x(2, 2)
            up(1, 1, look_up(1))
            with pe.Fori(0, SLOTS // UNR - 1) as rnd:
                for i in range(UNR):
                    turn_of_slot(rnd * UNR + i + 1, (i + 1) % UNR)
            for s in range(SLOTS - UNR + 1, SLOTS):
                turn_of_slot(s, s % UNR, s == SLOTS - 1)
            dn(SLOTS - 1, (SLOTS - 1) % UNR, look_up(SLOTS - 1))

        @block.scalar
        def _(act):
            act.sem_inc(s_rl, 1)
            act.sem_inc(s_dute, 1)
            act.sem_inc(s_sks, 1)
            act.sem_inc(s_cst, 1)
            act.sem_inc(s_zte, 1)
            def wait_apart(s, value):
                act.wait_ge(s, value)
                act.sem_inc(s_apart, 1)

            act.wait_ge(s_w, NW * 16)
            nc.scalar.activation(tgx[:], gx[:], ACT.Tanh).then_inc(s_tg, 1)
            nc.scalar.activation(Aexp[:], Alog[:], ACT.Exp).then_inc(s_A, 1)
            act.wait_ge(s_mv, NT)
            act.wait_ge(s_eps, 1)
            nc.scalar.activation(std[:], mv[:, :, 1], ACT.Sqrt, bias=eps[:]).then_inc(s_sd, 1)

            with act.Fori(0, NB) as b:
                act.wait_ge(s_ctxt, b + 1)
                act.wait_ge(s_xin, b * ET + 1)
                nc.scalar.copy(ctxT[:, 1, :], bank[1][:]).then_inc(s_ctxe, 1)
                act.wait_ge(s_dut, b * LC + 1)
                for et in range(ET):
                    act.wait_ge(s_xin, b * ET + et + 1 + 1)
                    nc.scalar.activation(w0[:, et, :], bank[2 + et][:], ACT.Identity, bias=cb[:, et:et + 1],
                                         scale=cw[:, et, TAPS - 1:TAPS]).then_inc(s_tap, 1)
                act.wait_ge(s_du, b + 1)
                for et in range(ET):
                    act.wait_ge(s_conv, b * ET + et + 1)
                    nc.scalar.activation(u[:, et, :], w0[:, et, :], ACT.Silu).then_inc(s_u, 1)
                act.wait_ge(s_sks, b * 16 + 1)
                for et in range(ET):
                    act.wait_ge(s_u, b * ET + et + 1)
                    nc.scalar.mul(skip[:, et, :], u[:, et, :], Dp[:, et:et + 1]).then_inc(s_skc, 1)
                act.wait_ge(s_t2, b + 1)
                for et in range(ET):
                    act.wait_ge(s_dp, b * ET + et + 1 + 1)
                    nc.scalar.activation(w1[:, et, :], bank[et][:], ACT.Abs, bias=dtb[:, et:et + 1]).then_inc(s_abs, 1)
                    nc.scalar.activation(w0[:, et, :], bank[et][:], ACT.Relu, bias=dtb[:, et:et + 1]).then_inc(s_rl, 1)
                act.wait_ge(s_abs, b * ET + ET)
                nc.scalar.activation(w2[:], w1[:], ACT.Exp, scale=-1.0).then_inc(s_ez, 1)
                act.wait_ge(s_ez, b + 1)
                nc.scalar.activation(w1[:], w2[:], ACT.Ln, bias=1.0).then_inc(s_lw, 1)
                for lc in range(LC // 2):
                    wait_apart(s_dut, b * LC + lc + 1 + 1)
                    nc.scalar.copy(tile(duT, b * LC + lc), bank[4 + lc][:]).then_inc(s_dute, 1)

            act.wait_ge(s_nm, 1)
            act.wait_ge(s_dl, NB)
            with act.Fori(0, NB) as b:
                wait_apart(s_zt, b * LC + 1)
                for et in range(ET):
                    t = b * ET + et
                    nc.scalar.activation(w3[:, et, :], tile(x1, t), ACT.Silu, bias=nmr[:, bass.ds(t, 1)],
                                         scale=rstd[:, bass.ds(t, 1)]).then_inc(s_zn, 1)
                for lc in range(LC // 2):
                    wait_apart(s_zt, b * LC + lc + 1 + 1)
                    nc.scalar.mul(tile(zT, b * LC + lc), bank[lc][:], tgx[:]).then_inc(s_zte, 1)

            act.wait_ge(s_t2, NB + 1)
            act.wait_ge(s_dut, NB * LC + 1)
            act.wait_ge(s_dute, NB * LC + 1)
            act.wait_ge(s_An, 1)
            act.wait_ge(s_sks, NB * 16 + 1)
            with act.Fori(0, NB) as b:
                def scale_b(n, q):
                    m = b * NS + n
                    wait_apart(s_dbu, m * ET + RING)
                    for lc in range(LC - 1):
                        nc.scalar.mul(dBuT[q][:, lc, :], tile(duT, b * LC + lc),
                                      BT[:, bass.ds(b, 1), bass.ds(n + lc * NS, 1)].rearrange("p o n -> p (o n)")).then_inc(s_bua, 1)

                def decay(n, q):
                    for et in range(ET):
                        k = (b * NS + n) * ET + et
                        wait_apart(s_h, k + 1)
                        nc.scalar.activation(dA[et], delta[:, bass.ds(b, 1), et, :].rearrange("p o n -> p (o n)"),
                                             ACT.Exp, scale=Aneg[:, et, bass.ds(n, 1)]).then_inc(s_dA, 1)

                act.wait_ge(s_sku, b + 1)
                act.dma_start(skip[:].rearrange("p t n -> p (t n)"),
                              skip_dram[bass.ds(b, 1)].rearrange("o p n -> (o p) n")).then_inc(s_skl, 16)
                scale_b(0, 0)
                with act.Fori(0, NS - 2, 2) as n:
                    for q in range(2):
                        scale_b(n + q + 1, 1 - q)
                        decay(n + q, q)
                scale_b(NS - 1, 1)
                decay(NS - 2, 0)
                decay(NS - 1, 1)

            act.wait_ge(r_gl, 16)
            nc.scalar.activation(tgf[:], gf[:], ACT.Tanh).then_inc(r_ex, 1)
            for b in range(NB):
                act.wait_ge(r_mv2, (b + 1) * LC)
                nc.scalar.activation(std2[:], mv2[:, :, 1], ACT.Sqrt, bias=eps[:]).then_inc(r_sd2, 1)
                for t in range(LC // 2):
                    act.wait_ge(r_xnt, b * LC + t + 1)
                    if b:
                        act.wait_ge(r_lg, b)
                    nc.scalar.copy(xnT[:, t, :], bank[t][:]).then_inc(r_xnte, 1)
                act.wait_ge(r_sub, b + 1)
                nc.scalar.activation(ex[:], ex[:], ACT.Exp).then_inc(r_ex, 1)

            def x_hi(s, q):
                act.wait_ge(r_mmx, s + 1)
                act.wait_ge(r_gu, s + 1)
                nc.scalar.copy(xhi[q % 2][:], bank[q % 2][:]).then_inc(r_xh, 1)

            act.wait_ge(r_cum, NB)
            act.sem_inc(r_gh, 2)
            nc.scalar.preload_act_table(ACT.Silu)
            x_hi(0, 0)

            def slot(s, q, more):
                if more:
                    x_hi(s + 1, (q + 1) % UNR)
                act.wait_ge(r_gu, s + 1 + 2)
                act.wait_ge(r_gd, s + 1)
                nc.scalar.activation(sg[q % 2][:], bank[2 + q % 2][:, 0:FI], ACT.Silu).then_inc(r_sg, 1)
                act.wait_ge(r_gt, s + 1)
                act.wait_ge(r_dn, s + 1)
                nc.scalar.copy(gT[q % 2][0:HK, :], bank[4 + q % 2][0:HK, 0:2 * P]).then_inc(r_gh, 1)

            with act.Fori(0, SLOTS // UNR - 1) as rnd:
                for q in range(UNR):
                    slot(rnd * UNR + q, q, True)
            for q in range(UNR):
                slot(SLOTS - UNR + q, q, q < UNR - 1)

        @block.vector
        def _(dve):
            dve.sem_inc(s_du, 1)
            dve.sem_inc(s_yz, 1)
            nc.vector.memset(eps[:], LN_EPS).then_inc(s_eps, 1)
            dve.wait_ge(s_A, 1)
            nc.vector.tensor_scalar_mul(Aneg[:], Aexp[:], -1.0).then_inc(s_An, 1)
            for ct in range(CT):
                dve.wait_ge(s_wt, ct + 1)
                nc.vector.tensor_copy(w_inT[:, ct, :], bank[ct][:]).then_inc(s_wtc, 1)
            dve.wait_ge(s_wt, CT + 1)
            nc.vector.tensor_copy(xprojT[:].rearrange("p t n -> p (t n)"), bank[2][:, 0:ET * XR]).then_inc(s_wtc, 1)
            dve.wait_ge(s_wt, CT + 2)
            nc.vector.tensor_copy(dtwT[:], bank[3][0:DR, :]).then_inc(s_wtc, 1)
            dve.wait_ge(s_x, 16)
            for t in range(NT):
                nc.vector.bn_stats(stats[:, t, :], x1[:, t, :]).then_inc(s_st, 1)
            for t in range(NT):
                dve.wait_ge(s_st, t + 1)
                nc.vector.bn_aggr(mv[:, t, :], stats[:, t, :]).then_inc(s_mv, 1)
            dve.wait_ge(s_sd, 1)
            nc.vector.reciprocal(rstd[:], std[:]).then_inc(s_rs, 1)
            dve.wait_ge(s_rs, 1)
            nc.vector.scalar_tensor_tensor(out=nmr[:], in0=mv[:, :, 0], scalar=-1.0, in1=rstd[:],
                                           op0=ALU.mult, op1=ALU.mult).then_inc(s_nm, 1)

            with dve.Fori(0, NB) as b:
                dve.wait_ge(s_ctxt, b + 1)
                dve.wait_ge(s_xin, b * ET + 1)
                nc.vector.tensor_copy(ctxT[:, 0, :], bank[0][:]).then_inc(s_ctxe, 1)
                for j, k in enumerate(range(TAPS - 2, -1, -1)):
                    s = TAPS - 1 - k
                    for et in range(ET):
                        if j == 0:
                            dve.wait_ge(s_tap, b * ET + et + 1)
                        else:
                            dve.wait_ge(s_cv, b * (ET * (TAPS - 2)) + (j - 1) * ET + et + 1)
                        nc.vector.scalar_tensor_tensor(
                            out=w0[:, et, s:], in0=bank[2 + et][:, 0:L - s], scalar=cw[:, et, k:k + 1],
                            in1=w0[:, et, s:], op0=ALU.mult, op1=ALU.add,
                        ).then_inc(s_conv if k == 0 else s_cv, 1)
                dve.wait_ge(s_xd, b + 1)
                dve.wait_ge(s_dp, b * ET + 1)
                dve.wait_ge(s_cst, b * 16 + 1)
                nc.vector.tensor_copy(xdbl[:], bank[6][0:XR, :]).then_inc(s_xde, 1)
                nc.vector.tensor_copy(tile(BT, b), bank[7][:, 0:LC * NS]).then_inc(s_xde, 1)
                dve.wait_ge(s_ez, b + 1)
                nc.vector.tensor_scalar(w3[:], w2[:], 1.0, 1.0, ALU.add, ALU.subtract).then_inc(s_wm, 1)
                dve.wait_ge(s_t2, b + 1 + 1)
                dve.wait_ge(s_rl, b * ET + ET + 1)
                nc.vector.tensor_tensor(tile(delta[:].rearrange("p b t n -> p b (t n)"), b), w0[:].rearrange("p t n -> p (t n)"),
                                        w3[:].rearrange("p t n -> p (t n)"), ALU.add).then_inc(s_dl, 1)
                dve.wait_ge(s_dl, b + 1)
                nc.vector.tensor_tensor(w0[:].rearrange("p t n -> p (t n)"), tile(delta[:].rearrange("p b t n -> p b (t n)"), b),
                                        u[:].rearrange("p t n -> p (t n)"), ALU.mult).then_inc(s_du, 1)
                for lc in range(LC // 2, LC):
                    dve.wait_ge(s_dut, b * LC + lc + 1 + 1)
                    nc.vector.tensor_copy(tile(duT, b * LC + lc), bank[4 + lc][:]).then_inc(s_dute, 1)

            dve.wait_ge(s_tg, 1)
            with dve.Fori(0, NB) as b:
                for lc in range(LC // 2, LC):
                    dve.wait_ge(s_zt, b * LC + lc + 1 + 1)
                    nc.vector.tensor_scalar_mul(tile(zT, b * LC + lc), bank[lc][:], tgx[:]).then_inc(s_zte, 1)

            dve.sem_inc(s_h, RING)
            dve.wait_ge(s_t2, NB + 1)
            dve.wait_ge(s_dute, NB * LC + 1)
            with dve.Fori(0, NB) as b:
                def scale_b(n, q):
                    dve.wait_ge(s_dbu, (b * NS + n) * ET + RING)
                    nc.vector.tensor_scalar_mul(
                        dBuT[q][:, LC - 1, :], tile(duT, b * LC + LC - 1),
                        BT[:, bass.ds(b, 1), bass.ds(n + (LC - 1) * NS, 1)].rearrange("p o n -> p (o n)")).then_inc(s_bud, 1)

                def scans(n):
                    for et in range(ET):
                        k = (b * NS + n) * ET + et
                        dve.wait_ge(s_dbu, k + 1 + 2 * RING)
                        dve.wait_ge(s_dA, k + 1)
                        dve.wait_ge(s_hc, k + 1)
                        nc.vector.tensor_tensor_scan(out=h[et], data0=dA[et], data1=bank[et][:], initial=0.0,
                                                     op0=ALU.mult, op1=ALU.add).then_inc(s_h, 1)

                scale_b(0, 0)
                with dve.Fori(0, NS - 2, 2) as n:
                    for q in range(2):
                        scale_b(n + q + 1, 1 - q)
                        scans(n + q)
                scale_b(NS - 1, 1)
                scans(NS - 2)
                scans(NS - 1)
                dve.wait_ge(s_y, (b + 1) * (NS * ET) + RING)
                for lc in range(LC):
                    t = b * LC + lc
                    nc.vector.tensor_tensor(tile(zT, t), bank[4 + lc][:], tile(zT, t), ALU.mult).then_inc(s_yz, 1)

            dve.wait_ge(s_x1, NT)
            nc.vector.memset(cum[:], 0.0).then_inc(r_cumb, 1)
            dve.wait_ge(r_cumb, 1)
            dve.wait_ge(r_cst2, 4)
            for b in range(NB):
                for t in range(LC):
                    nc.vector.bn_stats(stats2[:, t, :], x1[:, b * LC + t, :]).then_inc(r_st2, 1)
                for t in range(LC):
                    dve.wait_ge(r_st2, b * LC + t + 1)
                    nc.vector.bn_aggr(mv2[:, t, :], stats2[:, t, :]).then_inc(r_mv2, 1)
                dve.wait_ge(r_sd2, b + 1)
                nc.vector.reciprocal(rstd2[:], std2[:]).then_inc(r_rs2, 1)
                dve.wait_ge(r_rs2, b + 1)
                nc.vector.scalar_tensor_tensor(out=nmr2[:], in0=mv2[:, :, 0], scalar=-1.0, in1=rstd2[:],
                                               op0=ALU.mult, op1=ALU.mult).then_inc(r_nm2, 1)
                dve.wait_ge(r_nm2, b + 1)
                if b:
                    dve.wait_ge(r_sc, b * LC * TOPK * 16)
                    dve.wait_ge(r_xnt, b * LC)
                for t in range(LC):
                    nc.vector.tensor_scalar(xn[:, t, :], x1[:, b * LC + t, :], rstd2[:, t:t + 1], nmr2[:, t:t + 1],
                                            ALU.mult, ALU.add).then_inc(r_xn2, 1)
                for t in range(LC // 2, LC):
                    dve.wait_ge(r_xnt, b * LC + t + 1)
                    if b:
                        dve.wait_ge(r_lg, b)
                    nc.vector.tensor_copy(xnT[:, t, :], bank[t][:]).then_inc(r_xnte, 1)
                dve.wait_ge(r_lg, b + 1)
                nc.vector.tensor_copy(logit[:].rearrange("p t e -> p (t e)"), bank[4][:, 0:LC * NE]).then_inc(r_lgc, 1)
                dve.wait_ge(r_lgc, b + 1)
                for t in range(LC):
                    nc.vector.max(out=top[:, t, :], in_=logit[:, t, :]).then_inc(r_mx, 1)
                for t in range(LC):
                    dve.wait_ge(r_mx, b * LC + t + 1)
                    nc.vector.max_index(out=topi[:, t, :], in_max=top[:, t, :], in_values=logit[:, t, :]).then_inc(r_mi, 1)
                nc.vector.tensor_tensor(ex[:], top[:, :, 0:TOPK], top[:, :, 0:1].broadcast_to([P, LC, TOPK]),
                                        ALU.subtract).then_inc(r_sub, 1)
                dve.wait_ge(r_mi, (b + 1) * LC)
                mine = topf[:, b * LC * TOPK:(b + 1) * LC * TOPK]
                nc.vector.tensor_copy(mine.rearrange("p (t j) -> p t j", j=TOPK), topi[:, :, 0:TOPK]).then_inc(r_tf, 1)
                dve.wait_ge(r_tf, b + 1)
                nc.vector.tensor_tensor(onehot[:], eidx[:].unsqueeze(1).broadcast_to([P, LC * TOPK, NE]),
                                        mine.unsqueeze(2).broadcast_to([P, LC * TOPK, NE]), ALU.is_equal).then_inc(r_oh, 1)
                dve.wait_ge(r_oh, b + 1)
                with nc.allow_low_precision(reason="zeros and ones"):
                    nc.vector.tensor_reduce(chosen[:], onehot[:].rearrange("p (t j) e -> p t e j", j=TOPK), AX.X,
                                            ALU.add).then_inc(r_ch, 1)
                dve.wait_ge(r_ex, b + 2)
                nc.vector.tensor_reduce(exs[:], ex[:], AX.X, ALU.add).then_inc(r_exsum, 1)
                dve.wait_ge(r_exsum, b + 1)
                nc.vector.reciprocal(exs[:], exs[:]).then_inc(r_exr, 1)
                dve.wait_ge(r_exr, b + 1)
                nc.vector.scalar_tensor_tensor(out=weight[:, b * LC:(b + 1) * LC, :], in0=ex[:], scalar=tgf[:],
                                               in1=exs[:].unsqueeze(2).broadcast_to([P, LC, TOPK]),
                                               op0=ALU.mult, op1=ALU.mult).then_inc(r_w, 1)
                nc.vector.tensor_tensor(cumb[:], cum[:], ebase[:], ALU.add).then_inc(r_cumb, 1)
                dve.wait_ge(r_cumb, b + 2)
                dve.wait_ge(r_pos, b + 1)
                nc.vector.tensor_tensor(picked[:, 0:LC, :], bank[5][:, 0:LC * NE].rearrange("p (t e) -> p t e", e=NE),
                                        cumb[:].unsqueeze(1).broadcast_to([P, LC, NE]), ALU.add).then_inc(r_posb, 1)
                nc.vector.tensor_tensor(cum[:], cum[:], bank[5][:, LC * NE:(LC + 1) * NE], ALU.add).then_inc(r_cum, 1)
                dve.wait_ge(r_posb, b + 1)
                nc.vector.tensor_tensor(onehot[:].rearrange("p (t j) e -> p t j e", j=TOPK),
                                        onehot[:].rearrange("p (t j) e -> p t j e", j=TOPK),
                                        picked[:, 0:LC, :].unsqueeze(2).broadcast_to([P, LC, TOPK, NE]), ALU.mult).then_inc(r_pk, 1)
                dve.wait_ge(r_pk, b + 1)
                nc.vector.tensor_reduce(slot_f[:, b * LC:(b + 1) * LC, :].rearrange("p t j -> p (t j)"), onehot[:], AX.X,
                                        ALU.add).then_inc(r_sf, 1)
                dve.wait_ge(r_sf, b + 1)
                nc.vector.tensor_copy(slot_i[:, b * LC:(b + 1) * LC, :], slot_f[:, b * LC:(b + 1) * LC, :]).then_inc(r_si, 1)
                dve.wait_ge(r_cum, b + 1)

            steps = [0]

            def step(ins):
                steps[0] += 1
                ins.then_inc(r_tb, 1)
                dve.wait_ge(r_tb, steps[0])

            step(nc.vector.tensor_scalar(nti[:], cum[:], float(P - 1), None, ALU.add))
            step(nc.vector.tensor_scalar(nti[:], nti[:], P.bit_length() - 1, None, ALU.arith_shift_right))
            step(nc.vector.tensor_copy(ntf[:], nti[:]))
            step(nc.vector.memset(ntone[:], 1.0))
            step(nc.vector.tensor_tensor_scan(out=ntcum[:], data0=ntone[:], data1=ntf[:], initial=0.0,
                                              op0=ALU.mult, op1=ALU.add))
            step(nc.vector.tensor_scalar(last_slot[:], ntcum[0:1, :], 1.0, None, ALU.add))
            step(nc.vector.tensor_tensor(shift[:], cum[:], ebase[:], ALU.add))
            step(nc.vector.scalar_tensor_tensor(out=shift[:], in0=ntcum[:], scalar=float(-P), in1=shift[:],
                                                op0=ALU.mult, op1=ALU.add))
            over = [1, SLOTS, NE]
            step(nc.vector.tensor_tensor(compare, sidx[:].unsqueeze(2).broadcast_to(over),
                                         ntcum[0:1, :].unsqueeze(1).broadcast_to(over), ALU.is_ge))
            step(nc.vector.tensor_reduce(slot_e[:], compare, AX.X, ALU.add))
            step(nc.vector.tensor_tensor(compare, slot_e[:].unsqueeze(2).broadcast_to(over),
                                         eidx[0:1, :].unsqueeze(1).broadcast_to(over), ALU.is_equal))
            step(nc.vector.tensor_tensor(compare, compare, shift[0:1, :].unsqueeze(1).broadcast_to(over), ALU.mult))
            step(nc.vector.tensor_reduce(srow[:], compare, AX.X, ALU.add))
            step(nc.vector.scalar_tensor_tensor(out=srow[:], in0=sidx[:], scalar=float(P), in1=srow[:],
                                                op0=ALU.mult, op1=ALU.add))
            step(nc.vector.tensor_scalar(svalid[:], slot_e[:], float(NE), None, ALU.is_lt))
            step(nc.vector.scalar_tensor_tensor(out=stmp[:], in0=srow[:], scalar=float(-DUMMY), in1=svalid[:],
                                                op0=ALU.add, op1=ALU.mult))
            step(nc.vector.tensor_scalar(tab[:, SLOTS:2 * SLOTS], stmp[:], float(DUMMY), None, ALU.add))
            step(nc.vector.tensor_scalar(slot_e[:], slot_e[:], float(NE - 1), None, ALU.min))
            step(nc.vector.tensor_scalar(tab[:, 0:SLOTS], slot_e[:], 2.0, 2.0, ALU.mult, ALU.add))
            dve.sem_inc(r_tbl, 1)
            over = [P, NT * TOPK, NE]
            match = ygat[:, :, :].rearrange("p a b -> p (a b)")[:, 0:NT * TOPK * NE].rearrange("p (s e) -> p s e", e=NE)
            step(nc.vector.tensor_tensor(match, topf[:].unsqueeze(2).broadcast_to(over),
                                         eidx[:].unsqueeze(1).broadcast_to(over), ALU.is_equal))
            step(nc.vector.tensor_tensor(match, match, shift[:].unsqueeze(1).broadcast_to(over), ALU.mult))
            mine = picked[:].rearrange("p a b -> p (a b)")[:, 0:NT * TOPK]
            step(nc.vector.tensor_reduce(mine, match, AX.X, ALU.add))
            nc.vector.tensor_tensor(y_i[:].rearrange("p t j -> p (t j)"), slot_f[:].rearrange("p t j -> p (t j)"),
                                    mine, ALU.subtract).then_inc(r_yi, 1)

            def x_lo(s, q):
                dve.wait_ge(r_xh, s + 1)
                dve.wait_ge(r_gu, s + 1)
                nc.vector.tensor_tensor(xlo[q % 2][:], bank[q % 2][:], xhi[q % 2][:].bitcast(F32), ALU.subtract).then_inc(r_xlo, 1)

            def y_out(s, q):
                dve.wait_ge(r_dn, s + 1 + 1)
                if not isinstance(s, int) or s >= NX:
                    dve.wait_ge(r_ys[q], (s - q) * (16 // NX))
                nc.vector.tensor_copy(yrow[q][:], bank[6 + q % 2][:]).then_inc(r_ye, 1)

            def slot(s, q, first, more):
                if more:
                    x_lo(s + 1, (q + 1) % UNR)
                dve.wait_ge(r_sg, s + 1)
                if not first:
                    dve.wait_ge(r_gt, s)
                nc.vector.tensor_tensor(gated[q % 2][:], bank[2 + q % 2][:, FI:2 * FI], sg[q % 2][:], ALU.mult).then_inc(r_gd, 1)
                if not first:
                    y_out(s - 1, (q - 1) % UNR)

            dve.sem_inc(r_xlo, 2)
            dve.sem_inc(r_gd, 2)
            dve.sem_inc(r_ye, UNR)
            x_lo(0, 0)
            for s in range(UNR + 1):
                slot(s, s % UNR, s == 0, True)
            with dve.Fori(1, SLOTS // UNR - 1) as rnd:
                for i in range(UNR):
                    slot(rnd * UNR + i + 1, (i + 1) % UNR, False, True)
            for s in range(SLOTS - UNR + 1, SLOTS):
                slot(s, s % UNR, False, s + 1 < SLOTS)
            y_out(SLOTS - 1, (SLOTS - 1) % UNR)
            for t in range(NT):
                for j in range(TOPK):
                    k = t * TOPK + j
                    dve.wait_ge(r_yg[k % NY], (k // NY + 1) * 16)
                    if k:
                        dve.wait_ge(r_acc, k)
                    nc.vector.scalar_tensor_tensor(out=x1[:, t, :], in0=ygat[:, k % NY, :], scalar=weight[:, t, j:j + 1],
                                                   in1=x1[:, t, :], op0=ALU.mult, op1=ALU.add).then_inc(r_acc, 1)


_INS = ['x', 'ctx_1024', 'g_xattn', 'g_ffn', 'L0_xattn_in_proj_w', 'L0_xattn_conv_w', 'L0_xattn_conv_b',
        'L0_xattn_x_proj_w', 'L0_xattn_dt_proj_w', 'L0_xattn_dt_proj_b', 'L0_xattn_A_log', 'L0_xattn_D',
        'L0_ffn_gate', 'L0_ffn_gate_up_proj', 'L0_ffn_down_proj']


def kernel(**inputs):
    import numpy as _np
    import concourse.bacc as _bacc
    from concourse import mybir as _mybir
    from concourse.bass_utils import run_bass_kernel_spmd as _run

    nc = _bacc.Bacc("TRN2", target_bir_lowering=False, num_devices=1)
    arrays, args = {}, []
    for name in _INS:
        a = _np.ascontiguousarray(inputs[name])
        arrays[f"in_{name}_dram"] = a
        args.append(nc.dram_tensor(f"in_{name}_dram", a.shape, _mybir.dt.from_np(a.dtype), kind="ExternalInput").ap())
    args.append(nc.dram_tensor("out_dram", inputs['x'].shape, _mybir.dt.float32, kind="ExternalOutput").ap())
    flamingo_kernel(nc, *args)
    r = _run(nc, [arrays], core_ids=[0])
    return r.results[0]["out_dram"]
```

```python
from contextlib import ExitStack

import concourse.bass as bass
from concourse import mybir

P = 128
F32 = mybir.dt.float32
F32R = mybir.dt.float32r
BF16 = mybir.dt.bfloat16
I32 = mybir.dt.int32
U32 = mybir.dt.uint32
ALU = mybir.AluOpType
ACT = mybir.ActivationFunctionType
AX = mybir.AxisListType
LN_EPS = 1e-5


def flamingo_kernel(nc, x, ctx_in, g_xattn, g_ffn, in_proj_w, conv_w, conv_b, x_proj_w,
                    dt_proj_w, dt_proj_b, A_log, D, gate, gate_up, down, out):
    NB, L, DM = x.shape
    DC = ctx_in.shape[2]
    DI = in_proj_w.shape[0]
    TAPS = conv_w.shape[1]
    DR = dt_proj_w.shape[1]
    NS = A_log.shape[1]
    assert DI == L == DM
    ET, LC, CT = DI // P, L // P, DC // P
    NT = NB * LC
    XR = DR + 2 * NS
    PC = 2 * ET - 1
    RING = ET

    NE = gate.shape[1]
    TOPK = 4
    FI = gate_up.shape[2] // 2
    TOK = NB * L
    UNR = 4
    SLOTS = -(-(TOK * TOPK // P + NE - 1) // UNR) * UNR
    REGION = P + TOK
    DUMMY = NE * REGION
    HK = FI // 2

    stack = ExitStack()
    first_branch = ExitStack()
    with stack:
        def keep(name, shape, dt=F32):
            return stack.enter_context(nc.sbuf_tensor(name, shape, dt))

        def sb(name, shape, dt=F32):
            return first_branch.enter_context(nc.sbuf_tensor(name, shape, dt))

        def sem(name):
            return stack.enter_context(nc.semaphore(name))

        bank = [stack.enter_context(nc.psum_tensor(f"bank{i}", [P, 512], F32)) for i in range(8)]
        c_dram = nc.dram_tensor("c_rows", [NB * NS, L], F32, kind="Internal").ap()
        skip_dram = nc.dram_tensor("skip_rows", [NB, P, ET * L], F32, kind="Internal").ap()

        xs_dram = nc.dram_tensor("tokens_by_expert", [DUMMY + P, DM], F32, kind="Internal").ap()
        ys_dram = nc.dram_tensor("results_by_expert", [SLOTS * P, DM], F32, kind="Internal").ap()

        ident = keep("ident", [P, P])
        x1 = keep("x1", [P, NT, DM])
        eps = keep("eps", [P, 1])
        zeros = keep("zeros", [P, DM])
        slot_f = keep("slot_f", [P, NT, TOPK])
        slot_i = keep("slot_i", [P, NT, TOPK], I32)
        y_i = keep("y_i", [P, NT, TOPK], I32)
        weight = keep("weight", [P, NT, TOPK])
        gf = keep("gf", [P, 1])
        tgf = keep("tgf", [P, 1])
        stats = keep("stats", [P, NT, 6])
        mv = keep("mv", [P, NT, 2])
        std = keep("std", [P, NT])
        rstd = keep("rstd", [P, NT])
        nmr = keep("nmr", [P, NT])
        w_in_nat = sb("w_in_nat", [P, ET, DC])
        w_inT = sb("w_inT", [P, CT, DI])
        xproj_nat = sb("xproj_nat", [XR, DI])
        xprojT = sb("xprojT", [P, ET, XR])
        dtw_nat = sb("dtw_nat", [P, ET, DR])
        dtwT = sb("dtwT", [DR, DI])
        cw = sb("cw", [P, ET, TAPS])
        cb = sb("cb", [P, ET])
        dtb = sb("dtb", [P, ET])
        Dp = sb("Dp", [P, ET])
        Alog = sb("Alog", [P, ET, NS])
        Aexp = sb("Aexp", [P, ET, NS])
        Aneg = sb("Aneg", [P, ET, NS])
        gx = sb("gx", [P, 1])
        tgx = sb("tgx", [P, 1])
        zT = sb("zT", [P, NT, DI])
        delta = sb("delta", [P, NB, ET, L])
        duT = sb("duT", [P, NT, DI])
        BT = sb("BT", [P, NB, LC * NS])
        ctxn = sb("ctxn", [P, LC, DC])
        ctxT = sb("ctxT", [P, CT, L])
        times_c_buf = sb("times_c", [P, ET, L])
        w0, w1, w2, w3 = [sb(f"work{i}", [P, ET, L]) for i in range(4)]
        xdbl = sb("xdbl", [XR, L])
        skip = sb("skip", [P, ET, L])
        u = [zT[:, b * ET:(b + 1) * ET, :] for b in range(NB)]
        expneg = [duT[:, b * ET:(b + 1) * ET, :] for b in range(NB)]
        conv = w0
        rounding = [w1, w2]
        logw = w3
        silu_z = [w0, w1]
        dBuT = [w0, w1]
        dA = [w2[:, i, :] for i in range(RING)]
        h = [w3[:, i, :] for i in range(RING)]
        hC = [times_c_buf[:, i, :] for i in range(RING)]
        crow = [ctxT[:, i, :] for i in range(2)]
        first_branch.close()

        gate_sb = keep("gate_sb", [P, DM // P, NE])
        upper = keep("upper", [P, P], BF16)
        ones = keep("ones", [P, P], BF16)
        eidx = keep("eidx", [P, NE])
        ebase = keep("ebase", [P, NE])
        xn_own = keep("xn", [P, LC, DM])
        xnT = keep("xnT", [P, LC, DM])
        logit = keep("logit", [P, LC, NE])
        top = keep("top", [P, LC, 8])
        topi = keep("topi", [P, LC, 8], U32)
        topf = keep("topf", [P, NT * TOPK])
        ex = keep("ex", [P, LC, TOPK])
        exs = keep("exs", [P, LC])
        onehot = keep("onehot", [P, LC * TOPK, NE])
        picked = keep("picked", [P, LC * TOPK, NE])
        chosen = keep("chosen", [P, LC, NE], BF16)
        cum = keep("cum", [P, NE])
        cumb = keep("cumb", [P, NE])
        nti = keep("nti", [P, NE], I32)
        ntf = keep("ntf", [P, NE])
        ntcum = keep("ntcum", [P, NE])
        ntone = keep("ntone", [P, NE])
        shift = keep("shift", [P, NE])
        sidx = keep("sidx", [1, SLOTS])
        slot_e = keep("slot_e", [1, SLOTS])
        tab = keep("tab", [1, 2 * SLOTS], I32)
        last_slot = keep("last_slot", [1, NE], I32)
        srow = keep("srow", [1, SLOTS])
        svalid = keep("svalid", [1, SLOTS])
        stmp = keep("stmp", [1, SLOTS])
        NWR = 4
        WG, WD = (DM // P) * 2 * FI, 2 * DM
        raw = [keep(f"raw{i}", [P, WG]) for i in range(2)]
        whi = keep("whi", [P, NWR * WG], F32R)
        wlo = keep("wlo", [P, NWR * WG], F32R)
        wdn = keep("wdn", [P, NWR * WD])
        NX = 4
        xrows = keep("xrows", [P, NX, DM])
        xrow = [xrows[:, i, :] for i in range(NX)]
        xhi = [keep(f"xhi{i}", [P, DM], F32R) for i in range(2)]
        xlo = [keep(f"xlo{i}", [P, DM], F32R) for i in range(2)]
        sg = [keep(f"sg{i}", [P, FI]) for i in range(2)]
        gated = [keep(f"gated{i}", [P, FI]) for i in range(2)]
        gT = [keep(f"gT{i}", [P, 2 * P]) for i in range(2)]
        yrows = keep("yrows", [P, NX, DM])
        yrow = [yrows[:, i, :] for i in range(NX)]
        NY = 6
        ygat = keep("ygat", [P, NY, DM])
        xn = [ygat[:, 0:LC, :], xn_own, xrows, yrows]
        assert NB == len(xn) and LC == NX
        compare = ygat[0:1, :, :].rearrange("p a b -> p (a b)")[:, 0:SLOTS * NE].rearrange("p (s e) -> p s e", e=NE)

        s_w = sem("weights_loaded")
        s_x = sem("x_loaded")
        s_id0 = sem("ident_zeroed")
        s_eps = sem("eps_ready")
        s_apart = sem("act_waits_passed")
        s_id = sem("ident_ready")
        s_ctx = sem("ctx_loaded")
        s_wt = sem("weights_transposed")
        s_wtc = sem("weights_copied")
        s_ctxt = sem("ctx_transposed")
        s_ctxe = sem("ctx_copied")
        s_xin = sem("in_proj_done")
        s_tap = sem("last_tap_done")
        s_cv = sem("conv_chain")
        s_conv = sem("conv_done")
        s_u = sem("u_ready")
        s_xd = sem("x_proj_done")
        s_bt = sem("x_proj_transposed")
        s_xde = sem("x_proj_copied")
        s_cst = sem("c_rows_stored")
        s_dp = sem("dt_proj_done")
        s_abs = sem("abs_done")
        s_ez = sem("expneg_done")
        s_lw = sem("ln_done")
        s_wm = sem("rounded_minus_one")
        s_t1 = sem("rounding_error_done")
        s_t2 = sem("log1p_done")
        s_rl = sem("relu_done")
        s_dl = sem("delta_ready")
        s_du = sem("du_ready")
        s_dut = sem("du_transposed")
        s_dute_a = sem("duT_copied_by_act")
        s_dute_d = sem("duT_copied_by_dve")
        s_skc = sem("skip_computed")
        s_sks = sem("skip_stored")
        s_skl = sem("skip_loaded")
        s_sku = sem("skip_used")
        s_A = sem("A_exp_done")
        s_An = sem("A_negated")
        s_tg = sem("tanh_g_ready")
        s_st = sem("stats_done")
        s_mv = sem("mean_var_done")
        s_sd = sem("std_done")
        s_rs = sem("rstd_done")
        s_nm = sem("nmr_done")
        s_zn = sem("silu_z_done")
        s_zt = sem("z_transposed")
        s_zte_a = sem("zT_copied_by_act")
        s_zte_d = sem("zT_copied_by_dve")
        s_bua = sem("dBuT_scaled_act")
        s_bud = sem("dBuT_scaled_dve")
        s_dbu = sem("dBu_in_psum")
        s_h = sem("scan_done")
        s_hc = sem("hC_ready")
        s_hcd = sem("hC_ready_by_dve")
        s_y = sem("y_accumulated")
        s_dA = sem("dA_ready")
        s_c = [sem(f"c_row_loaded{i}") for i in range(2)]
        s_yz = sem("y_times_z")
        s_x1 = sem("x1_ready")
        r_gl = sem("gate_and_g_loaded")
        r_cst0 = sem("router_constants_filled")
        r_cst2 = sem("router_constants_ready")
        r_st2 = sem("stats2_done")
        r_mv2 = sem("mean_var2_done")
        r_sd2 = sem("std2_done")
        r_rs2 = sem("rstd2_done")
        r_nm2 = sem("nmr2_done")
        r_xn2 = sem("normed_ready")
        r_xnt = sem("normed_transposed")
        r_xnte = sem("normed_copied")
        r_lg = sem("logits_done")
        r_lgc = sem("logits_copied")
        r_mx = sem("top8_done")
        r_mi = sem("top8_index_done")
        r_tf = sem("index_float_done")
        r_sub = sem("max_subtracted")
        r_ex = sem("exp_done")
        r_exsum = sem("exp_sum_done")
        r_exr = sem("exp_sum_inverted")
        r_w = sem("weights_of_tokens_done")
        r_oh = sem("onehot_done")
        r_ch = sem("chosen_done")
        r_pos = sem("positions_done")
        r_posb = sem("rows_based")
        r_cumb = sem("base_done")
        r_cum = sem("counts_added")
        r_pk = sem("picked_done")
        r_sf = sem("rows_float_done")
        r_si = sem("rows_ready")
        r_zero = sem("zeros_ready")
        r_zst = sem("zeros_stored")
        r_sc = [sem(f"tokens_scattered{b}") for b in range(NB)]
        r_tb = sem("table_step")
        r_tbl = sem("table_ready")
        r_hi = sem("weights_hi_done")
        r_spl = sem("weights_split")
        r_mmx = sem("x_transposed")
        r_xh = sem("xhi_ready")
        r_gu = sem("gate_up_done")
        r_sg = sem("silu_g_ready")
        r_gd = sem("gated_ready")
        r_gt = sem("gated_transposed")
        r_gh = sem("gT_ready")
        r_dnl = sem("down_loaded")
        r_dn = sem("down_done")
        r_ye = sem("y_copied")
        r_xlo = sem("xlo_ready")
        r_raw = [sem(f"weights_loaded{i}") for i in range(2)]
        r_xl = [sem(f"x_rows_loaded{i}") for i in range(NX)]
        r_ys = [sem(f"y_rows_stored{i}") for i in range(NX)]
        r_yg = [sem(f"y_rows_gathered{i}") for i in range(6)]
        r_acc = sem("y_added")
        r_yi = sem("rows_of_y_ready")
        r_apart = sem("pool_waits_passed")
        r_out = sem("out_stored")

        x_rows = x.rearrange("b (c p) d -> p (b c) d", p=P)
        ctx_rows = ctx_in.rearrange("b (c p) d -> b p c d", p=P)
        NW = 9
        block = stack.enter_context(nc.Block())

        def cols(i, n=P):
            return slice(i * n, (i + 1) * n)

        def tile(t, i, k=1):
            return t[:, bass.ds(i, k), :].rearrange("p t n -> p (t n)")

        @block.sync
        def _(sp):
            sp.dma_start(w_in_nat[:], in_proj_w.rearrange("(t p) d -> p t d", p=P)).then_inc(s_w, 16)
            sp.dma_start(ctxn[:], ctx_rows[0]).then_inc(s_ctx, 16)
            sp.dma_start(xproj_nat[:], x_proj_w).then_inc(s_w, 16)
            sp.dma_start(dtw_nat[:], dt_proj_w.rearrange("(t p) r -> p t r", p=P)).then_inc(s_w, 16)
            sp.dma_start(cw[:], conv_w.rearrange("(t p) k -> p t k", p=P)).then_inc(s_w, 16)
            sp.dma_start(Alog[:], A_log.rearrange("(t p) n -> p t n", p=P)).then_inc(s_w, 16)
            for dst, src in ((cb, conv_b), (dtb, dt_proj_b), (Dp, D)):
                sp.dma_start(dst[:], src.rearrange("(t p) -> p t", p=P), allow_slow_non_contiguous=True).then_inc(s_w, 16)
            sp.dma_start(gx[:], g_xattn.partition_broadcast(P)).then_inc(s_w, 16)
            sp.dma_start(gf[:], g_ffn.partition_broadcast(P)).then_inc(r_gl, 16)

            def load_ctx(b):
                sp.wait_ge(s_ctxt, b)
                sp.dma_start(ctxn[:], ctx_rows[b]).then_inc(s_ctx, 16)

            load_ctx(1)
            for b in range(NB):
                if b + 2 < NB:
                    load_ctx(b + 2)
                sp.dma_start(x1[:, b * LC:(b + 1) * LC, :], x_rows[:, b * LC:(b + 1) * LC, :]).then_inc(s_x, 16)
                sp.wait_ge(s_xde, b * 2 + 1)
                sp.dma_start(c_dram[b * NS:(b + 1) * NS, :], xdbl[DR + NS:XR, :]).then_inc(s_cst, 16)
                sp.wait_ge(s_skc, b * ET + ET)
                sp.dma_start(skip_dram[b], skip[:].rearrange("p t n -> p (t n)")).then_inc(s_sks, 16)
                if b == 0:
                    sp.wait_ge(r_zero, 1)
                for e in range(b * (NE + 1) // NB, (b + 1) * (NE + 1) // NB):
                    sp.dma_start(xs_dram[e * REGION:e * REGION + P, :], zeros[:]).then_inc(r_zst, 16)

            sp.wait_ge(s_cst, NB * 16)
            sp.wait_ge(s_xin, NB * ET)
            for q in range(2):
                sp.dma_start(crow[q], c_dram[q:q + 1, :].partition_broadcast(P)).then_inc(s_c[q], 16)
            with sp.Fori(1, NB * NS // 2) as j:
                for q in range(2):
                    sp.wait_ge(s_y, j * (2 * ET) + q * ET)
                    sp.dma_start(crow[q], c_dram[bass.ds(j * 2 + q, 1), :].partition_broadcast(P)).then_inc(s_c[q], 16)

            sp.wait_ge(s_x1, NT)
            sp.dma_start(gate_sb[:], gate.rearrange("(k p) e -> p k e", p=P)).then_inc(r_gl, 16)

            def load_gate_up(e, q):
                sp.dma_start(raw[q][:].rearrange("p (k f) -> p k f", f=2 * FI),
                             gate_up[bass.ds(e, 1)].rearrange("o (k p) f -> p (o k) f", p=P)).then_inc(r_raw[q], 16)

            def load_down(e, r):
                sp.dma_start(wdn[0:HK, r * WD:(r + 1) * WD].rearrange("p (k n) -> p k n", n=DM),
                             down[bass.ds(e, 1)].rearrange("o (k p) n -> p (o k) n", p=HK)).then_inc(r_dnl, 16)

            load_gate_up(0, 0)
            load_gate_up(1, 1)
            load_down(0, 0)
            for e in range(1, NWR):
                sp.wait_ge(r_spl, 2 * e)
                load_gate_up(e + 1, (e + 1) % 2)
                load_down(e, e)
            sp.wait_ge(r_tbl, 1)

            with sp.Fori(1, NE // NWR - 1) as rnd:
                for i in range(NWR):
                    e = rnd * NWR + i
                    sp.wait_ge(r_spl, e * 2)
                    load_gate_up(e + 1, (i + 1) % 2)
                    used = sp.value_load(last_slot[0:1, bass.ds(e - NWR, 1)], min_val=1, max_val=SLOTS + 1)
                    sp.wait_ge(r_dn, used)
                    load_down(e, i)

            for e in range(NE - NWR, NE):
                sp.wait_ge(r_spl, e * 2)
                if e + 1 < NE:
                    load_gate_up(e + 1, (e + 1) % 2)
                used = sp.value_load(last_slot[0:1, e - NWR:e - NWR + 1], min_val=1, max_val=SLOTS + 1)
                sp.wait_ge(r_dn, used)
                load_down(e, e % NWR)
            for t in range(NT):
                sp.wait_ge(r_acc, (t + 1) * TOPK)
                sp.dma_start(out.rearrange("b (c p) d -> (b c) p d", p=P)[t], x1[:, t, :]).then_inc(r_out, 16)
            sp.wait_ge(r_out, NT * 16)

        @block.gpsimd
        def _(pool):
            nc.gpsimd.memset(ident[:], 0.0).then_inc(s_id0, 1)
            pool.wait_ge(s_id0, 1)
            nc.gpsimd.affine_select(out=ident[:], in_=ident[:], compare_op=ALU.not_equal, fill=1.0, base=0,
                                    pattern=[[-1, P]], channel_multiplier=1).then_inc(s_id, 1)
            nc.gpsimd.memset(zeros[:], 0.0).then_inc(r_zero, 1)
            pool.sem_inc(s_hc, RING)
            for b in range(NB):
                t = rounding[b % 2]
                pool.wait_ge(s_wm, b + 1)
                nc.gpsimd.tensor_tensor(t[:], t[:], expneg[b], ALU.subtract).then_inc(s_t1, 1)
                pool.wait_ge(s_lw, b + 1)
                pool.wait_ge(s_t1, b + 1)
                nc.gpsimd.tensor_tensor(t[:], logw[:], t[:], ALU.subtract).then_inc(s_t2, 1)

            with pool.Fori(0, NB) as b:
                def times_c(j, q):
                    n = j * 2 + q
                    m = b * NS + n
                    pool.wait_ge(s_c[q], b * (NS * 8) + (n - q) * 8 + 16)
                    for et in range(ET - q):
                        k = m * ET + et
                        pool.wait_ge(s_h, k + 1 + RING)
                        pool.wait_ge(s_y, k + 1)
                        nc.gpsimd.tensor_tensor(hC[et], h[et], crow[q], ALU.mult).then_inc(s_hc, 1)

                with pool.Fori(0, NS // 2) as j:
                    for q in range(2):
                        times_c(j, q)
                for lc in range(LC):
                    pool.wait_ge(s_yz, b * LC + lc + 1 + 1)
                    t = b * LC + lc
                    nc.gpsimd.tensor_tensor(tile(x1, t), tile(x1, t), tile(zT, t), ALU.add).then_inc(s_x1, 1)

            pool.wait_ge(s_x1, NT)
            nc.gpsimd.memset(ones[:], 1.0).then_inc(r_cst0, 1)
            nc.gpsimd.memset(upper[:], 1.0).then_inc(r_cst0, 1)
            pool.wait_ge(r_cst0, 2)
            nc.gpsimd.affine_select(out=upper[:], in_=upper[:], compare_op=ALU.is_gt, fill=0.0, base=0,
                                    pattern=[[1, P]], channel_multiplier=-1).then_inc(r_cst2, 1)
            nc.gpsimd.iota(eidx[:], pattern=[[1, NE]], base=0, channel_multiplier=0,
                           allow_small_or_imprecise_dtypes=True).then_inc(r_cst2, 1)
            nc.gpsimd.iota(ebase[:], pattern=[[REGION, NE]], base=P, channel_multiplier=0,
                           allow_small_or_imprecise_dtypes=True).then_inc(r_cst2, 1)
            nc.gpsimd.iota(sidx[:], pattern=[[1, SLOTS]], base=0, channel_multiplier=0,
                           allow_small_or_imprecise_dtypes=True).then_inc(r_cst2, 1)

            def split(e, q, r):
                at = slice(r * WG, (r + 1) * WG)
                pool.wait_ge(r_raw[q], (e - q) * 8 + 16)
                pool.sem_inc(r_apart, 1)
                nc.gpsimd.tensor_copy(whi[:, at], raw[q][:]).then_inc(r_hi, 1)
                pool.wait_ge(r_hi, e + 1)
                nc.gpsimd.tensor_tensor(wlo[:, at], raw[q][:], whi[:, at].bitcast(F32), ALU.subtract).then_inc(r_spl, 1)
                pool.wait_ge(r_dnl, e * 16 + 16)
                pool.sem_inc(r_spl, 1)

            EARLY = 2
            for e in range(EARLY):
                split(e, e % 2, e)
            for b in range(NB):
                pool.wait_ge(r_si, b + 1)
                for t in range(LC):
                    for j in range(TOPK):
                        nc.gpsimd.indirect_dma_start(
                            out=xs_dram, out_offset=bass.IndirectOffsetOnAxis(ap=slot_i[:, b * LC + t, j:j + 1], axis=0),
                            in_=xn[b][:, t, :], in_offset=None).then_inc(r_sc[b], 16)
            for e in range(EARLY, NWR):
                split(e, e % 2, e)
            pool.wait_ge(r_tbl, 1)
            with pool.Fori(1, NE // NWR) as rnd:
                for i in range(NWR):
                    e = rnd * NWR + i
                    used = pool.value_load(last_slot[0:1, bass.ds(e - NWR, 1)], min_val=1, max_val=SLOTS + 1)
                    pool.wait_ge(r_dn, used)
                    split(e, i % 2, i)
            pool.wait_ge(r_yi, 1)
            for q in range(NX):
                pool.wait_ge(r_ys[q], SLOTS // NX * 16)
            for t in range(NT):
                for j in range(TOPK):
                    k = t * TOPK + j
                    if k >= NY:
                        pool.wait_ge(r_acc, k - NY + 1)
                    nc.gpsimd.indirect_dma_start(
                        out=ygat[:, k % NY, :], out_offset=None, in_=ys_dram,
                        in_offset=bass.IndirectOffsetOnAxis(ap=y_i[:, t, j:j + 1], axis=0)).then_inc(r_yg[k % NY], 16)

        @block.tensor
        def _(pe):
            pe.sem_inc(s_sku, 1)
            def turn(dst, src, start=True, stop=True):
                k = src.shape[0]
                return nc.tensor.matmul(dst, src, ident[0:k, 0:k], start=start, stop=stop, is_transpose=True)

            pe.wait_ge(s_id, 1)
            pe.wait_ge(s_w, NW * 16)
            for ct in range(CT):
                for et in range(ET):
                    last = turn(bank[ct][:, cols(et)], w_in_nat[:, et, cols(ct)])
                last.then_inc(s_wt, 1)
            for et in range(ET):
                last = turn(bank[2][:, cols(et, XR)], xproj_nat[:, cols(et)])
            last.then_inc(s_wt, 1)
            for et in range(ET):
                last = turn(bank[3][0:DR, cols(et)], dtw_nat[:, et, :])
            last.then_inc(s_wt, 1)
            pe.wait_ge(s_wtc, 4)

            def turn_ctx(b):
                pe.wait_ge(s_ctx, b * 16 + 16)
                if b:
                    pe.wait_ge(s_ctxe, b * CT)
                if b >= 2:
                    pe.wait_ge(s_xde, b * 2 - 2)
                for ct in range(CT):
                    for lc in range(LC):
                        last = turn(bank[ct][:, cols(lc)], ctxn[:, lc, cols(ct)])
                last.then_inc(s_ctxt, 1)

            def in_proj(b, ets):
                pe.wait_ge(s_ctxe, b * CT + CT)
                for et in ets:
                    if b:
                        pe.wait_ge(s_conv, (b - 1) * ET + et + 1)
                    for ct in range(CT):
                        last = nc.tensor.matmul(bank[2 + et][:], w_inT[:, ct, cols(et)], ctxT[:, ct, :],
                                                start=(ct == 0), stop=(ct == CT - 1))
                    last.then_inc(s_xin, 1)

            turn_ctx(0)
            in_proj(0, range(ET))
            turn_ctx(1)
            for b in range(NB):
                if b + 1 < NB:
                    in_proj(b + 1, range(ET // 2))
                pe.wait_ge(s_u, b * ET + ET)
                for et in range(ET):
                    last = nc.tensor.matmul(bank[0][0:XR, :], xprojT[:, et, :], u[b][:, et, :],
                                            start=(et == 0), stop=(et == ET - 1))
                last.then_inc(s_xd, 1)
                if b + 1 < NB:
                    in_proj(b + 1, range(ET // 2, ET))
                pe.wait_ge(s_xde, b * 2 + 1)
                for lc in range(LC):
                    last = turn(bank[1][:, cols(lc, XR)], xdbl[:, cols(lc)])
                last.then_inc(s_bt, 1)
                for et in range(ET):
                    if b * ET + et >= 2:
                        pe.wait_ge(s_rl, b * ET + et - 1)
                    nc.tensor.matmul(bank[6 + et % 2][:], dtwT[:, cols(et)], xdbl[0:DR, :],
                                     start=True, stop=True).then_inc(s_dp, 1)
                if b + 2 < NB:
                    turn_ctx(b + 2)

            pe.wait_ge(s_rl, NB * ET)
            pe.wait_ge(s_conv, NB * ET)
            for b in range(NB):
                if b:
                    pe.wait_ge(s_dute_a, b * (LC // 2))
                    pe.wait_ge(s_dute_d, b * (LC // 2))
                pe.wait_ge(s_du, b + 1)
                for lc in range(LC):
                    for et in range(ET):
                        last = turn(bank[4 + lc][:, cols(et)], u[b][:, et, cols(lc)])
                    last.then_inc(s_dut, 1)

            pe.wait_ge(s_xde, NB * 2)
            for b in range(NB):
                pe.wait_ge(s_zn, b * ET + ET)
                if b:
                    pe.wait_ge(s_zte_a, b * (LC // 2))
                    pe.wait_ge(s_zte_d, b * (LC // 2))
                for lc in range(LC):
                    for et in range(ET):
                        last = turn(bank[lc][:, cols(et)], silu_z[b % 2][:, et, cols(lc)])
                    last.then_inc(s_zt, 1)

            pe.sem_inc(s_dbu, 2 * RING)
            pe.sem_inc(s_y, RING)
            pe.wait_ge(s_zte_a, NB * (LC // 2))
            pe.wait_ge(s_zte_d, NB * (LC // 2))
            pe.wait_ge(s_dute_a, NB * (LC // 2))
            pe.wait_ge(s_dute_d, NB * (LC // 2))
            with pe.Fori(0, NB) as b:
                def to_channels(n, q, et):
                    m = b * NS + n
                    if et == 0:
                        pe.wait_ge(s_bua, m * (LC - 1) + LC - 1)
                        pe.wait_ge(s_bud, m + 1)
                    pe.wait_ge(s_h, m * ET + et + 1)
                    for lc in range(LC):
                        last = turn(bank[et][:, cols(lc)], dBuT[q][:, lc, cols(et)])
                    last.then_inc(s_dbu, 1)

                def add_to_y(j, q, et, stop=False):
                    if q and et == ET - 1:
                        pe.wait_ge(s_hcd, b * (NS // 2) + j + 2)
                    else:
                        pe.wait_ge(s_hc, (b * (NS // 2) + j) * PC + q * ET + et + 1 + RING)
                    for lc in range(LC):
                        last = turn(bank[4 + lc][:, cols(et)], hC[et][:, cols(lc)], start=False, stop=stop)
                    last.then_inc(s_y, 1)

                pe.wait_ge(s_skl, b * 16 + 16)
                pe.wait_ge(s_yz, b * LC + 1)
                for et in range(ET):
                    for lc in range(LC):
                        last = turn(bank[4 + lc][:, cols(et)], skip[:, et, cols(lc)], start=(et == 0), stop=False)
                last.then_inc(s_sku, 1)
                for et in range(ET):
                    to_channels(0, 0, et)
                with pe.Fori(0, NS // 2 - 1) as j:
                    for q in range(2):
                        for et in range(ET):
                            to_channels(j * 2 + q + 1, 1 - q, et)
                            add_to_y(j, q, et)
                for et in range(ET):
                    to_channels(NS - 1, 1, et)
                    add_to_y(NS // 2 - 1, 0, et)
                for et in range(ET):
                    add_to_y(NS // 2 - 1, 1, et, stop=(et == ET - 1))

            pe.wait_ge(s_x1, NT)
            pe.wait_ge(r_gl, 32)
            pe.wait_ge(r_cst2, 4)

            def turn_normed(b):
                for t in range(LC):
                    pe.wait_ge(r_xn2, b * LC + t + 1)
                    if b:
                        pe.wait_ge(r_xnte, b * LC)
                    for d in range(DM // P):
                        last = turn(bank[t][:, cols(d)], xn[b][:, t, cols(d)])
                    last.then_inc(r_xnt, 1)

            turn_normed(0)
            for b in range(NB):
                pe.wait_ge(r_xnte, (b + 1) * LC)
                if b:
                    pe.wait_ge(r_lgc, b)
                for t in range(LC):
                    for d in range(DM // P):
                        last = nc.tensor.matmul(bank[4][:, cols(t, NE)], xnT[:, t, cols(d)], gate_sb[:, d, :],
                                                start=(d == 0), stop=(d == DM // P - 1))
                last.then_inc(r_lg, 1)
                if b + 1 < NB:
                    turn_normed(b + 1)
                pe.wait_ge(r_ch, b + 1)
                if b:
                    pe.wait_ge(r_cum, b)
                nc.tensor.matmul(bank[5][:, 0:LC * NE], upper[:], chosen[:].rearrange("p t e -> p (t e)"),
                                 start=True, stop=False)
                for t in range(LC - 1):
                    later = LC - 1 - t
                    nc.tensor.matmul(bank[5][:, (t + 1) * NE:LC * NE], ones[:],
                                     chosen[:, t:t + 1, :].broadcast_to([P, later, NE]), start=False, stop=(t == LC - 2))
                for t in range(LC):
                    last = nc.tensor.matmul(bank[5][:, LC * NE:(LC + 1) * NE], ones[:], chosen[:, t, :],
                                            start=(t == 0), stop=(t == LC - 1))
                last.then_inc(r_pos, 1)

            KD = DM // P

            def turn_x(s, q):
                pe.wait_ge(r_xl[q], (s - q) * (16 // NX) + 16)
                pe.wait_ge(r_xlo, s + 1)
                for d in range(KD):
                    last = turn(bank[q % 2][:, cols(d)], xrow[q][:, cols(d)])
                last.then_inc(r_mmx, 1)

            def three(dst, lh, ll, rh, rl, start, stop):
                nc.tensor.matmul(dst, lh, rh, start=start, stop=False)
                nc.tensor.matmul(dst, lh, rl, start=False, stop=False)
                return nc.tensor.matmul(dst, ll, rh, start=False, stop=stop)

            def look_up(s):
                return pe.value_load(tab[0:1, bass.ds(s, 1)], min_val=2, max_val=2 * NE)

            def column(need, width):
                return (((need >> 1) - 1) & (NWR - 1)) * width

            def up(s, q, need):
                pe.wait_ge(r_spl, need)
                pe.wait_ge(r_xlo, s + 1 + 2)
                pe.wait_ge(r_gd, s + 1)
                for d in range(KD):
                    at = column(need, WG) + d * 2 * FI
                    last = three(bank[2 + q % 2][:, 0:2 * FI], xhi[q % 2][:, cols(d)], xlo[q % 2][:, cols(d)],
                                 whi[:, bass.ds(at, 2 * FI)], wlo[:, bass.ds(at, 2 * FI)], d == 0, d == KD - 1)
                last.then_inc(r_gu, 1)

            def turn_g(s, q):
                pe.wait_ge(r_gd, s + 1 + 2)
                pe.wait_ge(r_gh, s + 1)
                for i in range(2):
                    last = turn(bank[4 + q % 2][0:HK, cols(i)], gated[q % 2][:, cols(i, HK)])
                last.then_inc(r_gt, 1)

            def dn(s, q, need):
                pe.wait_ge(r_gh, s + 1 + 2)
                pe.wait_ge(r_ye, s + 1 + UNR - 2)
                for i in range(2):
                    last = nc.tensor.matmul(bank[6 + q % 2][:], gT[q % 2][0:HK, cols(i)],
                                            wdn[0:HK, bass.ds(column(need, WD) + i * DM, DM)], start=(i == 0), stop=(i == 1))
                last.then_inc(r_dn, 1)

            pe.wait_ge(r_tbl, 1)
            pe.wait_ge(r_cum, NB)
            pe.sem_inc(r_dn, 1)
            pe.sem_inc(r_gu, 2)
            def turn_of_slot(s, i, last=False):
                dn(s - 1, (i - 1) % UNR, look_up(s - 1))
                need = None if last else look_up(s + 1)
                turn_g(s, i)
                if not isinstance(s, int) or s + 2 < SLOTS:
                    turn_x(s + 2, (i + 2) % UNR)
                if not last:
                    up(s + 1, (i + 1) % UNR, need)

            turn_x(0, 0)
            turn_x(1, 1)
            up(0, 0, look_up(0))
            turn_g(0, 0)
            turn_x(2, 2)
            up(1, 1, look_up(1))
            with pe.Fori(0, SLOTS // UNR - 1) as rnd:
                for i in range(UNR):
                    turn_of_slot(rnd * UNR + i + 1, (i + 1) % UNR)
            for s in range(SLOTS - UNR + 1, SLOTS):
                turn_of_slot(s, s % UNR, s == SLOTS - 1)
            dn(SLOTS - 1, (SLOTS - 1) % UNR, look_up(SLOTS - 1))

        @block.scalar
        def _(act):
            def wait_apart(s, value):
                act.wait_ge(s, value)
                act.sem_inc(s_apart, 1)

            act.wait_ge(s_w, NW * 16)
            nc.scalar.activation(tgx[:], gx[:], ACT.Tanh).then_inc(s_tg, 1)
            nc.scalar.activation(Aexp[:], Alog[:], ACT.Exp).then_inc(s_A, 1)

            def copy_ctx(b):
                act.wait_ge(s_ctxt, b + 1)
                if b:
                    act.wait_ge(s_xin, b * ET)
                for ct in range(CT):
                    nc.scalar.copy(ctxT[:, ct, :], bank[ct][:]).then_inc(s_ctxe, 1)

            def last_tap(b):
                for et in range(ET):
                    act.wait_ge(s_xin, b * ET + et + 1)
                    if b:
                        act.wait_ge(s_u, (b - 1) * ET + et + 1)
                    nc.scalar.activation(conv[:, et, :], bank[2 + et][:], ACT.Identity, bias=cb[:, et:et + 1],
                                         scale=cw[:, et, TAPS - 1:TAPS]).then_inc(s_tap, 1)

            copy_ctx(0)
            last_tap(0)
            copy_ctx(1)
            for b in range(NB + 1):
                if b < NB:
                    for et in range(ET):
                        act.wait_ge(s_conv, b * ET + et + 1)
                        nc.scalar.activation(u[b][:, et, :], conv[:, et, :], ACT.Silu).then_inc(s_u, 1)
                if b + 1 < NB:
                    last_tap(b + 1)
                if b >= 1:
                    act.wait_ge(s_abs, b * ET)
                    nc.scalar.activation(expneg[b - 1], expneg[b - 1], ACT.Exp, scale=-1.0).then_inc(s_ez, 1)
                    act.wait_ge(s_ez, b)
                    if b >= 2:
                        act.wait_ge(s_t2, b - 1)
                    nc.scalar.activation(logw[:], expneg[b - 1], ACT.Ln, bias=1.0).then_inc(s_lw, 1)
                if b < NB:
                    for et in range(ET):
                        act.wait_ge(s_dp, b * ET + et + 1)
                        nc.scalar.activation(expneg[b][:, et, :], bank[6 + et % 2][:], ACT.Abs, bias=dtb[:, et:et + 1]).then_inc(s_abs, 1)
                        nc.scalar.activation(delta[:, b, et, :], bank[6 + et % 2][:], ACT.Relu, bias=dtb[:, et:et + 1]).then_inc(s_rl, 1)
                if b + 2 < NB:
                    copy_ctx(b + 2)

            act.wait_ge(s_mv, NT)
            act.wait_ge(s_eps, 1)
            nc.scalar.activation(std[:], mv[:, :, 1], ACT.Sqrt, bias=eps[:]).then_inc(s_sd, 1)
            act.wait_ge(s_nm, 1)

            def silu_of_norm(b):
                if b >= 2:
                    act.wait_ge(s_zt, (b - 1) * LC)
                for et in range(ET):
                    t = b * ET + et
                    nc.scalar.activation(silu_z[b % 2][:, et, :], x1[:, t, :], ACT.Silu, bias=nmr[:, t:t + 1],
                                         scale=rstd[:, t:t + 1]).then_inc(s_zn, 1)

            silu_of_norm(0)
            act.wait_ge(s_dl, NB - 1)
            silu_of_norm(1)
            for b in range(NB):
                for lc in range(LC // 2):
                    act.wait_ge(s_dut, b * LC + lc + 1)
                    nc.scalar.copy(duT[:, b * LC + lc, :], bank[4 + lc][:]).then_inc(s_dute_a, 1)
            for b in range(NB):
                for lc in range(LC // 2):
                    act.wait_ge(s_zt, b * LC + lc + 1)
                    nc.scalar.mul(zT[:, b * LC + lc, :], bank[lc][:], tgx[:]).then_inc(s_zte_a, 1)
                if b + 2 < NB:
                    silu_of_norm(b + 2)

            act.wait_ge(s_dl, NB)
            act.wait_ge(s_zt, NB * LC)
            act.wait_ge(s_dute_a, NB * (LC // 2))
            act.wait_ge(s_dute_d, NB * (LC // 2))
            act.wait_ge(s_An, 1)
            act.wait_ge(s_sks, NB * 16)
            with act.Fori(0, NB) as b:
                def scale_b(n, q):
                    m = b * NS + n
                    wait_apart(s_dbu, m * ET + RING)
                    for lc in range(LC - 1):
                        nc.scalar.mul(dBuT[q][:, lc, :], tile(duT, b * LC + lc),
                                      BT[:, bass.ds(b, 1), bass.ds(n + lc * NS, 1)].rearrange("p o n -> p (o n)")).then_inc(s_bua, 1)

                def decay(n, q):
                    for et in range(ET):
                        k = (b * NS + n) * ET + et
                        wait_apart(s_h, k + 1)
                        nc.scalar.activation(dA[et], delta[:, bass.ds(b, 1), et, :].rearrange("p o n -> p (o n)"),
                                             ACT.Exp, scale=Aneg[:, et, bass.ds(n, 1)]).then_inc(s_dA, 1)

                act.wait_ge(s_sku, b + 1)
                act.dma_start(skip[:].rearrange("p t n -> p (t n)"),
                              skip_dram[bass.ds(b, 1)].rearrange("o p n -> (o p) n")).then_inc(s_skl, 16)
                scale_b(0, 0)
                with act.Fori(0, NS - 2, 2) as n:
                    for q in range(2):
                        scale_b(n + q + 1, 1 - q)
                        decay(n + q, q)
                scale_b(NS - 1, 1)
                decay(NS - 2, 0)
                decay(NS - 1, 1)

            act.wait_ge(r_gl, 16)
            nc.scalar.activation(tgf[:], gf[:], ACT.Tanh).then_inc(r_ex, 1)
            act.wait_ge(r_mv2, NT)
            nc.scalar.activation(std[:], mv[:, :, 1], ACT.Sqrt, bias=eps[:]).then_inc(r_sd2, 1)
            for b in range(NB):
                for t in range(LC // 2):
                    act.wait_ge(r_xnt, b * LC + t + 1)
                    if b:
                        act.wait_ge(r_lg, b)
                    nc.scalar.copy(xnT[:, t, :], bank[t][:]).then_inc(r_xnte, 1)
                act.wait_ge(r_sub, b + 1)
                nc.scalar.activation(ex[:], ex[:], ACT.Exp).then_inc(r_ex, 1)

            def x_hi(s, q):
                act.wait_ge(r_mmx, s + 1)
                act.wait_ge(r_gu, s + 1)
                nc.scalar.copy(xhi[q % 2][:], bank[q % 2][:]).then_inc(r_xh, 1)

            def load_x(s, q):
                row = act.value_load(tab[0:1, bass.ds(s + SLOTS, 1)], min_val=0, max_val=DUMMY)
                act.dma_start(xrow[q], xs_dram[bass.ds(row, P), :]).then_inc(r_xl[q], 16)

            def store_y(s, q):
                act.wait_ge(r_ye, s + 1 + UNR)
                act.dma_start(ys_dram[bass.ds(s * P, P), :], yrow[q]).then_inc(r_ys[q], 16)

            act.wait_ge(r_cum, NB)
            act.sem_inc(r_gh, 2)
            nc.scalar.preload_act_table(ACT.Silu)
            act.wait_ge(r_zst, (NE + 1) * 16)
            act.wait_ge(r_tbl, 1)
            for b in range(NB):
                act.wait_ge(r_sc[b], LC * TOPK * 16)
            for s in range(NX):
                load_x(s, s)
            x_hi(0, 0)
            load_x(NX, 0)

            def slot(s, q, first=False, more=True, loads=True):
                if more:
                    x_hi(s + 1, (q + 1) % UNR)
                if loads:
                    load_x(s + 1 + NX, (q + 1) % NX)
                act.wait_ge(r_gu, s + 1 + 2)
                act.wait_ge(r_gd, s + 1)
                nc.scalar.activation(sg[q % 2][:], bank[2 + q % 2][:, 0:FI], ACT.Silu).then_inc(r_sg, 1)
                act.wait_ge(r_gt, s + 1)
                act.wait_ge(r_dn, s + 1)
                nc.scalar.copy(gT[q % 2][0:HK, :], bank[4 + q % 2][0:HK, 0:2 * P]).then_inc(r_gh, 1)
                if not first:
                    store_y(s - 2, (q - 2) % UNR)

            for s in range(UNR):
                slot(s, s, first=s < 2)
            with act.Fori(1, SLOTS // UNR - 2) as rnd:
                for q in range(UNR):
                    slot(rnd * UNR + q, q)
            for s in range(SLOTS - 2 * UNR, SLOTS):
                slot(s, s % UNR, more=s < SLOTS - 1, loads=s + 1 + NX < SLOTS)
            for s in range(SLOTS - 2, SLOTS):
                store_y(s, s % UNR)

        @block.vector
        def _(dve):
            dve.sem_inc(s_yz, 1)
            nc.vector.memset(eps[:], LN_EPS).then_inc(s_eps, 1)
            dve.wait_ge(s_A, 1)
            nc.vector.tensor_scalar_mul(Aneg[:], Aexp[:], -1.0).then_inc(s_An, 1)
            for ct in range(CT):
                dve.wait_ge(s_wt, ct + 1)
                nc.vector.tensor_copy(w_inT[:, ct, :], bank[ct][:]).then_inc(s_wtc, 1)
            dve.wait_ge(s_wt, CT + 1)
            nc.vector.tensor_copy(xprojT[:].rearrange("p t n -> p (t n)"), bank[2][:, 0:ET * XR]).then_inc(s_wtc, 1)
            dve.wait_ge(s_wt, CT + 2)
            nc.vector.tensor_copy(dtwT[:], bank[3][0:DR, :]).then_inc(s_wtc, 1)

            def earlier_taps(b):
                for j, k in enumerate(range(TAPS - 2, -1, -1)):
                    s = TAPS - 1 - k
                    for et in range(ET):
                        if j == 0:
                            dve.wait_ge(s_tap, b * ET + et + 1)
                        else:
                            dve.wait_ge(s_cv, b * (ET * (TAPS - 2)) + (j - 1) * ET + et + 1)
                        nc.vector.scalar_tensor_tensor(
                            out=conv[:, et, s:], in0=bank[2 + et][:, 0:L - s], scalar=cw[:, et, k:k + 1],
                            in1=conv[:, et, s:], op0=ALU.mult, op1=ALU.add,
                        ).then_inc(s_conv if k == 0 else s_cv, 1)

            def skip_and_rows(b):
                if b:
                    dve.wait_ge(s_sks, b * 16)
                for et in range(ET):
                    dve.wait_ge(s_u, b * ET + et + 1)
                    nc.vector.tensor_scalar_mul(skip[:, et, :], u[b][:, et, :], Dp[:, et:et + 1]).then_inc(s_skc, 1)
                dve.wait_ge(s_xd, b + 1)
                if b:
                    dve.wait_ge(s_dp, b * ET)
                    dve.wait_ge(s_cst, b * 16)
                nc.vector.tensor_copy(xdbl[:], bank[0][0:XR, :]).then_inc(s_xde, 1)
                dve.wait_ge(s_bt, b + 1)
                nc.vector.tensor_copy(BT[:, b, :].rearrange("p (c n) -> p c n", n=NS),
                                      bank[1][:, 0:LC * XR].rearrange("p (c r) -> p c r", r=XR)[:, :, DR:DR + NS]).then_inc(s_xde, 1)

            def rounded(b):
                dve.wait_ge(s_ez, b + 1)
                nc.vector.tensor_scalar(rounding[b % 2][:], expneg[b], 1.0, 1.0, ALU.add, ALU.subtract).then_inc(s_wm, 1)

            def delta_and_du(b):
                dve.wait_ge(s_t2, b + 1)
                dve.wait_ge(s_rl, b * ET + ET)
                nc.vector.tensor_tensor(delta[:, b], delta[:, b], rounding[b % 2][:], ALU.add).then_inc(s_dl, 1)
                dve.wait_ge(s_dl, b + 1)
                nc.vector.tensor_tensor(u[b], delta[:, b], u[b], ALU.mult).then_inc(s_du, 1)

            earlier_taps(0)
            skip_and_rows(0)
            for b in range(1, NB + 1):
                if b < NB:
                    earlier_taps(b)
                if b >= 2:
                    rounded(b - 2)
                if b >= 3:
                    delta_and_du(b - 3)
                if b < NB:
                    skip_and_rows(b)
            dve.wait_ge(s_x, NB * 16)
            for t in range(NT):
                nc.vector.bn_stats(stats[:, t, :], x1[:, t, :]).then_inc(s_st, 1)
            for t in range(NT):
                dve.wait_ge(s_st, t + 1)
                nc.vector.bn_aggr(mv[:, t, :], stats[:, t, :]).then_inc(s_mv, 1)
            rounded(NB - 1)
            delta_and_du(NB - 2)
            dve.wait_ge(s_sd, 1)
            nc.vector.reciprocal(rstd[:], std[:]).then_inc(s_rs, 1)
            dve.wait_ge(s_rs, 1)
            nc.vector.scalar_tensor_tensor(out=nmr[:], in0=mv[:, :, 0], scalar=-1.0, in1=rstd[:],
                                           op0=ALU.mult, op1=ALU.mult).then_inc(s_nm, 1)
            delta_and_du(NB - 1)
            for b in range(NB):
                for lc in range(LC // 2, LC):
                    dve.wait_ge(s_dut, b * LC + lc + 1)
                    nc.vector.tensor_copy(duT[:, b * LC + lc, :], bank[4 + lc][:]).then_inc(s_dute_d, 1)
            dve.wait_ge(s_tg, 1)
            for b in range(NB):
                for lc in range(LC // 2, LC):
                    dve.wait_ge(s_zt, b * LC + lc + 1)
                    nc.vector.tensor_scalar_mul(zT[:, b * LC + lc, :], bank[lc][:], tgx[:]).then_inc(s_zte_d, 1)

            dve.sem_inc(s_h, RING)
            dve.sem_inc(s_hcd, 1)
            dve.wait_ge(s_dute_a, NB * (LC // 2))
            dve.wait_ge(s_dute_d, NB * (LC // 2))
            with dve.Fori(0, NB) as b:
                def scale_b(n, q):
                    dve.wait_ge(s_dbu, (b * NS + n) * ET + RING)
                    nc.vector.tensor_scalar_mul(
                        dBuT[q][:, LC - 1, :], tile(duT, b * LC + LC - 1),
                        BT[:, bass.ds(b, 1), bass.ds(n + (LC - 1) * NS, 1)].rearrange("p o n -> p (o n)")).then_inc(s_bud, 1)

                def scans(j, q):
                    n = j * 2 + q
                    pair = b * (NS // 2) + j
                    for et in range(ET):
                        k = (b * NS + n) * ET + et
                        dve.wait_ge(s_dbu, k + 1 + 2 * RING)
                        dve.wait_ge(s_dA, k + 1)
                        if q:
                            dve.wait_ge(s_hc, pair * PC + et + 1 + RING)
                        elif et < ET - 1:
                            dve.wait_ge(s_hc, pair * PC - PC + ET + et + 1 + RING)
                        else:
                            dve.wait_ge(s_hcd, pair + 1)
                        nc.vector.tensor_tensor_scan(out=h[et], data0=dA[et], data1=bank[et][:], initial=0.0,
                                                     op0=ALU.mult, op1=ALU.add).then_inc(s_h, 1)
                    if q:
                        dve.wait_ge(s_c[q], pair * 16 + 16)
                        dve.wait_ge(s_h, k + 1 + RING)
                        dve.wait_ge(s_y, k + 1)
                        nc.vector.tensor_tensor(hC[et], h[et], crow[q], ALU.mult).then_inc(s_hcd, 1)

                scale_b(0, 0)
                with dve.Fori(0, NS // 2 - 1) as j:
                    for q in range(2):
                        scale_b(j * 2 + q + 1, 1 - q)
                        scans(j, q)
                scale_b(NS - 1, 1)
                scans(NS // 2 - 1, 0)
                scans(NS // 2 - 1, 1)
                dve.wait_ge(s_y, (b + 1) * (NS * ET) + RING)
                for lc in range(LC):
                    t = b * LC + lc
                    nc.vector.tensor_tensor(tile(zT, t), bank[4 + lc][:], tile(zT, t), ALU.mult).then_inc(s_yz, 1)

            for t in range(NT):
                if t % LC == 0:
                    dve.wait_ge(s_x1, t + LC)
                nc.vector.bn_stats(stats[:, t, :], x1[:, t, :]).then_inc(r_st2, 1)
            for t in range(NT):
                dve.wait_ge(r_st2, t + 1)
                nc.vector.bn_aggr(mv[:, t, :], stats[:, t, :]).then_inc(r_mv2, 1)
            nc.vector.memset(cum[:], 0.0).then_inc(r_cumb, 1)
            dve.wait_ge(r_sd2, 1)
            nc.vector.reciprocal(rstd[:], std[:]).then_inc(r_rs2, 1)
            dve.wait_ge(r_rs2, 1)
            nc.vector.scalar_tensor_tensor(out=nmr[:], in0=mv[:, :, 0], scalar=-1.0, in1=rstd[:],
                                           op0=ALU.mult, op1=ALU.mult).then_inc(r_nm2, 1)
            dve.wait_ge(r_nm2, 1)
            dve.wait_ge(r_cumb, 1)
            dve.wait_ge(r_cst2, 4)

            def normed(b):
                for t in range(LC):
                    m = b * LC + t
                    nc.vector.tensor_scalar(xn[b][:, t, :], x1[:, m, :], rstd[:, m:m + 1], nmr[:, m:m + 1],
                                            ALU.mult, ALU.add).then_inc(r_xn2, 1)

            def copy_normed(b):
                for t in range(LC // 2, LC):
                    dve.wait_ge(r_xnt, b * LC + t + 1)
                    if b:
                        dve.wait_ge(r_lg, b)
                    nc.vector.tensor_copy(xnT[:, t, :], bank[t][:]).then_inc(r_xnte, 1)

            normed(0)
            copy_normed(0)
            for b in range(NB):
                if b + 1 < NB:
                    normed(b + 1)
                dve.wait_ge(r_lg, b + 1)
                nc.vector.tensor_copy(logit[:].rearrange("p t e -> p (t e)"), bank[4][:, 0:LC * NE]).then_inc(r_lgc, 1)
                dve.wait_ge(r_lgc, b + 1)
                for t in range(LC):
                    nc.vector.max(out=top[:, t, :], in_=logit[:, t, :]).then_inc(r_mx, 1)
                for t in range(LC):
                    dve.wait_ge(r_mx, b * LC + t + 1)
                    nc.vector.max_index(out=topi[:, t, :], in_max=top[:, t, :], in_values=logit[:, t, :]).then_inc(r_mi, 1)
                nc.vector.tensor_tensor(ex[:], top[:, :, 0:TOPK], top[:, :, 0:1].broadcast_to([P, LC, TOPK]),
                                        ALU.subtract).then_inc(r_sub, 1)
                dve.wait_ge(r_mi, (b + 1) * LC)
                mine = topf[:, b * LC * TOPK:(b + 1) * LC * TOPK]
                nc.vector.tensor_copy(mine.rearrange("p (t j) -> p t j", j=TOPK), topi[:, :, 0:TOPK]).then_inc(r_tf, 1)
                dve.wait_ge(r_tf, b + 1)
                nc.vector.tensor_tensor(onehot[:], eidx[:].unsqueeze(1).broadcast_to([P, LC * TOPK, NE]),
                                        mine.unsqueeze(2).broadcast_to([P, LC * TOPK, NE]), ALU.is_equal).then_inc(r_oh, 1)
                dve.wait_ge(r_oh, b + 1)
                with nc.allow_low_precision(reason="zeros and ones"):
                    nc.vector.tensor_reduce(chosen[:], onehot[:].rearrange("p (t j) e -> p t e j", j=TOPK), AX.X,
                                            ALU.add).then_inc(r_ch, 1)
                dve.wait_ge(r_ex, b + 2)
                nc.vector.tensor_reduce(exs[:], ex[:], AX.X, ALU.add).then_inc(r_exsum, 1)
                dve.wait_ge(r_exsum, b + 1)
                nc.vector.reciprocal(exs[:], exs[:]).then_inc(r_exr, 1)
                dve.wait_ge(r_exr, b + 1)
                nc.vector.scalar_tensor_tensor(out=weight[:, b * LC:(b + 1) * LC, :], in0=ex[:], scalar=tgf[:],
                                               in1=exs[:].unsqueeze(2).broadcast_to([P, LC, TOPK]),
                                               op0=ALU.mult, op1=ALU.mult).then_inc(r_w, 1)
                nc.vector.tensor_tensor(cumb[:], cum[:], ebase[:], ALU.add).then_inc(r_cumb, 1)
                if b + 1 < NB:
                    copy_normed(b + 1)
                dve.wait_ge(r_cumb, b + 2)
                dve.wait_ge(r_pos, b + 1)
                nc.vector.tensor_tensor(picked[:, 0:LC, :], bank[5][:, 0:LC * NE].rearrange("p (t e) -> p t e", e=NE),
                                        cumb[:].unsqueeze(1).broadcast_to([P, LC, NE]), ALU.add).then_inc(r_posb, 1)
                nc.vector.tensor_tensor(cum[:], cum[:], bank[5][:, LC * NE:(LC + 1) * NE], ALU.add).then_inc(r_cum, 1)
                dve.wait_ge(r_posb, b + 1)
                nc.vector.tensor_tensor(onehot[:].rearrange("p (t j) e -> p t j e", j=TOPK),
                                        onehot[:].rearrange("p (t j) e -> p t j e", j=TOPK),
                                        picked[:, 0:LC, :].unsqueeze(2).broadcast_to([P, LC, TOPK, NE]), ALU.mult).then_inc(r_pk, 1)
                dve.wait_ge(r_pk, b + 1)
                nc.vector.tensor_reduce(slot_f[:, b * LC:(b + 1) * LC, :].rearrange("p t j -> p (t j)"), onehot[:], AX.X,
                                        ALU.add).then_inc(r_sf, 1)
                dve.wait_ge(r_sf, b + 1)
                nc.vector.tensor_copy(slot_i[:, b * LC:(b + 1) * LC, :], slot_f[:, b * LC:(b + 1) * LC, :]).then_inc(r_si, 1)
                dve.wait_ge(r_cum, b + 1)

            steps = [0]

            def step(ins):
                steps[0] += 1
                ins.then_inc(r_tb, 1)
                dve.wait_ge(r_tb, steps[0])

            step(nc.vector.tensor_scalar(nti[:], cum[:], float(P - 1), None, ALU.add))
            step(nc.vector.tensor_scalar(nti[:], nti[:], P.bit_length() - 1, None, ALU.arith_shift_right))
            step(nc.vector.tensor_copy(ntf[:], nti[:]))
            step(nc.vector.memset(ntone[:], 1.0))
            step(nc.vector.tensor_tensor_scan(out=ntcum[:], data0=ntone[:], data1=ntf[:], initial=0.0,
                                              op0=ALU.mult, op1=ALU.add))
            step(nc.vector.tensor_scalar(last_slot[:], ntcum[0:1, :], 1.0, None, ALU.add))
            step(nc.vector.tensor_tensor(shift[:], cum[:], ebase[:], ALU.add))
            step(nc.vector.scalar_tensor_tensor(out=shift[:], in0=ntcum[:], scalar=float(-P), in1=shift[:],
                                                op0=ALU.mult, op1=ALU.add))
            over = [1, SLOTS, NE]
            dve.wait_ge(r_sc[0], LC * TOPK * 16)
            step(nc.vector.tensor_tensor(compare, sidx[:].unsqueeze(2).broadcast_to(over),
                                         ntcum[0:1, :].unsqueeze(1).broadcast_to(over), ALU.is_ge))
            step(nc.vector.tensor_reduce(slot_e[:], compare, AX.X, ALU.add))
            step(nc.vector.tensor_tensor(compare, slot_e[:].unsqueeze(2).broadcast_to(over),
                                         eidx[0:1, :].unsqueeze(1).broadcast_to(over), ALU.is_equal))
            step(nc.vector.tensor_tensor(compare, compare, shift[0:1, :].unsqueeze(1).broadcast_to(over), ALU.mult))
            step(nc.vector.tensor_reduce(srow[:], compare, AX.X, ALU.add))
            step(nc.vector.scalar_tensor_tensor(out=srow[:], in0=sidx[:], scalar=float(P), in1=srow[:],
                                                op0=ALU.mult, op1=ALU.add))
            step(nc.vector.tensor_scalar(svalid[:], slot_e[:], float(NE), None, ALU.is_lt))
            step(nc.vector.scalar_tensor_tensor(out=stmp[:], in0=srow[:], scalar=float(-DUMMY), in1=svalid[:],
                                                op0=ALU.add, op1=ALU.mult))
            step(nc.vector.tensor_scalar(tab[:, SLOTS:2 * SLOTS], stmp[:], float(DUMMY), None, ALU.add))
            step(nc.vector.tensor_scalar(slot_e[:], slot_e[:], float(NE - 1), None, ALU.min))
            step(nc.vector.tensor_scalar(tab[:, 0:SLOTS], slot_e[:], 2.0, 2.0, ALU.mult, ALU.add))
            dve.sem_inc(r_tbl, 1)
            over = [P, NT * TOPK, NE]
            match = ygat[:, :, :].rearrange("p a b -> p (a b)")[:, 0:NT * TOPK * NE].rearrange("p (s e) -> p s e", e=NE)
            step(nc.vector.tensor_tensor(match, topf[:].unsqueeze(2).broadcast_to(over),
                                         eidx[:].unsqueeze(1).broadcast_to(over), ALU.is_equal))
            step(nc.vector.tensor_tensor(match, match, shift[:].unsqueeze(1).broadcast_to(over), ALU.mult))
            mine = picked[:].rearrange("p a b -> p (a b)")[:, 0:NT * TOPK]
            step(nc.vector.tensor_reduce(mine, match, AX.X, ALU.add))
            nc.vector.tensor_tensor(y_i[:].rearrange("p t j -> p (t j)"), slot_f[:].rearrange("p t j -> p (t j)"),
                                    mine, ALU.subtract).then_inc(r_yi, 1)

            def x_lo(s, q):
                dve.wait_ge(r_xh, s + 1)
                dve.wait_ge(r_gu, s + 1)
                nc.vector.tensor_tensor(xlo[q % 2][:], bank[q % 2][:], xhi[q % 2][:].bitcast(F32), ALU.subtract).then_inc(r_xlo, 1)

            def y_out(s, q):
                dve.wait_ge(r_dn, s + 1 + 1)
                if not isinstance(s, int) or s >= NX:
                    dve.wait_ge(r_ys[q], (s - q) * (16 // NX))
                nc.vector.tensor_copy(yrow[q], bank[6 + q % 2][:]).then_inc(r_ye, 1)

            def slot(s, q, first, more):
                if more:
                    x_lo(s + 1, (q + 1) % UNR)
                dve.wait_ge(r_sg, s + 1)
                if not first:
                    dve.wait_ge(r_gt, s)
                nc.vector.tensor_tensor(gated[q % 2][:], bank[2 + q % 2][:, FI:2 * FI], sg[q % 2][:], ALU.mult).then_inc(r_gd, 1)
                if not first:
                    y_out(s - 1, (q - 1) % UNR)

            dve.sem_inc(r_xlo, 2)
            dve.sem_inc(r_gd, 2)
            dve.sem_inc(r_ye, UNR)
            x_lo(0, 0)
            for s in range(UNR + 1):
                slot(s, s % UNR, s == 0, True)
            with dve.Fori(1, SLOTS // UNR - 1) as rnd:
                for i in range(UNR):
                    slot(rnd * UNR + i + 1, (i + 1) % UNR, False, True)
            for s in range(SLOTS - UNR + 1, SLOTS):
                slot(s, s % UNR, False, s + 1 < SLOTS)
            y_out(SLOTS - 1, (SLOTS - 1) % UNR)
            for t in range(NT):
                for j in range(TOPK):
                    k = t * TOPK + j
                    dve.wait_ge(r_yg[k % NY], (k // NY + 1) * 16)
                    if k:
                        dve.wait_ge(r_acc, k)
                    nc.vector.scalar_tensor_tensor(out=x1[:, t, :], in0=ygat[:, k % NY, :], scalar=weight[:, t, j:j + 1],
                                                   in1=x1[:, t, :], op0=ALU.mult, op1=ALU.add).then_inc(r_acc, 1)


_INS = ['x', 'ctx_1024', 'g_xattn', 'g_ffn', 'L0_xattn_in_proj_w', 'L0_xattn_conv_w', 'L0_xattn_conv_b',
        'L0_xattn_x_proj_w', 'L0_xattn_dt_proj_w', 'L0_xattn_dt_proj_b', 'L0_xattn_A_log', 'L0_xattn_D',
        'L0_ffn_gate', 'L0_ffn_gate_up_proj', 'L0_ffn_down_proj']


def kernel(**inputs):
    import numpy as _np
    import concourse.bacc as _bacc
    from concourse import mybir as _mybir
    from concourse.bass_utils import run_bass_kernel_spmd as _run

    nc = _bacc.Bacc("TRN2", target_bir_lowering=False, num_devices=1)
    arrays, args = {}, []
    for name in _INS:
        a = _np.ascontiguousarray(inputs[name])
        arrays[f"in_{name}_dram"] = a
        args.append(nc.dram_tensor(f"in_{name}_dram", a.shape, _mybir.dt.from_np(a.dtype), kind="ExternalInput").ap())
    args.append(nc.dram_tensor("out_dram", inputs['x'].shape, _mybir.dt.float32, kind="ExternalOutput").ap())
    flamingo_kernel(nc, *args)
    r = _run(nc, [arrays], core_ids=[0])
    return r.results[0]["out_dram"]
```

```python
from contextlib import ExitStack

import concourse.bass as bass
from concourse import mybir

P = 128
F32 = mybir.dt.float32
F32R = mybir.dt.float32r
BF16 = mybir.dt.bfloat16
I32 = mybir.dt.int32
U32 = mybir.dt.uint32
ALU = mybir.AluOpType
ACT = mybir.ActivationFunctionType
AX = mybir.AxisListType
LN_EPS = 1e-5


def flamingo_kernel(nc, x, ctx_in, g_xattn, g_ffn, in_proj_w, conv_w, conv_b, x_proj_w,
                    dt_proj_w, dt_proj_b, A_log, D, gate, gate_up, down, out):
    NB, L, DM = x.shape
    DC = ctx_in.shape[2]
    DI = in_proj_w.shape[0]
    TAPS = conv_w.shape[1]
    DR = dt_proj_w.shape[1]
    NS = A_log.shape[1]
    assert DI == L == DM
    ET, LC, CT = DI // P, L // P, DC // P
    NT = NB * LC
    XR = DR + 2 * NS
    PC = 2 * ET - 1
    RING = ET

    NE = gate.shape[1]
    TOPK = 4
    FI = gate_up.shape[2] // 2
    TOK = NB * L
    UNR = 4
    SLOTS = -(-(TOK * TOPK // P + NE - 1) // UNR) * UNR
    REGION = P + TOK
    DUMMY = NE * REGION
    HK = FI // 2

    stack = ExitStack()
    first_branch = ExitStack()
    with stack:
        def keep(name, shape, dt=F32):
            return stack.enter_context(nc.sbuf_tensor(name, shape, dt))

        def sb(name, shape, dt=F32):
            return first_branch.enter_context(nc.sbuf_tensor(name, shape, dt))

        def sem(name):
            return stack.enter_context(nc.semaphore(name))

        bank = [stack.enter_context(nc.psum_tensor(f"bank{i}", [P, 512], F32)) for i in range(8)]
        c_dram = nc.dram_tensor("c_rows", [NB * NS, L], F32, kind="Internal").ap()
        skip_dram = nc.dram_tensor("skip_rows", [NB, P, ET * L], F32, kind="Internal").ap()

        xs_dram = nc.dram_tensor("tokens_by_expert", [DUMMY + P, DM], F32, kind="Internal").ap()
        ys_dram = nc.dram_tensor("results_by_expert", [SLOTS * P, DM], F32, kind="Internal").ap()

        ident = keep("ident", [P, P])
        x1 = keep("x1", [P, NT, DM])
        eps = keep("eps", [P, 1])
        zeros = keep("zeros", [P, DM])
        slot_f = keep("slot_f", [P, NT, TOPK])
        slot_i = keep("slot_i", [P, NT, TOPK], I32)
        y_i = keep("y_i", [P, NT, TOPK], I32)
        weight = keep("weight", [P, NT, TOPK])
        gf = keep("gf", [P, 1])
        tgf = keep("tgf", [P, 1])
        stats = keep("stats", [P, NT, 6])
        mv = keep("mv", [P, NT, 2])
        std = keep("std", [P, NT])
        rstd = keep("rstd", [P, NT])
        nmr = keep("nmr", [P, NT])
        w_in_nat = sb("w_in_nat", [P, ET, DC])
        w_inT = sb("w_inT", [P, CT, DI])
        xproj_nat = sb("xproj_nat", [XR, DI])
        xprojT = sb("xprojT", [P, ET, XR])
        dtw_nat = sb("dtw_nat", [P, ET, DR])
        dtwT = sb("dtwT", [DR, DI])
        cw = sb("cw", [P, ET, TAPS])
        cb = sb("cb", [P, ET])
        dtb = sb("dtb", [P, ET])
        Dp = sb("Dp", [P, ET])
        Alog = sb("Alog", [P, ET, NS])
        Aexp = sb("Aexp", [P, ET, NS])
        Aneg = sb("Aneg", [P, ET, NS])
        gx = sb("gx", [P, 1])
        tgx = sb("tgx", [P, 1])
        zT = sb("zT", [P, NT, DI])
        delta = sb("delta", [P, NB, ET, L])
        duT = sb("duT", [P, NT, DI])
        BT = sb("BT", [P, NB, LC * NS])
        ctxn = sb("ctxn", [P, LC, DC])
        ctxT = sb("ctxT", [P, CT, L])
        times_c_buf = sb("times_c", [P, ET, L])
        w0, w1, w2, w3 = [sb(f"work{i}", [P, ET, L]) for i in range(4)]
        xdbl = sb("xdbl", [XR, L])
        skip = sb("skip", [P, ET, L])
        u = [zT[:, b * ET:(b + 1) * ET, :] for b in range(NB)]
        expneg = [duT[:, b * ET:(b + 1) * ET, :] for b in range(NB)]
        conv = w0
        rounding = [w1, w2]
        logw = w3
        silu_z = [w0, w1]
        dBuT = [w0, w1]
        dA = [w2[:, i, :] for i in range(RING)]
        h = [w3[:, i, :] for i in range(RING)]
        hC = [times_c_buf[:, i, :] for i in range(RING)]
        crow = [ctxT[:, i, :] for i in range(2)]
        first_branch.close()

        gate_sb = keep("gate_sb", [P, DM // P, NE])
        upper = keep("upper", [P, P], BF16)
        ones = keep("ones", [P, P], BF16)
        eidx = keep("eidx", [P, NE])
        ebase = keep("ebase", [P, NE])
        xn_own = keep("xn", [P, LC, DM])
        xnT = keep("xnT", [P, LC, DM])
        logit = keep("logit", [P, LC, NE])
        top = keep("top", [P, LC, 8])
        topi = keep("topi", [P, LC, 8], U32)
        topf = keep("topf", [P, NT * TOPK])
        ex = keep("ex", [P, LC, TOPK])
        exs = keep("exs", [P, LC])
        onehot = keep("onehot", [P, LC * TOPK, NE])
        picked = keep("picked", [P, LC * TOPK, NE])
        chosen = keep("chosen", [P, LC, NE], BF16)
        cum = keep("cum", [P, NE])
        cumb = keep("cumb", [P, NE])
        nti = keep("nti", [P, NE], I32)
        ntf = keep("ntf", [P, NE])
        ntcum = keep("ntcum", [P, NE])
        ntone = keep("ntone", [P, NE])
        shift = keep("shift", [P, NE])
        present = keep("present", [P, NE])
        entry = keep("entry", [P, NE])
        hits = keep("hits", [P, NE])
        pidx = keep("pidx", [P, 1])
        slot_e = keep("slot_e", [P, 1])
        slot_c = keep("slot_c", [P, 1])
        srow = keep("srow", [P, 1])
        svalid = keep("svalid", [P, 1])
        upto = keep("upto", [P, 1])
        behind = keep("behind", [P, 1])
        assert max(SLOTS, NE) <= P
        AHEAD = 2
        columns = keep("columns", [P, 4])
        table = keep("table", [1, 4 * P], I32)
        slot_need = table[:, 0:P]
        slot_row = table[:, P:2 * P]
        expert_of = table[:, 2 * P:3 * P]
        last_slot = table[:, 3 * P:4 * P]
        NWR = 4
        WG, WD = (DM // P) * 2 * FI, 2 * DM
        raw = [keep(f"raw{i}", [P, WG]) for i in range(2)]
        whi = keep("whi", [P, NWR * WG], F32R)
        wlo = keep("wlo", [P, NWR * WG], F32R)
        wdn = keep("wdn", [P, NWR * WD])
        NX = 4
        xrows = keep("xrows", [P, NX, DM])
        xrow = [xrows[:, i, :] for i in range(NX)]
        xhi = [keep(f"xhi{i}", [P, DM], F32R) for i in range(2)]
        xlo = [keep(f"xlo{i}", [P, DM], F32R) for i in range(2)]
        sg = [keep(f"sg{i}", [P, FI]) for i in range(2)]
        gated = [keep(f"gated{i}", [P, FI]) for i in range(2)]
        gT = [keep(f"gT{i}", [P, 2 * P]) for i in range(2)]
        yrows = keep("yrows", [P, NX, DM])
        yrow = [yrows[:, i, :] for i in range(NX)]
        NY = 6
        ygat = keep("ygat", [P, NY, DM])
        xn = [ygat[:, 0:LC, :], xn_own, xrows, yrows]
        assert NB == len(xn) and LC == NX

        s_win = sem("in_proj_loaded")
        s_w = sem("projections_loaded")
        s_wa = sem("channel_factors_loaded")
        s_x = [sem(f"x_loaded{b}") for b in range(NB)]
        s_id0 = sem("ident_zeroed")
        s_eps = sem("eps_ready")
        s_apart = sem("act_waits_passed")
        s_id = sem("ident_ready")
        s_ctx = sem("ctx_loaded")
        s_wt = sem("weights_transposed")
        s_wtc = sem("weights_copied")
        s_ctxt = sem("ctx_transposed")
        s_ctxe = sem("ctx_copied")
        s_xin = sem("in_proj_done")
        s_tap = sem("last_tap_done")
        s_cv = sem("conv_chain")
        s_conv = sem("conv_done")
        s_u = sem("u_ready")
        s_xd = sem("x_proj_done")
        s_bt = sem("x_proj_transposed")
        s_xde = sem("x_proj_copied")
        s_cst = sem("c_rows_stored")
        s_dp = sem("dt_proj_done")
        s_abs = sem("abs_done")
        s_ez = sem("expneg_done")
        s_lw = sem("ln_done")
        s_wm = sem("rounded_minus_one")
        s_t1 = sem("rounding_error_done")
        s_t2 = sem("log1p_done")
        s_t1d = sem("rounding_error_done_by_dve")
        s_t2d = sem("log1p_done_by_dve")
        s_rl = sem("relu_done")
        s_dl = sem("delta_ready")
        s_du = sem("du_ready")
        s_dut = sem("du_transposed")
        s_dute_a = sem("duT_copied_by_act")
        s_dute_d = sem("duT_copied_by_dve")
        s_skc = sem("skip_computed")
        s_sks = sem("skip_stored")
        s_skl = sem("skip_loaded")
        s_sku = sem("skip_used")
        s_A = sem("A_exp_done")
        s_An = sem("A_negated")
        s_tg = sem("tanh_g_ready")
        s_st = sem("stats_done")
        s_mv = sem("mean_var_done")
        s_sd = sem("std_done")
        s_rs = sem("rstd_done")
        s_nm = sem("nmr_done")
        s_zn = sem("silu_z_done")
        s_zt = sem("z_transposed")
        s_zte_a = sem("zT_copied_by_act")
        s_zte_d = sem("zT_copied_by_dve")
        s_bua = sem("dBuT_scaled_act")
        s_bud = sem("dBuT_scaled_dve")
        s_dbu = sem("dBu_in_psum")
        s_h = sem("scan_done")
        s_hc = sem("hC_ready")
        s_hcd = sem("hC_ready_by_dve")
        s_y = sem("y_accumulated")
        s_dA = sem("dA_ready")
        s_c = [sem(f"c_row_loaded{i}") for i in range(2)]
        s_yz = sem("y_times_z")
        s_x1 = sem("x1_ready")
        r_gl = sem("gate_and_g_loaded")
        r_cst0 = sem("router_constants_filled")
        r_cst2 = sem("router_constants_ready")
        r_st2 = sem("stats2_done")
        r_mv2 = sem("mean_var2_done")
        r_sd2 = sem("std2_done")
        r_rs2 = sem("rstd2_done")
        r_nm2 = sem("nmr2_done")
        r_xn2 = sem("normed_ready")
        r_xnt = sem("normed_transposed")
        r_xnte = sem("normed_copied")
        r_lg = sem("logits_done")
        r_lgc = sem("logits_copied")
        r_mx = sem("top8_done")
        r_mi = sem("top8_index_done")
        r_tf = sem("index_float_done")
        r_sub = sem("max_subtracted")
        r_ex = sem("exp_done")
        r_exsum = sem("exp_sum_done")
        r_exr = sem("exp_sum_inverted")
        r_w = sem("weights_of_tokens_done")
        r_oh = sem("onehot_done")
        r_ch = sem("chosen_done")
        r_pos = sem("positions_done")
        r_posb = sem("rows_based")
        r_cumb = sem("base_done")
        r_cum = sem("counts_added")
        r_pk = sem("picked_done")
        r_sf = sem("rows_float_done")
        r_si = sem("rows_ready")
        r_zero = sem("zeros_ready")
        r_zst = sem("zeros_stored")
        r_sc = [sem(f"tokens_scattered{b}") for b in range(NB)]
        r_tb = sem("table_step")
        r_col = sem("table_columns_ready")
        r_colt = sem("table_columns_transposed")
        r_tbl = sem("table_ready")
        r_hi = sem("weights_hi_done")
        r_spl = sem("weights_split")
        r_mmx = sem("x_transposed")
        r_xh = sem("xhi_ready")
        r_gu = sem("gate_up_done")
        r_sg = sem("silu_g_ready")
        r_gd = sem("gated_ready")
        r_gt = sem("gated_transposed")
        r_gh = sem("gT_ready")
        r_dnl = sem("down_loaded")
        r_dn = sem("down_done")
        r_ye = sem("y_copied")
        r_xlo = sem("xlo_ready")
        r_raw = [sem(f"weights_loaded{i}") for i in range(2)]
        r_xl = [sem(f"x_rows_loaded{i}") for i in range(NX)]
        r_ys = [sem(f"y_rows_stored{i}") for i in range(NX)]
        r_yg = [sem(f"y_rows_gathered{i}") for i in range(NY)]
        r_acc = sem("y_added")
        r_yi = sem("rows_of_y_ready")
        r_apart = sem("pool_waits_passed")
        r_apart_sp = sem("sp_waits_passed")
        r_out = sem("out_stored")

        x_rows = x.rearrange("b (c p) d -> p (b c) d", p=P)
        ctx_rows = ctx_in.rearrange("b (c p) d -> b p c d", p=P)
        block = stack.enter_context(nc.Block())

        def cols(i, n=P):
            return slice(i * n, (i + 1) * n)

        def tile(t, i, k=1):
            return t[:, bass.ds(i, k), :].rearrange("p t n -> p (t n)")

        @block.sync
        def _(sp):
            sp.dma_start(w_in_nat[:], in_proj_w.rearrange("(t p) d -> p t d", p=P)).then_inc(s_win, 16)
            sp.dma_start(ctxn[:], ctx_rows[0]).then_inc(s_ctx, 16)
            sp.dma_start(xproj_nat[:], x_proj_w).then_inc(s_w, 16)
            sp.dma_start(dtw_nat[:], dt_proj_w.rearrange("(t p) r -> p t r", p=P)).then_inc(s_w, 16)
            sp.dma_start(gf[:], g_ffn.partition_broadcast(P)).then_inc(r_gl, 16)

            def load_ctx(b):
                sp.wait_ge(s_ctxt, b)
                sp.dma_start(ctxn[:], ctx_rows[b]).then_inc(s_ctx, 16)

            def load_x_rows(b):
                sp.dma_start(x1[:, b * LC:(b + 1) * LC, :], x_rows[:, b * LC:(b + 1) * LC, :]).then_inc(s_x[b], 16)

            load_x_rows(0)
            load_x_rows(1)
            load_ctx(1)
            for b in range(NB):
                if b + 2 < NB:
                    load_ctx(b + 2)
                if b < NB - 2:
                    load_x_rows(b + 2)
                sp.wait_ge(s_xde, b * 2 + 1)
                sp.dma_start(c_dram[b * NS:(b + 1) * NS, :], xdbl[DR + NS:XR, :]).then_inc(s_cst, 16)
                sp.wait_ge(s_skc, b * ET + ET)
                sp.dma_start(skip_dram[b], skip[:].rearrange("p t n -> p (t n)")).then_inc(s_sks, 16)
                if b == 0:
                    sp.wait_ge(r_zero, 1)
                for e in range(b * (NE + 1) // NB, (b + 1) * (NE + 1) // NB):
                    sp.dma_start(xs_dram[e * REGION:e * REGION + P, :], zeros[:]).then_inc(r_zst, 16)

            sp.wait_ge(s_cst, NB * 16)
            sp.wait_ge(s_xin, NB * ET)
            for q in range(2):
                sp.dma_start(crow[q], c_dram[q:q + 1, :].partition_broadcast(P)).then_inc(s_c[q], 16)
            with sp.Fori(1, NB * NS // 2) as j:
                for q in range(2):
                    sp.wait_ge(s_y, j * (2 * ET) + q * ET)
                    sp.dma_start(crow[q], c_dram[bass.ds(j * 2 + q, 1), :].partition_broadcast(P)).then_inc(s_c[q], 16)

            sp.wait_ge(s_x1, NT)
            sp.dma_start(gate_sb[:], gate.rearrange("(k p) e -> p k e", p=P)).then_inc(r_gl, 16)

            def load_gate_up(e, q):
                sp.dma_start(raw[q][:].rearrange("p (k f) -> p k f", f=2 * FI),
                             gate_up[bass.ds(e, 1)].rearrange("o (k p) f -> p (o k) f", p=P)).then_inc(r_raw[q], 16)

            def load_down(e, r):
                sp.dma_start(wdn[0:HK, r * WD:(r + 1) * WD].rearrange("p (k n) -> p k n", n=DM),
                             down[bass.ds(e, 1)].rearrange("o (k p) n -> p (o k) n", p=HK)).then_inc(r_dnl, 16)

            def listed(c):
                return sp.value_load(expert_of[0:1, bass.ds(c, 1)], min_val=0, max_val=NE - 1)

            def listed_with_use(c):
                return (listed(c + 1) if not isinstance(c, int) or c + 1 < NE else None, listed(c),
                        sp.value_load(last_slot[0:1, bass.ds(c - NWR, 1)], min_val=1, max_val=SLOTS + 1))

            load_gate_up(0, 0)
            load_gate_up(1, 1)
            load_down(0, 0)
            sp.wait_ge(r_spl, 2)
            load_down(1, 1)
            sp.wait_ge(r_tbl, 1)
            sp.sem_inc(r_apart_sp, 1)
            load_gate_up(listed(AHEAD), 0)
            for c in range(AHEAD, NWR):
                following, this = listed(c + 1), listed(c)
                sp.wait_ge(r_spl, c * 2)
                load_gate_up(following, (c + 1) % 2)
                load_down(this, c)
            with sp.Fori(1, NE // NWR - 1) as rnd:
                for i in range(NWR):
                    c = rnd * NWR + i
                    following, this, used = listed_with_use(c)
                    sp.wait_ge(r_spl, c * 2)
                    load_gate_up(following, (i + 1) % 2)
                    sp.wait_ge(r_dn, used)
                    load_down(this, i)
            for c in range(NE - NWR, NE):
                following, this, used = listed_with_use(c)
                sp.wait_ge(r_spl, c * 2)
                if c + 1 < NE:
                    load_gate_up(following, (c + 1) % 2)
                sp.wait_ge(r_dn, used)
                load_down(this, c % NWR)
            for t in range(NT):
                sp.wait_ge(r_acc, (t + 1) * TOPK)
                sp.dma_start(out.rearrange("b (c p) d -> (b c) p d", p=P)[t], x1[:, t, :]).then_inc(r_out, 16)
            sp.wait_ge(r_out, NT * 16)

        @block.gpsimd
        def _(pool):
            nc.gpsimd.memset(ident[:], 0.0).then_inc(s_id0, 1)
            pool.wait_ge(s_id0, 1)
            nc.gpsimd.affine_select(out=ident[:], in_=ident[:], compare_op=ALU.not_equal, fill=1.0, base=0,
                                    pattern=[[-1, P]], channel_multiplier=1).then_inc(s_id, 1)
            nc.gpsimd.memset(zeros[:], 0.0).then_inc(r_zero, 1)
            pool.sem_inc(s_hc, RING)
            for b in range(NB - 1):
                t = rounding[b % 2]
                pool.wait_ge(s_wm, b + 1)
                nc.gpsimd.tensor_tensor(t[:], t[:], expneg[b], ALU.subtract).then_inc(s_t1, 1)
                pool.wait_ge(s_lw, b + 1)
                pool.wait_ge(s_t1, b + 1)
                nc.gpsimd.tensor_tensor(t[:], logw[:], t[:], ALU.subtract).then_inc(s_t2, 1)

            with pool.Fori(0, NB) as b:
                def times_c(j, q):
                    n = j * 2 + q
                    m = b * NS + n
                    pool.wait_ge(s_c[q], b * (NS * 8) + (n - q) * 8 + 16)
                    for et in range(ET - q):
                        k = m * ET + et
                        pool.wait_ge(s_h, k + 1 + RING)
                        pool.wait_ge(s_y, k + 1)
                        nc.gpsimd.tensor_tensor(hC[et], h[et], crow[q], ALU.mult).then_inc(s_hc, 1)

                with pool.Fori(0, NS // 2) as j:
                    for q in range(2):
                        times_c(j, q)
                for lc in range(LC):
                    pool.wait_ge(s_yz, b * LC + lc + 1 + 1)
                    t = b * LC + lc
                    nc.gpsimd.tensor_tensor(tile(x1, t), tile(x1, t), tile(zT, t), ALU.add).then_inc(s_x1, 1)

            pool.wait_ge(s_x1, NT)
            nc.gpsimd.memset(ones[:], 1.0).then_inc(r_cst0, 1)
            nc.gpsimd.memset(upper[:], 1.0).then_inc(r_cst0, 1)
            pool.wait_ge(r_cst0, 2)
            nc.gpsimd.affine_select(out=upper[:], in_=upper[:], compare_op=ALU.is_gt, fill=0.0, base=0,
                                    pattern=[[1, P]], channel_multiplier=-1).then_inc(r_cst2, 1)
            nc.gpsimd.iota(eidx[:], pattern=[[1, NE]], base=0, channel_multiplier=0,
                           allow_small_or_imprecise_dtypes=True).then_inc(r_cst2, 1)
            nc.gpsimd.iota(ebase[:], pattern=[[REGION, NE]], base=P, channel_multiplier=0,
                           allow_small_or_imprecise_dtypes=True).then_inc(r_cst2, 1)
            nc.gpsimd.iota(pidx[:], pattern=[[1, 1]], base=0, channel_multiplier=1,
                           allow_small_or_imprecise_dtypes=True).then_inc(r_cst2, 1)

            def split(c, q, r):
                at = slice(r * WG, (r + 1) * WG)
                pool.wait_ge(r_raw[q], (c - q) * 8 + 16)
                pool.sem_inc(r_apart, 1)
                nc.gpsimd.tensor_copy(whi[:, at], raw[q][:]).then_inc(r_hi, 1)
                pool.wait_ge(r_hi, c + 1)
                nc.gpsimd.tensor_tensor(wlo[:, at], raw[q][:], whi[:, at].bitcast(F32), ALU.subtract).then_inc(r_spl, 1)
                pool.wait_ge(r_dnl, c * 16 + 16)
                pool.sem_inc(r_spl, 1)

            EARLY = 1
            for c in range(EARLY):
                split(c, c % 2, c)
            for b in range(NB):
                pool.wait_ge(r_si, b + 1)
                for t in range(LC):
                    for j in range(TOPK):
                        nc.gpsimd.indirect_dma_start(
                            out=xs_dram, out_offset=bass.IndirectOffsetOnAxis(ap=slot_i[:, b * LC + t, j:j + 1], axis=0),
                            in_=xn[b][:, t, :], in_offset=None).then_inc(r_sc[b], 16)
            for c in range(EARLY, NWR):
                split(c, c % 2, c)
            pool.wait_ge(r_tbl, 1)
            with pool.Fori(1, NE // NWR) as rnd:
                for i in range(NWR):
                    c = rnd * NWR + i
                    used = pool.value_load(last_slot[0:1, bass.ds(c - NWR, 1)], min_val=1, max_val=SLOTS + 1)
                    pool.wait_ge(r_dn, used)
                    split(c, i % 2, i)
            pool.wait_ge(r_yi, 1)
            for q in range(NX):
                pool.wait_ge(r_ys[q], SLOTS // NX * 16)
            for t in range(NT):
                for j in range(TOPK):
                    k = t * TOPK + j
                    if k >= NY:
                        pool.wait_ge(r_acc, k - NY + 1)
                    nc.gpsimd.indirect_dma_start(
                        out=ygat[:, k % NY, :], out_offset=None, in_=ys_dram,
                        in_offset=bass.IndirectOffsetOnAxis(ap=y_i[:, t, j:j + 1], axis=0)).then_inc(r_yg[k % NY], 16)

        @block.tensor
        def _(pe):
            pe.sem_inc(s_sku, 1)
            def turn(dst, src, start=True, stop=True):
                k = src.shape[0]
                return nc.tensor.matmul(dst, src, ident[0:k, 0:k], start=start, stop=stop, is_transpose=True)

            pe.wait_ge(s_id, 1)
            pe.wait_ge(s_win, 16)
            for ct in range(CT):
                for et in range(ET):
                    last = turn(bank[ct][:, cols(et)], w_in_nat[:, et, cols(ct)])
                last.then_inc(s_wt, 1)
            pe.wait_ge(s_w, 2 * 16)
            for et in range(ET):
                last = turn(bank[2][:, cols(et, XR)], xproj_nat[:, cols(et)])
            last.then_inc(s_wt, 1)
            for et in range(ET):
                last = turn(bank[3][0:DR, cols(et)], dtw_nat[:, et, :])
            last.then_inc(s_wt, 1)
            pe.wait_ge(s_wtc, 4)

            def turn_ctx(b):
                pe.wait_ge(s_ctx, b * 16 + 16)
                if b:
                    pe.wait_ge(s_ctxe, b * CT)
                if b >= 2:
                    pe.wait_ge(s_xde, b * 2 - 2)
                for ct in range(CT):
                    for lc in range(LC):
                        last = turn(bank[ct][:, cols(lc)], ctxn[:, lc, cols(ct)])
                last.then_inc(s_ctxt, 1)

            def in_proj(b, ets):
                pe.wait_ge(s_ctxe, b * CT + CT)
                for et in ets:
                    if b:
                        pe.wait_ge(s_conv, (b - 1) * ET + et + 1)
                    for ct in range(CT):
                        last = nc.tensor.matmul(bank[2 + et][:], w_inT[:, ct, cols(et)], ctxT[:, ct, :],
                                                start=(ct == 0), stop=(ct == CT - 1))
                    last.then_inc(s_xin, 1)

            turn_ctx(0)
            in_proj(0, range(ET))
            turn_ctx(1)
            for b in range(NB):
                if b + 1 < NB:
                    in_proj(b + 1, range(ET // 2))
                pe.wait_ge(s_u, b * ET + ET)
                for et in range(ET):
                    last = nc.tensor.matmul(bank[0][0:XR, :], xprojT[:, et, :], u[b][:, et, :],
                                            start=(et == 0), stop=(et == ET - 1))
                last.then_inc(s_xd, 1)
                if b + 1 < NB:
                    in_proj(b + 1, range(ET // 2, ET))
                pe.wait_ge(s_xde, b * 2 + 1)
                for lc in range(LC):
                    last = turn(bank[1][:, cols(lc, XR)], xdbl[:, cols(lc)])
                last.then_inc(s_bt, 1)
                for et in range(ET):
                    if b * ET + et >= 2:
                        pe.wait_ge(s_rl, b * ET + et - 1)
                    nc.tensor.matmul(bank[6 + et % 2][:], dtwT[:, cols(et)], xdbl[0:DR, :],
                                     start=True, stop=True).then_inc(s_dp, 1)
                if b + 2 < NB:
                    turn_ctx(b + 2)

            pe.wait_ge(s_rl, NB * ET)
            pe.wait_ge(s_conv, NB * ET)

            def turn_du(b):
                if b:
                    pe.wait_ge(s_dute_a, b * (LC // 2))
                    pe.wait_ge(s_dute_d, b * (LC // 2))
                pe.wait_ge(s_du, b + 1)
                for lc in range(LC):
                    for et in range(ET):
                        last = turn(bank[4 + lc][:, cols(et)], u[b][:, et, cols(lc)])
                    last.then_inc(s_dut, 1)

            def turn_z(b):
                pe.wait_ge(s_zn, b * ET + ET)
                if b:
                    pe.wait_ge(s_zte_a, b * (LC // 2))
                    pe.wait_ge(s_zte_d, b * (LC // 2))
                for lc in range(LC):
                    for et in range(ET):
                        last = turn(bank[lc][:, cols(et)], silu_z[b % 2][:, et, cols(lc)])
                    last.then_inc(s_zt, 1)

            for b in range(NB - 1):
                turn_du(b)
            pe.wait_ge(s_xde, NB * 2)
            for b in range(NB - 2):
                turn_z(b)
            turn_du(NB - 1)
            for b in range(NB - 2, NB):
                turn_z(b)

            pe.sem_inc(s_dbu, 2 * RING)
            pe.sem_inc(s_y, RING)
            pe.wait_ge(s_zte_a, NB * (LC // 2))
            pe.wait_ge(s_zte_d, NB * (LC // 2))
            pe.wait_ge(s_dute_a, NB * (LC // 2))
            pe.wait_ge(s_dute_d, NB * (LC // 2))
            with pe.Fori(0, NB) as b:
                def to_channels(n, q, et):
                    m = b * NS + n
                    if et == 0:
                        pe.wait_ge(s_bua, b * (NS * (LC - 1) + 1) + n * (LC - 1) + LC)
                        if not isinstance(n, int) or n > 0:
                            pe.wait_ge(s_bud, b * (NS - 1) + n)
                    pe.wait_ge(s_h, m * ET + et + 1)
                    for lc in range(LC):
                        last = turn(bank[et][:, cols(lc)], dBuT[q][:, lc, cols(et)])
                    last.then_inc(s_dbu, 1)

                def add_to_y(j, q, et, stop=False):
                    if q and et == ET - 1:
                        pe.wait_ge(s_hcd, b * (NS // 2) + j + 2)
                    else:
                        pe.wait_ge(s_hc, (b * (NS // 2) + j) * PC + q * ET + et + 1 + RING)
                    for lc in range(LC):
                        last = turn(bank[4 + lc][:, cols(et)], hC[et][:, cols(lc)], start=False, stop=stop)
                    last.then_inc(s_y, 1)

                for et in range(ET):
                    to_channels(0, 0, et)
                pe.wait_ge(s_skl, b * 16 + 16)
                pe.wait_ge(s_yz, b * LC + 1)
                for et in range(ET):
                    for lc in range(LC):
                        last = turn(bank[4 + lc][:, cols(et)], skip[:, et, cols(lc)], start=(et == 0), stop=False)
                last.then_inc(s_sku, 1)
                with pe.Fori(0, NS // 2 - 1) as j:
                    for q in range(2):
                        for et in range(ET):
                            to_channels(j * 2 + q + 1, 1 - q, et)
                            add_to_y(j, q, et)
                for et in range(ET):
                    to_channels(NS - 1, 1, et)
                    add_to_y(NS // 2 - 1, 0, et)
                for et in range(ET):
                    add_to_y(NS // 2 - 1, 1, et, stop=(et == ET - 1))

            pe.wait_ge(s_x1, NT)
            pe.wait_ge(r_gl, 32)
            pe.wait_ge(r_cst2, 4)

            def turn_normed(b):
                for t in range(LC):
                    pe.wait_ge(r_xn2, b * LC + t + 1)
                    if b:
                        pe.wait_ge(r_xnte, b * LC)
                    for d in range(DM // P):
                        last = turn(bank[t][:, cols(d)], xn[b][:, t, cols(d)])
                    last.then_inc(r_xnt, 1)

            turn_normed(0)
            for b in range(NB):
                pe.wait_ge(r_xnte, (b + 1) * LC)
                if b:
                    pe.wait_ge(r_lgc, b)
                for t in range(LC):
                    for d in range(DM // P):
                        last = nc.tensor.matmul(bank[4][:, cols(t, NE)], xnT[:, t, cols(d)], gate_sb[:, d, :],
                                                start=(d == 0), stop=(d == DM // P - 1))
                last.then_inc(r_lg, 1)
                if b + 1 < NB:
                    turn_normed(b + 1)
                pe.wait_ge(r_ch, b + 1)
                if b:
                    pe.wait_ge(r_cum, b)
                nc.tensor.matmul(bank[5][:, 0:LC * NE], upper[:], chosen[:].rearrange("p t e -> p (t e)"),
                                 start=True, stop=False)
                for t in range(LC - 1):
                    later = LC - 1 - t
                    nc.tensor.matmul(bank[5][:, (t + 1) * NE:LC * NE], ones[:],
                                     chosen[:, t:t + 1, :].broadcast_to([P, later, NE]), start=False, stop=(t == LC - 2))
                for t in range(LC):
                    last = nc.tensor.matmul(bank[5][:, LC * NE:(LC + 1) * NE], ones[:], chosen[:, t, :],
                                            start=(t == 0), stop=(t == LC - 1))
                last.then_inc(r_pos, 1)

            KD = DM // P

            def turn_x(s, q):
                pe.wait_ge(r_xl[q], (s - q) * (16 // NX) + 16)
                pe.wait_ge(r_xlo, s + 1)
                for d in range(KD):
                    last = turn(bank[q % 2][:, cols(d)], xrow[q][:, cols(d)])
                last.then_inc(r_mmx, 1)

            def three(dst, lh, ll, rh, rl, start, stop):
                nc.tensor.matmul(dst, lh, rh, start=start, stop=False)
                nc.tensor.matmul(dst, lh, rl, start=False, stop=False)
                return nc.tensor.matmul(dst, ll, rh, start=False, stop=stop)

            def look_up(s):
                return pe.value_load(slot_need[0:1, bass.ds(s, 1)], min_val=2, max_val=2 * NE)

            def column(need, width):
                return (((need >> 1) - 1) & (NWR - 1)) * width

            def up(s, q, need):
                pe.wait_ge(r_spl, need)
                pe.wait_ge(r_xlo, s + 1 + 2)
                pe.wait_ge(r_gd, s + 1)
                for d in range(KD):
                    at = column(need, WG) + d * 2 * FI
                    last = three(bank[2 + q % 2][:, 0:2 * FI], xhi[q % 2][:, cols(d)], xlo[q % 2][:, cols(d)],
                                 whi[:, bass.ds(at, 2 * FI)], wlo[:, bass.ds(at, 2 * FI)], d == 0, d == KD - 1)
                last.then_inc(r_gu, 1)

            def turn_g(s, q):
                pe.wait_ge(r_gd, s + 1 + 2)
                pe.wait_ge(r_gh, s + 1)
                for i in range(2):
                    last = turn(bank[4 + q % 2][0:HK, cols(i)], gated[q % 2][:, cols(i, HK)])
                last.then_inc(r_gt, 1)

            def dn(s, q, need):
                pe.wait_ge(r_gh, s + 1 + 2)
                pe.wait_ge(r_ye, s + 1 + UNR - 2)
                for i in range(2):
                    last = nc.tensor.matmul(bank[6 + q % 2][:], gT[q % 2][0:HK, cols(i)],
                                            wdn[0:HK, bass.ds(column(need, WD) + i * DM, DM)], start=(i == 0), stop=(i == 1))
                last.then_inc(r_dn, 1)

            pe.wait_ge(r_cum, NB)
            pe.wait_ge(r_col, 1)
            for i in range(4):
                last = turn(bank[5][0:1, cols(i)], columns[:, i:i + 1])
            last.then_inc(r_colt, 1)
            pe.wait_ge(r_tbl, 1)
            pe.sem_inc(r_dn, 1)
            pe.sem_inc(r_gu, 2)
            def turn_of_slot(s, i, last=False):
                dn(s - 1, (i - 1) % UNR, look_up(s - 1))
                need = None if last else look_up(s + 1)
                turn_g(s, i)
                if not isinstance(s, int) or s + 2 < SLOTS:
                    turn_x(s + 2, (i + 2) % UNR)
                if not last:
                    up(s + 1, (i + 1) % UNR, need)

            turn_x(0, 0)
            turn_x(1, 1)
            up(0, 0, look_up(0))
            turn_g(0, 0)
            turn_x(2, 2)
            up(1, 1, look_up(1))
            with pe.Fori(0, SLOTS // UNR - 1) as rnd:
                for i in range(UNR):
                    turn_of_slot(rnd * UNR + i + 1, (i + 1) % UNR)
            for s in range(SLOTS - UNR + 1, SLOTS):
                turn_of_slot(s, s % UNR, s == SLOTS - 1)
            dn(SLOTS - 1, (SLOTS - 1) % UNR, look_up(SLOTS - 1))

        @block.scalar
        def _(act):
            def wait_apart(s, value):
                act.wait_ge(s, value)
                act.sem_inc(s_apart, 1)

            act.dma_start(Alog[:], A_log.rearrange("(t p) n -> p t n", p=P)).then_inc(s_wa, 16)
            act.dma_start(cw[:], conv_w.rearrange("(t p) k -> p t k", p=P)).then_inc(s_wa, 16)
            for dst, src in ((cb, conv_b), (dtb, dt_proj_b), (Dp, D)):
                act.dma_start(dst[:], src.rearrange("(t p) -> p t", p=P), allow_slow_non_contiguous=True).then_inc(s_wa, 16)
            act.dma_start(gx[:], g_xattn.partition_broadcast(P)).then_inc(s_wa, 16)

            def copy_ctx(b):
                act.wait_ge(s_ctxt, b + 1)
                if b:
                    act.wait_ge(s_xin, b * ET)
                for ct in range(CT):
                    nc.scalar.copy(ctxT[:, ct, :], bank[ct][:]).then_inc(s_ctxe, 1)

            def last_tap(b, ets):
                for et in ets:
                    act.wait_ge(s_xin, b * ET + et + 1)
                    if b:
                        act.wait_ge(s_u, (b - 1) * ET + et + 1)
                    nc.scalar.activation(conv[:, et, :], bank[2 + et][:], ACT.Identity, bias=cb[:, et:et + 1],
                                         scale=cw[:, et, TAPS - 1:TAPS]).then_inc(s_tap, 1)

            copy_ctx(0)
            act.wait_ge(s_wa, 6 * 16)
            last_tap(0, range(ET))
            copy_ctx(1)
            nc.scalar.activation(tgx[:], gx[:], ACT.Tanh).then_inc(s_tg, 1)
            nc.scalar.activation(Aexp[:], Alog[:], ACT.Exp).then_inc(s_A, 1)
            for b in range(NB + 1):
                if b < NB:
                    for et in range(ET):
                        act.wait_ge(s_conv, b * ET + et + 1)
                        nc.scalar.activation(u[b][:, et, :], conv[:, et, :], ACT.Silu).then_inc(s_u, 1)
                if b + 1 < NB:
                    last_tap(b + 1, range(ET // 2))
                if b >= 1:
                    act.wait_ge(s_abs, b * ET)
                    nc.scalar.activation(expneg[b - 1], expneg[b - 1], ACT.Exp, scale=-1.0).then_inc(s_ez, 1)
                if b + 1 < NB:
                    last_tap(b + 1, range(ET // 2, ET))
                if b < NB:
                    for et in range(ET):
                        act.wait_ge(s_dp, b * ET + et + 1)
                        nc.scalar.activation(expneg[b][:, et, :], bank[6 + et % 2][:], ACT.Abs, bias=dtb[:, et:et + 1]).then_inc(s_abs, 1)
                        nc.scalar.activation(delta[:, b, et, :], bank[6 + et % 2][:], ACT.Relu, bias=dtb[:, et:et + 1]).then_inc(s_rl, 1)
                if b + 2 < NB:
                    copy_ctx(b + 2)
                if b >= 1:
                    act.wait_ge(s_ez, b)
                    if b >= 2:
                        act.wait_ge(s_t2, b - 1)
                    nc.scalar.activation(logw[:], expneg[b - 1], ACT.Ln, bias=1.0).then_inc(s_lw, 1)

            def copy_du(b):
                for lc in range(LC // 2):
                    act.wait_ge(s_dut, b * LC + lc + 1)
                    nc.scalar.copy(duT[:, b * LC + lc, :], bank[4 + lc][:]).then_inc(s_dute_a, 1)

            def copy_z(b):
                for lc in range(LC // 2):
                    act.wait_ge(s_zt, b * LC + lc + 1)
                    nc.scalar.mul(zT[:, b * LC + lc, :], bank[lc][:], tgx[:]).then_inc(s_zte_a, 1)

            def silu_of_norm(b):
                if b >= 2:
                    act.wait_ge(s_zt, (b - 1) * LC)
                for et in range(ET):
                    t = b * ET + et
                    nc.scalar.activation(silu_z[b % 2][:, et, :], x1[:, t, :], ACT.Silu, bias=nmr[:, t:t + 1],
                                         scale=rstd[:, t:t + 1]).then_inc(s_zn, 1)

            copy_du(0)
            act.wait_ge(s_mv, NT)
            act.wait_ge(s_eps, 1)
            nc.scalar.activation(std[:], mv[:, :, 1], ACT.Sqrt, bias=eps[:]).then_inc(s_sd, 1)
            act.wait_ge(s_nm, 1)
            silu_of_norm(0)
            act.wait_ge(s_dl, NB - 1)
            for b in range(1, NB - 1):
                copy_du(b)
                if b == 1:
                    silu_of_norm(b)
            for b in range(NB - 2):
                copy_z(b)
                silu_of_norm(b + 2)
            copy_du(NB - 1)
            for b in range(NB - 2, NB):
                copy_z(b)

            act.wait_ge(s_dl, NB)
            act.wait_ge(s_zt, NB * LC)
            act.wait_ge(s_dute_a, NB * (LC // 2))
            act.wait_ge(s_dute_d, NB * (LC // 2))
            act.wait_ge(s_An, 1)
            act.wait_ge(s_sks, NB * 16)
            with act.Fori(0, NB) as b:
                def scale_b(n, q):
                    m = b * NS + n
                    wait_apart(s_dbu, m * ET + RING)
                    for lc in range(LC if isinstance(n, int) and n == 0 else LC - 1):
                        nc.scalar.mul(dBuT[q][:, lc, :], tile(duT, b * LC + lc),
                                      BT[:, bass.ds(b, 1), bass.ds(n + lc * NS, 1)].rearrange("p o n -> p (o n)")).then_inc(s_bua, 1)

                def decay(n, q):
                    for et in range(ET):
                        k = (b * NS + n) * ET + et
                        wait_apart(s_h, k + 1)
                        nc.scalar.activation(dA[et], delta[:, bass.ds(b, 1), et, :].rearrange("p o n -> p (o n)"),
                                             ACT.Exp, scale=Aneg[:, et, bass.ds(n, 1)]).then_inc(s_dA, 1)

                act.wait_ge(s_sku, b + 1)
                act.dma_start(skip[:].rearrange("p t n -> p (t n)"),
                              skip_dram[bass.ds(b, 1)].rearrange("o p n -> (o p) n")).then_inc(s_skl, 16)
                scale_b(0, 0)
                with act.Fori(0, NS - 2, 2) as n:
                    for q in range(2):
                        scale_b(n + q + 1, 1 - q)
                        decay(n + q, q)
                scale_b(NS - 1, 1)
                decay(NS - 2, 0)
                decay(NS - 1, 1)

            act.wait_ge(r_gl, 16)
            nc.scalar.activation(tgf[:], gf[:], ACT.Tanh).then_inc(r_ex, 1)
            for first, end in ((0, LC), (LC, NT)):
                act.wait_ge(r_mv2, end)
                nc.scalar.activation(std[:, first:end], mv[:, first:end, 1], ACT.Sqrt, bias=eps[:]).then_inc(r_sd2, 1)
                if first == 0:
                    for t in range(LC):
                        act.wait_ge(r_xnt, t + 1)
                        nc.scalar.copy(xnT[:, t, :], bank[t][:]).then_inc(r_xnte, 1)
            for b in range(NB):
                for t in range(LC // 2 if b else 0):
                    act.wait_ge(r_xnt, b * LC + t + 1)
                    act.wait_ge(r_lg, b)
                    nc.scalar.copy(xnT[:, t, :], bank[t][:]).then_inc(r_xnte, 1)
                act.wait_ge(r_sub, b + 1)
                nc.scalar.activation(ex[:], ex[:], ACT.Exp).then_inc(r_ex, 1)

            def x_hi(s, q):
                act.wait_ge(r_mmx, s + 1)
                act.wait_ge(r_gu, s + 1)
                nc.scalar.copy(xhi[q % 2][:], bank[q % 2][:]).then_inc(r_xh, 1)

            def load_x(s, q):
                row = act.value_load(slot_row[0:1, bass.ds(s, 1)], min_val=0, max_val=DUMMY)
                act.dma_start(xrow[q], xs_dram[bass.ds(row, P), :]).then_inc(r_xl[q], 16)

            def store_y(s, q):
                act.wait_ge(r_ye, s + 1 + UNR)
                act.dma_start(ys_dram[bass.ds(s * P, P), :], yrow[q]).then_inc(r_ys[q], 16)

            act.wait_ge(r_cum, NB)
            act.sem_inc(r_gh, 2)
            nc.scalar.preload_act_table(ACT.Silu)
            act.wait_ge(r_zst, (NE + 1) * 16)
            act.wait_ge(r_tbl, 1)
            for b in range(NB):
                act.wait_ge(r_sc[b], LC * TOPK * 16)
            for s in range(NX):
                load_x(s, s)
            x_hi(0, 0)
            load_x(NX, 0)

            def slot(s, q, first=False, more=True, loads=True):
                if more:
                    x_hi(s + 1, (q + 1) % UNR)
                if loads:
                    load_x(s + 1 + NX, (q + 1) % NX)
                act.wait_ge(r_gu, s + 1 + 2)
                act.wait_ge(r_gd, s + 1)
                nc.scalar.activation(sg[q % 2][:], bank[2 + q % 2][:, 0:FI], ACT.Silu).then_inc(r_sg, 1)
                act.wait_ge(r_gt, s + 1)
                act.wait_ge(r_dn, s + 1)
                nc.scalar.copy(gT[q % 2][0:HK, :], bank[4 + q % 2][0:HK, 0:2 * P]).then_inc(r_gh, 1)
                if not first:
                    store_y(s - 2, (q - 2) % UNR)

            for s in range(UNR):
                slot(s, s, first=s < 2)
            with act.Fori(1, SLOTS // UNR - 2) as rnd:
                for q in range(UNR):
                    slot(rnd * UNR + q, q)
            for s in range(SLOTS - 2 * UNR, SLOTS):
                slot(s, s % UNR, more=s < SLOTS - 1, loads=s + 1 + NX < SLOTS)
            for s in range(SLOTS - 2, SLOTS):
                store_y(s, s % UNR)

        @block.vector
        def _(dve):
            dve.sem_inc(s_yz, 1)
            nc.vector.memset(eps[:], LN_EPS).then_inc(s_eps, 1)
            for ct in range(CT):
                dve.wait_ge(s_wt, ct + 1)
                nc.vector.tensor_copy(w_inT[:, ct, :], bank[ct][:]).then_inc(s_wtc, 1)
            dve.wait_ge(s_wt, CT + 1)
            nc.vector.tensor_copy(xprojT[:].rearrange("p t n -> p (t n)"), bank[2][:, 0:ET * XR]).then_inc(s_wtc, 1)
            dve.wait_ge(s_wt, CT + 2)
            nc.vector.tensor_copy(dtwT[:], bank[3][0:DR, :]).then_inc(s_wtc, 1)

            def earlier_taps(b):
                for j, k in enumerate(range(TAPS - 2, -1, -1)):
                    s = TAPS - 1 - k
                    for et in range(ET):
                        if j == 0:
                            dve.wait_ge(s_tap, b * ET + et + 1)
                        else:
                            dve.wait_ge(s_cv, b * (ET * (TAPS - 2)) + (j - 1) * ET + et + 1)
                        nc.vector.scalar_tensor_tensor(
                            out=conv[:, et, s:], in0=bank[2 + et][:, 0:L - s], scalar=cw[:, et, k:k + 1],
                            in1=conv[:, et, s:], op0=ALU.mult, op1=ALU.add,
                        ).then_inc(s_conv if k == 0 else s_cv, 1)

            def skip_rows(b):
                if b:
                    dve.wait_ge(s_sks, b * 16)
                for et in range(ET):
                    dve.wait_ge(s_u, b * ET + et + 1)
                    nc.vector.tensor_scalar_mul(skip[:, et, :], u[b][:, et, :], Dp[:, et:et + 1]).then_inc(s_skc, 1)

            def stats_of(batches):
                for b in batches:
                    dve.wait_ge(s_x[b], 16)
                    for t in range(b * LC, (b + 1) * LC):
                        nc.vector.bn_stats(stats[:, t, :], x1[:, t, :]).then_inc(s_st, 1)
                for t in range(batches[0] * LC, (batches[-1] + 1) * LC):
                    dve.wait_ge(s_st, t + 1)
                    nc.vector.bn_aggr(mv[:, t, :], stats[:, t, :]).then_inc(s_mv, 1)

            def x_proj_rows(b):
                dve.wait_ge(s_xd, b + 1)
                if b:
                    dve.wait_ge(s_dp, b * ET)
                    dve.wait_ge(s_cst, b * 16)
                nc.vector.tensor_copy(xdbl[:], bank[0][0:XR, :]).then_inc(s_xde, 1)
                dve.wait_ge(s_bt, b + 1)
                nc.vector.tensor_copy(BT[:, b, :].rearrange("p (c n) -> p c n", n=NS),
                                      bank[1][:, 0:LC * XR].rearrange("p (c r) -> p c r", r=XR)[:, :, DR:DR + NS]).then_inc(s_xde, 1)

            def rounded(b):
                dve.wait_ge(s_ez, b + 1)
                nc.vector.tensor_scalar(rounding[b % 2][:], expneg[b], 1.0, 1.0, ALU.add, ALU.subtract).then_inc(s_wm, 1)

            def delta_and_du(b):
                if b < NB - 1:
                    dve.wait_ge(s_t2, b + 1)
                else:
                    dve.wait_ge(s_t2d, 1)
                dve.wait_ge(s_rl, b * ET + ET)
                nc.vector.tensor_tensor(delta[:, b], delta[:, b], rounding[b % 2][:], ALU.add).then_inc(s_dl, 1)
                dve.wait_ge(s_dl, b + 1)
                nc.vector.tensor_tensor(u[b], delta[:, b], u[b], ALU.mult).then_inc(s_du, 1)

            def copy_du(b):
                for lc in range(LC // 2, LC):
                    dve.wait_ge(s_dut, b * LC + lc + 1)
                    nc.vector.tensor_copy(duT[:, b * LC + lc, :], bank[4 + lc][:]).then_inc(s_dute_d, 1)

            def copy_z(b):
                for lc in range(LC // 2, LC):
                    dve.wait_ge(s_zt, b * LC + lc + 1)
                    nc.vector.tensor_scalar_mul(zT[:, b * LC + lc, :], bank[lc][:], tgx[:]).then_inc(s_zte_d, 1)

            for b in range(NB):
                earlier_taps(b)
                if b >= 2:
                    rounded(b - 2)
                if b >= 3:
                    delta_and_du(b - 3)
                skip_rows(b)
                if b == 0:
                    dve.wait_ge(s_A, 1)
                    nc.vector.tensor_scalar_mul(Aneg[:], Aexp[:], -1.0).then_inc(s_An, 1)
                if b < 2:
                    stats_of(range(b * NB // 2, (b + 1) * NB // 2))
                x_proj_rows(b)
            rounded(NB - 2)
            delta_and_du(NB - 3)
            rounded(NB - 1)
            last_t = rounding[(NB - 1) % 2]
            dve.wait_ge(s_wm, NB)
            nc.vector.tensor_tensor(last_t[:], last_t[:], expneg[NB - 1], ALU.subtract).then_inc(s_t1d, 1)
            delta_and_du(NB - 2)
            dve.wait_ge(s_lw, NB)
            dve.wait_ge(s_t1d, 1)
            nc.vector.tensor_tensor(last_t[:], logw[:], last_t[:], ALU.subtract).then_inc(s_t2d, 1)
            dve.wait_ge(s_sd, 1)
            nc.vector.reciprocal(rstd[:], std[:]).then_inc(s_rs, 1)
            dve.wait_ge(s_rs, 1)
            nc.vector.scalar_tensor_tensor(out=nmr[:], in0=mv[:, :, 0], scalar=-1.0, in1=rstd[:],
                                           op0=ALU.mult, op1=ALU.mult).then_inc(s_nm, 1)
            for b in range(NB - 1):
                copy_du(b)
            dve.wait_ge(s_tg, 1)
            copy_z(0)
            delta_and_du(NB - 1)
            for b in range(1, NB - 2):
                copy_z(b)
            copy_du(NB - 1)
            for b in range(NB - 2, NB):
                copy_z(b)

            dve.sem_inc(s_h, RING)
            dve.sem_inc(s_hcd, 1)
            dve.wait_ge(s_dute_a, NB * (LC // 2))
            dve.wait_ge(s_dute_d, NB * (LC // 2))
            with dve.Fori(0, NB) as b:
                def scale_b(n, q):
                    dve.wait_ge(s_dbu, (b * NS + n) * ET + RING)
                    nc.vector.tensor_scalar_mul(
                        dBuT[q][:, LC - 1, :], tile(duT, b * LC + LC - 1),
                        BT[:, bass.ds(b, 1), bass.ds(n + (LC - 1) * NS, 1)].rearrange("p o n -> p (o n)")).then_inc(s_bud, 1)

                def scans(j, q):
                    n = j * 2 + q
                    pair = b * (NS // 2) + j
                    for et in range(ET):
                        k = (b * NS + n) * ET + et
                        dve.wait_ge(s_dbu, k + 1 + 2 * RING)
                        dve.wait_ge(s_dA, k + 1)
                        if q:
                            dve.wait_ge(s_hc, pair * PC + et + 1 + RING)
                        elif et < ET - 1:
                            dve.wait_ge(s_hc, pair * PC - PC + ET + et + 1 + RING)
                        else:
                            dve.wait_ge(s_hcd, pair + 1)
                        nc.vector.tensor_tensor_scan(out=h[et], data0=dA[et], data1=bank[et][:], initial=0.0,
                                                     op0=ALU.mult, op1=ALU.add).then_inc(s_h, 1)
                    if q:
                        dve.wait_ge(s_c[q], pair * 16 + 16)
                        dve.wait_ge(s_h, k + 1 + RING)
                        dve.wait_ge(s_y, k + 1)
                        nc.vector.tensor_tensor(hC[et], h[et], crow[q], ALU.mult).then_inc(s_hcd, 1)

                with dve.Fori(0, NS // 2 - 1) as j:
                    for q in range(2):
                        scale_b(j * 2 + q + 1, 1 - q)
                        scans(j, q)
                scale_b(NS - 1, 1)
                scans(NS // 2 - 1, 0)
                scans(NS // 2 - 1, 1)
                dve.wait_ge(s_y, (b + 1) * (NS * ET) + RING)
                for lc in range(LC):
                    t = b * LC + lc
                    nc.vector.tensor_tensor(tile(zT, t), bank[4 + lc][:], tile(zT, t), ALU.mult).then_inc(s_yz, 1)

            def stats_of(first, end):
                for t in range(first, end):
                    if t % LC == 0:
                        dve.wait_ge(s_x1, t + LC)
                    nc.vector.bn_stats(stats[:, t, :], x1[:, t, :]).then_inc(r_st2, 1)
                for t in range(first, end):
                    dve.wait_ge(r_st2, t + 1)
                    nc.vector.bn_aggr(mv[:, t, :], stats[:, t, :]).then_inc(r_mv2, 1)

            def factors_of(first, end, i):
                dve.wait_ge(r_sd2, i)
                nc.vector.reciprocal(rstd[:, first:end], std[:, first:end]).then_inc(r_rs2, 1)
                dve.wait_ge(r_rs2, i)
                nc.vector.scalar_tensor_tensor(out=nmr[:, first:end], in0=mv[:, first:end, 0], scalar=-1.0,
                                               in1=rstd[:, first:end], op0=ALU.mult, op1=ALU.mult).then_inc(r_nm2, 1)
                dve.wait_ge(r_nm2, i)

            stats_of(0, LC)
            factors_of(0, LC, 1)
            dve.wait_ge(s_x1, NT)

            def normed(b):
                for t in range(LC):
                    m = b * LC + t
                    nc.vector.tensor_scalar(xn[b][:, t, :], x1[:, m, :], rstd[:, m:m + 1], nmr[:, m:m + 1],
                                            ALU.mult, ALU.add).then_inc(r_xn2, 1)

            def copy_normed(b):
                for t in range(LC // 2, LC):
                    dve.wait_ge(r_xnt, b * LC + t + 1)
                    dve.wait_ge(r_lg, b)
                    nc.vector.tensor_copy(xnT[:, t, :], bank[t][:]).then_inc(r_xnte, 1)

            normed(0)
            stats_of(LC, NT)
            factors_of(LC, NT, 2)
            nc.vector.memset(cum[:], 0.0).then_inc(r_cumb, 1)
            dve.wait_ge(r_cumb, 1)
            dve.wait_ge(r_cst2, 4)
            for b in range(NB):
                if b + 1 < NB:
                    normed(b + 1)
                dve.wait_ge(r_lg, b + 1)
                nc.vector.tensor_copy(logit[:].rearrange("p t e -> p (t e)"), bank[4][:, 0:LC * NE]).then_inc(r_lgc, 1)
                dve.wait_ge(r_lgc, b + 1)
                for t in range(LC):
                    nc.vector.max(out=top[:, t, :], in_=logit[:, t, :]).then_inc(r_mx, 1)
                for t in range(LC):
                    dve.wait_ge(r_mx, b * LC + t + 1)
                    nc.vector.max_index(out=topi[:, t, :], in_max=top[:, t, :], in_values=logit[:, t, :]).then_inc(r_mi, 1)
                nc.vector.tensor_tensor(ex[:], top[:, :, 0:TOPK], top[:, :, 0:1].broadcast_to([P, LC, TOPK]),
                                        ALU.subtract).then_inc(r_sub, 1)
                dve.wait_ge(r_mi, (b + 1) * LC)
                mine = topf[:, b * LC * TOPK:(b + 1) * LC * TOPK]
                nc.vector.tensor_copy(mine.rearrange("p (t j) -> p t j", j=TOPK), topi[:, :, 0:TOPK]).then_inc(r_tf, 1)
                dve.wait_ge(r_tf, b + 1)
                nc.vector.tensor_tensor(onehot[:], eidx[:].unsqueeze(1).broadcast_to([P, LC * TOPK, NE]),
                                        mine.unsqueeze(2).broadcast_to([P, LC * TOPK, NE]), ALU.is_equal).then_inc(r_oh, 1)
                dve.wait_ge(r_oh, b + 1)
                with nc.allow_low_precision(reason="zeros and ones"):
                    nc.vector.tensor_reduce(chosen[:], onehot[:].rearrange("p (t j) e -> p t e j", j=TOPK), AX.X,
                                            ALU.add).then_inc(r_ch, 1)
                dve.wait_ge(r_ex, b + 2)
                nc.vector.tensor_reduce(exs[:], ex[:], AX.X, ALU.add).then_inc(r_exsum, 1)
                dve.wait_ge(r_exsum, b + 1)
                nc.vector.reciprocal(exs[:], exs[:]).then_inc(r_exr, 1)
                dve.wait_ge(r_exr, b + 1)
                nc.vector.scalar_tensor_tensor(out=weight[:, b * LC:(b + 1) * LC, :], in0=ex[:], scalar=tgf[:],
                                               in1=exs[:].unsqueeze(2).broadcast_to([P, LC, TOPK]),
                                               op0=ALU.mult, op1=ALU.mult).then_inc(r_w, 1)
                nc.vector.tensor_tensor(cumb[:], cum[:], ebase[:], ALU.add).then_inc(r_cumb, 1)
                if b + 1 < NB:
                    copy_normed(b + 1)
                dve.wait_ge(r_cumb, b + 2)
                dve.wait_ge(r_pos, b + 1)
                nc.vector.tensor_tensor(picked[:, 0:LC, :], bank[5][:, 0:LC * NE].rearrange("p (t e) -> p t e", e=NE),
                                        cumb[:].unsqueeze(1).broadcast_to([P, LC, NE]), ALU.add).then_inc(r_posb, 1)
                nc.vector.tensor_tensor(cum[:], cum[:], bank[5][:, LC * NE:(LC + 1) * NE], ALU.add).then_inc(r_cum, 1)
                dve.wait_ge(r_posb, b + 1)
                nc.vector.tensor_tensor(onehot[:].rearrange("p (t j) e -> p t j e", j=TOPK),
                                        onehot[:].rearrange("p (t j) e -> p t j e", j=TOPK),
                                        picked[:, 0:LC, :].unsqueeze(2).broadcast_to([P, LC, TOPK, NE]), ALU.mult).then_inc(r_pk, 1)
                dve.wait_ge(r_pk, b + 1)
                nc.vector.tensor_reduce(slot_f[:, b * LC:(b + 1) * LC, :].rearrange("p t j -> p (t j)"), onehot[:], AX.X,
                                        ALU.add).then_inc(r_sf, 1)
                dve.wait_ge(r_sf, b + 1)
                nc.vector.tensor_copy(slot_i[:, b * LC:(b + 1) * LC, :], slot_f[:, b * LC:(b + 1) * LC, :]).then_inc(r_si, 1)
                dve.wait_ge(r_cum, b + 1)

            steps = [0]

            def step(ins):
                steps[0] += 1
                ins.then_inc(r_tb, 1)
                dve.wait_ge(r_tb, steps[0])

            step(nc.vector.tensor_scalar(nti[:], cum[:], float(P - 1), None, ALU.add))
            step(nc.vector.tensor_scalar(nti[:], nti[:], P.bit_length() - 1, None, ALU.arith_shift_right))
            step(nc.vector.tensor_copy(ntf[:], nti[:]))
            step(nc.vector.memset(ntone[:], 1.0))
            step(nc.vector.tensor_tensor_scan(out=ntcum[:], data0=ntone[:], data1=ntf[:], initial=0.0,
                                              op0=ALU.mult, op1=ALU.add))
            step(nc.vector.tensor_scalar(present[:], ntf[:], 0.0, None, ALU.is_gt))
            step(nc.vector.memset(present[:, 0:AHEAD], 1.0))
            step(nc.vector.tensor_tensor_scan(out=entry[:], data0=ntone[:], data1=present[:], initial=-1.0,
                                              op0=ALU.mult, op1=ALU.add))
            final = entry[:, NE - 1:NE]
            step(nc.vector.tensor_tensor(shift[:], cum[:], ebase[:], ALU.add))
            step(nc.vector.scalar_tensor_tensor(out=shift[:], in0=ntcum[:], scalar=float(-P), in1=shift[:],
                                                op0=ALU.mult, op1=ALU.add))
            step(nc.vector.tensor_scalar(hits[:], ntcum[:], pidx[:], None, ALU.is_le))
            step(nc.vector.tensor_reduce(slot_e[:], hits[:], AX.X, ALU.add))
            step(nc.vector.tensor_tensor(hits[:], hits[:], present[:], ALU.mult))
            step(nc.vector.tensor_reduce(slot_c[:], hits[:], AX.X, ALU.add))
            step(nc.vector.tensor_scalar(slot_c[:], slot_c[:], final, None, ALU.min))
            step(nc.vector.tensor_scalar(columns[:, 0:1], slot_c[:], 2.0, 2.0, ALU.mult, ALU.add))
            step(nc.vector.scalar_tensor_tensor(out=hits[:], in0=eidx[:], scalar=slot_e[:], in1=shift[:],
                                                op0=ALU.is_equal, op1=ALU.mult))
            step(nc.vector.tensor_reduce(srow[:], hits[:], AX.X, ALU.add))
            step(nc.vector.scalar_tensor_tensor(out=srow[:], in0=pidx[:], scalar=float(P), in1=srow[:],
                                                op0=ALU.mult, op1=ALU.add))
            step(nc.vector.tensor_scalar(svalid[:], slot_e[:], float(NE), None, ALU.is_lt))
            step(nc.vector.scalar_tensor_tensor(out=srow[:], in0=srow[:], scalar=float(-DUMMY), in1=svalid[:],
                                                op0=ALU.add, op1=ALU.mult))
            step(nc.vector.tensor_scalar(columns[:, 1:2], srow[:], float(DUMMY), None, ALU.add))
            step(nc.vector.scalar_tensor_tensor(out=present[:], in0=entry[:], scalar=pidx[:], in1=present[:],
                                                op0=ALU.is_equal, op1=ALU.mult))
            step(nc.vector.tensor_tensor(hits[:], present[:], eidx[:], ALU.mult))
            step(nc.vector.tensor_reduce(columns[:, 2:3], hits[:], AX.X, ALU.add))
            step(nc.vector.tensor_tensor(hits[:], present[:], ntcum[:], ALU.mult))
            step(nc.vector.tensor_reduce(upto[:], hits[:], AX.X, ALU.add))
            step(nc.vector.tensor_scalar(behind[:], pidx[:], final, float(SLOTS), ALU.is_ge, ALU.mult))
            step(nc.vector.tensor_tensor(upto[:], upto[:], behind[:], ALU.max))
            step(nc.vector.tensor_scalar(columns[:, 3:4], upto[:], 1.0, None, ALU.add))
            dve.sem_inc(r_col, 1)
            dve.wait_ge(r_colt, 1)
            nc.vector.tensor_copy(table[:], bank[5][0:1, :]).then_inc(r_tbl, 1)
            over = [P, NT * TOPK, NE]
            dve.wait_ge(r_sc[0], LC * TOPK * 16)
            match = ygat[:, :, :].rearrange("p a b -> p (a b)")[:, 0:NT * TOPK * NE].rearrange("p (s e) -> p s e", e=NE)
            step(nc.vector.tensor_tensor(match, topf[:].unsqueeze(2).broadcast_to(over),
                                         eidx[:].unsqueeze(1).broadcast_to(over), ALU.is_equal))
            step(nc.vector.tensor_tensor(match, match, shift[:].unsqueeze(1).broadcast_to(over), ALU.mult))
            mine = picked[:].rearrange("p a b -> p (a b)")[:, 0:NT * TOPK]
            step(nc.vector.tensor_reduce(mine, match, AX.X, ALU.add))
            nc.vector.tensor_tensor(y_i[:].rearrange("p t j -> p (t j)"), slot_f[:].rearrange("p t j -> p (t j)"),
                                    mine, ALU.subtract).then_inc(r_yi, 1)

            def x_lo(s, q):
                dve.wait_ge(r_xh, s + 1)
                dve.wait_ge(r_gu, s + 1)
                nc.vector.tensor_tensor(xlo[q % 2][:], bank[q % 2][:], xhi[q % 2][:].bitcast(F32), ALU.subtract).then_inc(r_xlo, 1)

            def y_out(s, q):
                dve.wait_ge(r_dn, s + 1 + 1)
                if not isinstance(s, int) or s >= NX:
                    dve.wait_ge(r_ys[q], (s - q) * (16 // NX))
                nc.vector.tensor_copy(yrow[q], bank[6 + q % 2][:]).then_inc(r_ye, 1)

            def slot(s, q, first, more):
                if more:
                    x_lo(s + 1, (q + 1) % UNR)
                dve.wait_ge(r_sg, s + 1)
                if not first:
                    dve.wait_ge(r_gt, s)
                nc.vector.tensor_tensor(gated[q % 2][:], bank[2 + q % 2][:, FI:2 * FI], sg[q % 2][:], ALU.mult).then_inc(r_gd, 1)
                if not first:
                    y_out(s - 1, (q - 1) % UNR)

            dve.sem_inc(r_xlo, 2)
            dve.sem_inc(r_gd, 2)
            dve.sem_inc(r_ye, UNR)
            x_lo(0, 0)
            for s in range(UNR + 1):
                slot(s, s % UNR, s == 0, True)
            with dve.Fori(1, SLOTS // UNR - 1) as rnd:
                for i in range(UNR):
                    slot(rnd * UNR + i + 1, (i + 1) % UNR, False, True)
            for s in range(SLOTS - UNR + 1, SLOTS):
                slot(s, s % UNR, False, s + 1 < SLOTS)
            y_out(SLOTS - 1, (SLOTS - 1) % UNR)
            for t in range(NT):
                for j in range(TOPK):
                    k = t * TOPK + j
                    dve.wait_ge(r_yg[k % NY], (k // NY + 1) * 16)
                    if k:
                        dve.wait_ge(r_acc, k)
                    nc.vector.scalar_tensor_tensor(out=x1[:, t, :], in0=ygat[:, k % NY, :], scalar=weight[:, t, j:j + 1],
                                                   in1=x1[:, t, :], op0=ALU.mult, op1=ALU.add).then_inc(r_acc, 1)


_INS = ['x', 'ctx_1024', 'g_xattn', 'g_ffn', 'L0_xattn_in_proj_w', 'L0_xattn_conv_w', 'L0_xattn_conv_b',
        'L0_xattn_x_proj_w', 'L0_xattn_dt_proj_w', 'L0_xattn_dt_proj_b', 'L0_xattn_A_log', 'L0_xattn_D',
        'L0_ffn_gate', 'L0_ffn_gate_up_proj', 'L0_ffn_down_proj']


def kernel(**inputs):
    import numpy as _np
    import concourse.bacc as _bacc
    from concourse import mybir as _mybir
    from concourse.bass_utils import run_bass_kernel_spmd as _run

    nc = _bacc.Bacc("TRN2", target_bir_lowering=False, num_devices=1)
    arrays, args = {}, []
    for name in _INS:
        a = _np.ascontiguousarray(inputs[name])
        arrays[f"in_{name}_dram"] = a
        args.append(nc.dram_tensor(f"in_{name}_dram", a.shape, _mybir.dt.from_np(a.dtype), kind="ExternalInput").ap())
    args.append(nc.dram_tensor("out_dram", inputs['x'].shape, _mybir.dt.float32, kind="ExternalOutput").ap())
    flamingo_kernel(nc, *args)
    r = _run(nc, [arrays], core_ids=[0])
    return r.results[0]["out_dram"]
```
